# Optimizing a Trainium2 kernel written in Bass

```python
import numpy as np
import jax
import jax.numpy as jnp

def _softmax(x, axis=-1):
    return jax.nn.softmax(x, axis=axis)

def _gelu(x):
    return jax.nn.gelu(x, approximate=True)

def _silu(x):
    return jax.nn.silu(x)

def _sigmoid(x):
    return jax.nn.sigmoid(x)

def _layernorm(x, axis=-1, eps=1e-05):
    m = jnp.mean(x, axis=axis, keepdims=True)
    v = jnp.var(x, axis=axis, keepdims=True)
    return (x - m) / jnp.sqrt(v + eps)

def _scatter_add(tgt, idx, src, axis=0):
    return tgt.at[idx].add(src)

def _segment_sum(src, seg, n):
    return jax.ops.segment_sum(src, seg, n)
kernel_name = 'mk_gnn_ffn_d1_gnn_r8_36dc0c'

def setup_inputs(seed: int=0):
    np.random.seed(seed)
    _w = jnp.asarray

    def _rec_inputs():
        import jax
        import jax.numpy as jnp
        _gk = jax.random.key(seed)
        x = -0.0002117 + 1 * jax.random.normal(jax.random.fold_in(_gk, 1), (1250, 1024), jnp.float32)
        src = jax.random.randint(jax.random.fold_in(_gk, 2), (40000,), 0, 1250, jnp.int32)
        dst = jnp.minimum((1250 * jax.random.uniform(jax.random.fold_in(_gk, 3), (40000,)) ** 2.0).astype(jnp.int32), 9999)
        _o = jnp.argsort(dst, stable=True)
        src = src[_o]
        dst = dst[_o]
        return (x, src, dst)
    x, src, dst = _rec_inputs()

    def _L0_gnn_setup():
        import jax, jax.numpy as jnp
        import numpy as np
        N_NODES = 3125
        N_EDGES = 50000
        D = 1024

        def _sage_layer(h, edge_src, edge_dst, deg_inv, W_self, W_neigh, b):
            msg = h[edge_src]
            agg = jax.ops.segment_sum(msg, edge_dst, num_segments=h.shape[0])
            mean = agg * deg_inv[:, None]
            return h @ W_self + mean @ W_neigh + b
        key = jax.random.key(seed)
        ks = jax.random.split(key, 8)
        s = 1.0 / np.sqrt(D)
        return {'x': jax.random.normal(ks[0], (N_NODES, D), dtype=jnp.float32), 'edge_src': jax.random.randint(ks[1], (N_EDGES,), 0, N_NODES, dtype=jnp.int32), 'edge_dst': jax.random.randint(ks[2], (N_EDGES,), 0, N_NODES, dtype=jnp.int32), 'W_self0': jax.random.normal(ks[3], (D, D), dtype=jnp.float32) * s, 'W_neigh0': jax.random.normal(ks[4], (D, D), dtype=jnp.float32) * s, 'b0': jnp.zeros((D,), dtype=jnp.float32), 'W_self1': jax.random.normal(ks[5], (D, D), dtype=jnp.float32) * s, 'W_neigh1': jax.random.normal(ks[6], (D, D), dtype=jnp.float32) * s, 'b1': jnp.zeros((D,), dtype=jnp.float32)}
    _L0_gnn_all = _L0_gnn_setup()
    _L0_gnn_in = {k: v for k, v in _L0_gnn_all.items() if k in ('W_self0', 'W_neigh0', 'b0', 'W_self1', 'W_neigh1', 'b1')}
    del _L0_gnn_all

    def _L0_ffn_setup():
        import jax, jax.numpy as jnp
        import numpy as np
        import math
        BETA = 0.9
        THRESHOLD = 1.0
        NUM_STEPS = 5
        ALPHA = 2.0

        @jax.custom_vjp
        def spike_fn(u):
            return (u > 0).astype(u.dtype)

        def _spike_fwd(u):
            return (spike_fn(u), u)

        def _spike_bwd(u, g):
            s = jnp.pi / 2.0 * ALPHA * u
            return (g * (ALPHA / 2.0) / (1.0 + s * s),)
        spike_fn.defvjp(_spike_fwd, _spike_bwd)
        key = jax.random.key(seed)
        k1, k2, k3 = jax.random.split(key, 3)
        n_embd = 1024
        x = jax.random.normal(k1, (4, 256, n_embd), dtype=jnp.float32)
        W_fc = jax.random.normal(k2, (4 * n_embd, n_embd), dtype=jnp.float32) / math.sqrt(n_embd)
        W_proj = jax.random.normal(k3, (n_embd, 4 * n_embd), dtype=jnp.float32) / math.sqrt(4 * n_embd)
        return {'x': x, 'W_fc': W_fc, 'W_proj': W_proj}
    _L0_ffn_all = _L0_ffn_setup()
    _L0_ffn_in = {k: v for k, v in _L0_ffn_all.items() if k in ('W_fc', 'W_proj')}
    del _L0_ffn_all
    return {'x': x, 'src': src, 'dst': dst, 'L0_gnn_W_self0': _L0_gnn_in['W_self0'], 'L0_gnn_W_neigh0': _L0_gnn_in['W_neigh0'], 'L0_gnn_b0': _L0_gnn_in['b0'], 'L0_gnn_W_self1': _L0_gnn_in['W_self1'], 'L0_gnn_W_neigh1': _L0_gnn_in['W_neigh1'], 'L0_gnn_b1': _L0_gnn_in['b1'], 'L0_ffn_W_fc': _L0_ffn_in['W_fc'], 'L0_ffn_W_proj': _L0_ffn_in['W_proj']}

def reference(x, src, dst, L0_gnn_W_self0, L0_gnn_W_neigh0, L0_gnn_b0, L0_gnn_W_self1, L0_gnn_W_neigh1, L0_gnn_b1, L0_ffn_W_fc, L0_ffn_W_proj):
    import jax
    import jax.numpy as jnp

    def _L0_gnn_ref(x, edge_src, edge_dst, W_self0, W_neigh0, b0, W_self1, W_neigh1, b1):
        import jax, jax.numpy as jnp
        import numpy as np
        N_NODES = 3125
        N_EDGES = 50000
        D = 1024

        def _sage_layer(h, edge_src, edge_dst, deg_inv, W_self, W_neigh, b):
            msg = h[edge_src]
            agg = jax.ops.segment_sum(msg, edge_dst, num_segments=h.shape[0])
            mean = agg * deg_inv[:, None]
            return h @ W_self + mean @ W_neigh + b
        N = x.shape[0]
        deg = jax.ops.segment_sum(jnp.ones_like(edge_dst, dtype=x.dtype), edge_dst, num_segments=N)
        deg_inv = 1.0 / jnp.maximum(deg, 1.0)
        h = jax.nn.relu(_sage_layer(x, edge_src, edge_dst, deg_inv, W_self0, W_neigh0, b0))
        out = _sage_layer(h, edge_src, edge_dst, deg_inv, W_self1, W_neigh1, b1)
        return out

    def _L0_ffn_ref(x, W_fc, W_proj):
        import jax, jax.numpy as jnp
        import numpy as np
        import math
        BETA = 0.9
        THRESHOLD = 1.0
        NUM_STEPS = 5
        ALPHA = 2.0

        @jax.custom_vjp
        def spike_fn(u):
            return (u > 0).astype(u.dtype)

        def _spike_fwd(u):
            return (spike_fn(u), u)

        def _spike_bwd(u, g):
            s = jnp.pi / 2.0 * ALPHA * u
            return (g * (ALPHA / 2.0) / (1.0 + s * s),)
        spike_fn.defvjp(_spike_fwd, _spike_bwd)
        h = jnp.square(jax.nn.relu(jnp.einsum('bsd,fd->bsf', x, W_fc)))
        y = jnp.einsum('bsf,df->bsd', h, W_proj)

        def step(mem, _):
            reset = jax.lax.stop_gradient(spike_fn(mem - THRESHOLD))
            mem_new = BETA * mem + y - reset * THRESHOLD
            spk = spike_fn(mem_new - THRESHOLD)
            return (mem_new, spk)
        mem0 = jnp.zeros_like(y)
        _, spks = jax.lax.scan(step, mem0, None, length=NUM_STEPS)
        return jnp.sum(spks, axis=0) / NUM_STEPS
    x = x + _L0_gnn_ref(_layernorm(x, axis=-1), src, dst, L0_gnn_W_self0, L0_gnn_W_neigh0, L0_gnn_b0, L0_gnn_W_self1, L0_gnn_W_neigh1, L0_gnn_b1)
    x = x + _L0_ffn_ref(_layernorm(x, axis=-1)[None], L0_ffn_W_fc, L0_ffn_W_proj)[0]
    return x

_drawn_inputs = setup_inputs


def setup_inputs(seed=0):
    import zlib

    import numpy as np

    out = dict(_drawn_inputs(seed))
    spreads = {'L0_gnn_b0': (0.0, 0.1), 'L0_gnn_b1': (0.0, 0.1)}
    factors = {}
    for name, (base, spread) in spreads.items():
        noise = np.random.default_rng([zlib.crc32(name.encode()), seed]).standard_normal(out[name].shape)
        drawn = base * np.exp(spread * noise) if base else spread * noise
        out[name] = jnp.asarray(drawn.astype(out[name].dtype))
    for name, factor in factors.items():
        out[name] = (out[name] * factor).astype(out[name].dtype)
    return out
```

```python
from contextlib import ExitStack

import concourse.bass as bass
from concourse import mybir

F32 = mybir.dt.float32
F32R = mybir.dt.float32r
BF16 = mybir.dt.bfloat16
F16 = mybir.dt.float16
I32 = mybir.dt.int32
ALU = mybir.AluOpType
ACT = mybir.ActivationFunctionType
AX = mybir.AxisListType
ds = bass.ds

NODES, D, F, EDGES = 1250, 1024, 4096, 40000
P = 125
TILES = NODES // P
KD = D // 128
CHUNKS = EDGES // P
GROUP = 4
GROUPS = CHUNKS // GROUP
HALF = 512
COUNT_COLS = ((0, 418), (418, 416), (834, 416))
HI, LO = 0, 1
EPS = 1e-5
LN_STEPS = 9
EXACT_COUNT = 4095.0
STEPS, BETA, THRESHOLD = 5, 0.9, 1.0
F_TILE = 128
F_TILES = F // F_TILE
BLOCK = 4
BLOCKS = F_TILES // BLOCK
GROUPS_OF_TILES = ((0, 6, ((0, 376), (376, 374))), (6, 4, ((0, 500),)))
Y_START = 16
LIF_STEPS = 3 * (STEPS - 1) + 2
PASSES = ((HI, HI), (HI, LO), (LO, HI))


def gnn_ffn(nc, x, dst_cols, src_cols, dst_rows, w_self0, w_neigh0, b0, w_self1, w_neigh1, b1,
            w_fc, w_proj, out, stop_after="all"):
    with ExitStack() as ctx:
        def sem(name):
            return ctx.enter_context(nc.semaphore(name))

        counts_dram = nc.dram_tensor("counts_dram", (TILES, P, NODES), F32, kind="Internal").ap()
        at_dram = nc.dram_tensor("at_dram", (TILES, P, TILES, 2, P), F32, kind="Internal").ap()
        xt_dram = [nc.dram_tensor(f"xt{l}_dram", (TILES, 128, 2, KD, P), F32, kind="Internal").ap()
                   for l in range(3)]
        x1_dram = nc.dram_tensor("x1_dram", (NODES, D), F32, kind="Internal").ap()

        cursor = [(nc.sbuf_base + 63) // 64 * 64]

        def at(address, name, shape, dt):
            return nc.alloc_sbuf_tensor_at(name, shape, dt, offset=address)

        def nbytes(shape, dt):
            n = 2 if dt in (BF16, F16) else 4
            for s in shape[1:]:
                n *= s
            return (n + 31) // 32 * 32

        def put(name, shape, dt):
            a = cursor[0]
            cursor[0] += nbytes(shape, dt)
            assert cursor[0] <= nc.sbuf_usable_end, (name, cursor[0])
            return at(a, name, shape, dt)

        ident = put("ident", [128, 128], F32)
        deg = put("deg", [P, TILES, 3], F32)
        dinv = put("dinv", [P, TILES], F32)
        deg_sum = put("deg_sum", [P, TILES], F32)
        deg_max = put("deg_max", [P, 1], F32)
        many = put("many", [1, 1], F32)
        many_int = put("many_int", [1, 1], I32)
        group_range = put("group_range", [1, 2 * TILES], I32)
        eps_col = put("eps_col", [P, 1], F32)
        stats = put("stats", [P, 2, 2, 6], F32)
        mean_var = put("mean_var", [P, 2, 2], F32)
        std = put("std", [P, 2], F32)
        rstd = put("rstd", [P, 2], F32)
        newton = put("newton", [P, 2], F32)
        base = cursor[0]
        z = put("z", [P, TILES, 2, D], F32R)
        w = put("w", [128, KD, 2, D], F32R)
        w_raw = put("w_raw", [128, 2, D], F32)
        xt = [put(f"xt{j}", [128, 2, KD, P], F32R) for j in range(2)]
        at_tile_at = cursor[0]
        at_tile = put("at_tile", [P, TILES, 2, P], F32R)
        rows = [put(f"rows{j}", [P, D], F32) for j in range(4)]
        xt_out_at = cursor[0]
        xt_out = put("xt_out", [128, 2, KD, P], F32R)
        bias = put("bias", [P, D], F32)
        counts_back = at(at_tile_at, "counts_back", [P, 2, NODES], F32)
        turned = at(xt_out_at, "turned", [P, TILES, 2, P], F32R)
        graph_end = cursor[0]

        def put_from(address, *what):
            made = []
            cursor[0] = address
            for name, shape, dt in what:
                made.append(put(name, shape, dt))
            return made

        z_end, w_end = base + nbytes([P, TILES, 2, D], F32R), base + nbytes([P, TILES, 2, D], F32R) + nbytes([128, KD, 2, D], F32R)
        raw_end = w_end + nbytes([128, 2, D], F32)
        n0, n1 = (count * P for _, count, _ in GROUPS_OF_TILES)
        pr_w, hid, y0 = put_from(base, ("pr_w", [128, BLOCK, 2, D], F32R), ("hid", [128, BLOCK, 2, n0], F32R),
                                 ("y0", [P, n0 // P, D], F32))
        assert cursor[0] <= z_end
        x2t0, fc_w = put_from(z_end, ("x2t0", [128, 2, KD, n0], F32R), ("fc_w", [128, 2, KD, 2, F_TILE], F32R))
        assert cursor[0] <= w_end
        (fc_raw,) = put_from(w_end, ("fc_raw", [128, 2, KD, F_TILE], F32))
        pr_raw, relu, square, x2t1, lif_a = put_from(
            raw_end, ("pr_raw", [128, 2, D], F32), ("relu", [128, 2, HALF], F32), ("square", [128, 2, HALF], F32),
            ("x2t1", [128, 2, KD, n1], F32R), ("lif_a", [P, n0 // P * D // BLOCKS], F32))
        assert cursor[0] <= nc.sbuf_usable_end
        y1, x1_0, lif_b, lif_c = put_from(z_end, ("y1", [P, n1 // P, D], F32), ("x1_0", [P, n0 // P, D], F32),
                                          ("lif_b", [P, n0 // P * D // BLOCKS], F32),
                                          ("lif_c", [P, n0 // P * D // BLOCKS], F32))
        assert cursor[0] <= z_end + nbytes([128, 2, KD, n0], F32R)
        x2t1_at = raw_end + nbytes([128, 2, D], F32) + 2 * nbytes([128, 2, HALF], F32)
        x1_1, last_a, last_b, last_c = put_from(x2t1_at, ("x1_1", [P, n1 // P, D], F32), ("last_a", [P, D], F32),
                                                ("last_b", [P, D], F32), ("last_c", [P, D], F32))
        assert cursor[0] <= x2t1_at + nbytes([128, 2, KD, n1], F32R)
        x2t, y, x1_tiles = (x2t0, x2t1), (y0, y1), (x1_0, x1_1)

        cursor[0] = base
        iota = put("iota", [P, NODES], F16)
        edge_int = put("edge_int", [P, 2, CHUNKS], I32)
        src_f = put("src_f", [P, CHUNKS], F32)
        minus_dst_f = put("minus_dst_f", [P, CHUNKS], F32)
        dst_int = put("dst_int", [GROUPS, GROUP * P], I32)
        dst_f = put("dst_f", [GROUPS, GROUP * P], F32)
        group_min = put("group_min", [GROUPS, 1], F32)
        group_max = put("group_max", [GROUPS, 1], F32)
        tile_first = put("tile_first", [GROUPS, TILES], F32)
        tile_next = put("tile_next", [GROUPS, TILES], F32)
        from_end = put("from_end", [GROUPS, TILES], F32)
        from_start = put("from_start", [GROUPS, TILES], F32)
        below = put("below", [GROUPS, TILES], F32)
        above = put("above", [GROUPS, TILES], F32)
        may_hold = put("may_hold", [GROUPS, TILES], F32)
        bounds = put("bounds", [GROUPS, 2 * TILES], F32)
        bound_col = put("bound_col", [2 * TILES, 1], F32)
        range_f = put("range_f", [1, 2 * TILES], F32)
        zero_w = put("zero_w", [P, P], F16)
        src_hot = put("src_hot", [P, GROUP, NODES], BF16)
        dst_hot = put("dst_hot", [P, GROUP, P], BF16)
        dist = put("dist", [P, GROUP, P], BF16)
        counts = put("counts", [P, 2, NODES], F32)
        assert cursor[0] <= base + nbytes([P, TILES, 2, D], F32R)

        bank = ctx.enter_context(nc.psum_tensor("bank", [128, 8, HALF], F32))

        edges_in = sem("edges_in")
        constants = sem("constants")
        edge_steps = sem("edge_steps")
        bounds_turned = sem("bounds_turned")
        range_ready = sem("range_ready")
        src_hot_ready = [sem(f"src_hot_ready{q}") for q in range(GROUP)]
        dst_hot_ready = [sem(f"dst_hot_ready{q}") for q in range(GROUP // 2)]
        dist_ready = [sem(f"dist_ready{q}") for q in range(GROUP // 2)]
        hot_used = [sem(f"hot_used{q}") for q in range(GROUP)]
        counts_summed = sem("counts_summed")
        counts_copied = sem("counts_copied")
        counts_free = sem("counts_free")
        counts_stored = sem("counts_stored")
        counts_in = [sem(f"counts_in{j}") for j in range(2)]
        counts_turned = sem("counts_turned")
        turned_high = sem("turned_high")
        turned_low = sem("turned_low")
        at_stored = sem("at_stored")
        turned_free = sem("turned_free")
        deg_steps = sem("deg_steps")
        deg_turned = sem("deg_turned")
        table_loaded = sem("table_loaded")
        many_ready = sem("many_ready")

        w_in = [sem(f"w_in{q}") for q in range(2)]
        w_high = sem("w_high")
        w_low = sem("w_low")
        w_used = sem("w_used")
        dense_done = sem("dense_done")
        xt_in = [sem(f"xt_in{j}") for j in range(2)]
        xt_stored = [sem(f"xt_stored{l}") for l in range(3)]
        x_in = [sem(f"x_in{j}") for j in range(2)]
        ln_steps = [sem(f"ln_steps{l}") for l in range(2)]
        ln_std = [sem(f"ln_std{l}") for l in range(2)]
        row_ready = [sem(f"row_ready{l}") for l in range(3)]
        row_turned = [sem(f"row_turned{l}") for l in range(3)]
        row_high = [sem(f"row_high{l}") for l in range(3)]
        row_low = [sem(f"row_low{l}") for l in range(3)]
        row_free = [sem(f"row_free{l}") for l in range(3)]
        z_high = sem("z_high")
        z_low = sem("z_low")
        at_in = sem("at_in")
        at_used = sem("at_used")
        bias_in = sem("bias_in")
        self_taken = sem("self_taken")
        x1_ready = sem("x1_ready")
        x1_stored = sem("x1_stored")
        x1_free = sem("x1_free")
        res_in = sem("res_in")
        res_used = sem("res_used")

        x2_in = [sem(f"x2_in{g}") for g in range(2)]
        fc_in = [sem(f"fc_in{q}") for q in range(2)]
        fc_high = sem("fc_high")
        fc_low = sem("fc_low")
        pr_in = [sem(f"pr_in{q}") for q in range(2)]
        pr_high = sem("pr_high")
        pr_low = sem("pr_low")
        hid_summed = sem("hid_summed")
        hid_relu = sem("hid_relu")
        hid_square = sem("hid_square")
        hid_high = sem("hid_high")
        hid_low = sem("hid_low")
        proj_summed = sem("proj_summed")
        y_added = sem("y_added")
        y_zero = sem("y_zero")
        x1_in = [sem(f"x1_in{g}") for g in range(2)]
        lif_steps = [sem(f"lif_steps{g}") for g in range(2)]
        out_stored = sem("out_stored")

        ROUNDS = ((0, 4), (4, 4), (8, 2))
        PAIRS = TILES // 2

        block = ctx.enter_context(nc.Block())


        @block.sync
        def _(sp):
            w_dram = [v.rearrange("(k p) n -> k p n", p=128) for v in (w_neigh0, w_self0, w_neigh1, w_self1)]
            x_tiles = x.rearrange("(t p) d -> t p d", p=P)

            def load_w(phase, k):
                if 8 * phase + k >= 2:
                    sp.wait_ge(w_low, KD * phase + k - 1)
                sp.dma_start(w_raw[:, k % 2, :], w_dram[phase][k]).then_inc(w_in[k % 2], 16)

            def load_xt(phase, n, j):
                sp.wait_ge(dense_done, 2 * (TILES * phase + n - 1))
                sp.dma_start(xt[j][:, :, :, :].bitcast(F32),
                             xt_dram[phase // 2][ds(n, 1)].rearrange("a p h k m -> (a p) h k m")).then_inc(xt_in[j], 16)

            sp.dma_start(dst_int[:, :], dst_rows).then_inc(edges_in, 16)
            sp.dma_start(edge_int[:, 0, :], src_cols).then_inc(edges_in, 16)
            sp.dma_start(edge_int[:, 1, :], dst_cols).then_inc(edges_in, 16)
            sp.dma_start(rows[0][:, :], x_tiles[0]).then_inc(x_in[0], 16)
            sp.dma_start(rows[1][:, :], x_tiles[1]).then_inc(x_in[1], 16)
            for k in range(KD):
                load_w(0, k)
            load_w(1, 0)
            load_w(1, 1)
            sp.wait_ge(counts_stored, 16 * TILES)

            def load_counts(n, j):
                sp.wait_ge(counts_turned, 3 * n - 3)
                sp.dma_start(counts_back[:, j, :], counts_dram[ds(n, 1)].rearrange("a p m -> (a p) m")).then_inc(counts_in[j], 16)

            def load_x(n, j):
                sp.wait_ge(row_ready[0], n - 1)
                sp.dma_start(rows[j][:, :], x_tiles[ds(n, 1)].rearrange("a p d -> (a p) d")).then_inc(x_in[j], 16)

            for j in range(2):
                sp.dma_start(counts_back[:, j, :], counts_dram[j]).then_inc(counts_in[j], 16)
            with sp.Fori(1, PAIRS) as i:
                for j in range(2):
                    load_x(2 * i + j, j)
                    load_counts(2 * i + j, j)

            for l in range(2):
                neigh, own = 2 * l, 2 * l + 1
                if l == 1:
                    load_w(own, 0)
                    load_w(own, 1)
                    sp.wait_ge(xt_stored[1], 32)
                    load_xt(neigh, 1, 1)
                    with sp.Fori(1, PAIRS) as i:
                        for j in range(2):
                            sp.wait_ge(xt_stored[1], 16 * (2 * i + j + 1))
                            load_xt(neigh, 2 * i + j, j)
                sp.wait_ge(xt_stored[l], 16 * TILES)
                load_xt(own, 0, 0)
                for k in range(2, KD):
                    load_w(own, k)
                if l == 0:
                    sp.wait_ge(at_stored, 16 * TILES)
                if l == 1:
                    sp.wait_ge(self_taken, TILES + 1)
                sp.dma_start(bias[:, :], (b0, b1)[l].partition_broadcast(P)).then_inc(bias_in, 16)

                def load_at(n):
                    sp.wait_ge(at_used, TILES * l + n + 1)
                    sp.dma_start(at_tile[:, :, :, :].bitcast(F32),
                                 at_dram[ds(n, 1)].rearrange("a p s h m -> (a p) s h m")).then_inc(at_in, 16)

                def load_res(n):
                    sp.wait_ge(res_used, n + 1)
                    sp.dma_start(rows[0][:, :], x_tiles[ds(n, 1)].rearrange("a p d -> (a p) d")).then_inc(res_in, 16)

                load_at(0)
                load_xt(own, 1, 1)
                if l == 0:
                    load_w(2, 0)
                    load_w(2, 1)
                else:
                    load_res(0)
                    load_res(1)
                with sp.Fori(1, PAIRS) as i:
                    for j in range(2):
                        load_xt(own, 2 * i + j, j)
                        load_at(2 * i + j - 1)
                        if l == 1:
                            load_res(2 * i + j)
                if l == 0:
                    sp.wait_ge(xt_stored[1], 16)
                    load_xt(2, 0, 0)
                load_at(TILES - 1)
                if l == 0:
                    for k in range(2, KD):
                        load_w(2, k)
            if stop_after == "GNN":
                sp.wait_ge(xt_stored[2], 16 * TILES)
                sp.wait_ge(x1_stored, 16 * TILES)
                return

            def load_fc(m, q, f, after_first=True):
                if after_first:
                    sp.wait_ge(fc_low, m - 1)
                sp.dma_start(fc_raw[:, q, :, :], w_fc[ds(f, 1)].rearrange("a p k c -> (a p) k c")).then_inc(fc_in[q], 16)

            def load_pr(m, q, f, after_first=True):
                if after_first:
                    sp.wait_ge(pr_low, m - 1)
                sp.dma_start(pr_raw[:, q, :], w_proj[ds(f, 1)].rearrange("a p d -> (a p) d")).then_inc(pr_in[q], 16)

            sp.wait_ge(w_low, 4 * KD)
            load_fc(0, 0, 0, after_first=False)
            load_fc(1, 1, 1, after_first=False)
            sp.wait_ge(dense_done, 2 * 4 * TILES)
            sp.wait_ge(xt_stored[2], 16 * GROUPS_OF_TILES[0][1])
            for n in range(GROUPS_OF_TILES[0][1]):
                sp.dma_start(x2t0[:, :, :, n * P:(n + 1) * P].bitcast(F32), xt_dram[2][n]).then_inc(x2_in[0], 16)
            load_pr(0, 0, 0, after_first=False)
            load_pr(1, 1, 1, after_first=False)
            for g in range(2):
                with sp.Fori(1 - g, F_TILES // 2) as i:
                    for q in range(2):
                        load_fc(F_TILES * g + 2 * i + q, q, 2 * i + q)
                        load_pr(F_TILES * g + 2 * i + q, q, 2 * i + q)
            sp.wait_ge(out_stored, 16 * TILES)

        @block.gpsimd
        def _(pool):
            nc.gpsimd.iota(tile_first[:, :], pattern=[[P, TILES]], base=0, channel_multiplier=0,
                           allow_small_or_imprecise_dtypes=True).then_inc(constants, 1)
            nc.gpsimd.iota(tile_next[:, :], pattern=[[P, TILES]], base=P, channel_multiplier=0,
                           allow_small_or_imprecise_dtypes=True).then_inc(constants, 1)
            nc.gpsimd.iota(from_start[:, :], pattern=[[0, TILES]], base=1, channel_multiplier=1,
                           allow_small_or_imprecise_dtypes=True).then_inc(constants, 1)
            nc.gpsimd.iota(from_end[:, :], pattern=[[0, TILES]], base=GROUPS, channel_multiplier=-1,
                           allow_small_or_imprecise_dtypes=True).then_inc(constants, 1)
            nc.gpsimd.memset(ident[:, :], 0.0).then_inc(constants, 1)
            pool.wait_ge(constants, 5)
            nc.gpsimd.affine_select(out=ident[:, :], in_=ident[:, :], compare_op=ALU.not_equal, fill=1.0,
                                    base=0, pattern=[[-1, 128]], channel_multiplier=1).then_inc(constants, 1)
            nc.gpsimd.memset(eps_col[:, :], EPS).then_inc(constants, 1)
            nc.gpsimd.memset(zero_w[:, :], 0.0).then_inc(constants, 1)
            nc.gpsimd.iota(iota[:, :], pattern=[[1, NODES]], base=0, channel_multiplier=0,
                           allow_small_or_imprecise_dtypes=True).then_inc(constants, 1)

            for k in range(KD):
                pool.wait_ge(w_in[k % 2], 16 * (k // 2 + 1))
                nc.gpsimd.tensor_copy(w[:, k, HI, :], w_raw[:, k % 2, :]).then_inc(w_high, 1)
                pool.wait_ge(w_high, k + 1)
                nc.gpsimd.tensor_tensor(w[:, k, LO, :], w_raw[:, k % 2, :], w[:, k, HI, :].bitcast(F32),
                                        ALU.subtract).then_inc(w_low, 1)

            pool.sem_inc(counts_free, 2)
            with pool.Fori(0, PAIRS) as i:
                for j in range(2):
                    pool.wait_ge(counts_copied, 2 * i + j + 3)
                    pool.dma_start(counts_dram[ds(2 * i + j, 1)].rearrange("a p m -> (a p) m"),
                                   counts[:, j, :]).then_inc(counts_stored, 16)
                    pool.wait_ge(counts_stored, 16 * (2 * i + j + 1))
                    pool.sem_inc(counts_free, 1)

            def store_xt(l, n, tile):
                pool.wait_ge(row_high[l], 2 * n + 2)
                pool.wait_ge(row_low[l], 2 * n + 4)
                pool.dma_start(xt_dram[l][ds(n, 1)].rearrange("a p h k m -> (a p) h k m"),
                               tile[:, :, :, :].bitcast(F32)).then_inc(xt_stored[l], 16)
                pool.wait_ge(xt_stored[l], 16 * (n + 1))
                pool.sem_inc(row_free[l], 1)

            def store_turned(n):
                pool.wait_ge(turned_high, 3 * n + 3)
                pool.wait_ge(turned_low, 3 * n + 5)
                pool.dma_start(at_dram[ds(n, 1)].rearrange("a p s h m -> (a p) s h m"),
                               turned[:, :, :, :].bitcast(F32)).then_inc(at_stored, 16)
                pool.wait_ge(at_stored, 16 * (n + 1))
                pool.sem_inc(turned_free, 1)

            pool.sem_inc(row_free[0], 2)
            pool.sem_inc(turned_free, 1)
            with pool.Fori(0, PAIRS) as i:
                for j in range(2):
                    store_xt(0, 2 * i + j, xt[j])
                    store_turned(2 * i + j)
            pool.sem_inc(row_free[1], 1)
            with pool.Fori(0, TILES) as n:
                store_xt(1, n, xt_out)
            pool.sem_inc(row_free[2], 1)
            pool.sem_inc(x1_free, 1)
            with pool.Fori(0, TILES) as n:
                pool.wait_ge(x1_ready, n + 1)
                pool.dma_start(x1_dram.rearrange("(t p) d -> t p d", p=P)[ds(n, 1)].rearrange("a p d -> (a p) d"),
                               rows[1][:, :]).then_inc(x1_stored, 16)
                pool.wait_ge(x1_stored, 16 * (n + 1))
                pool.sem_inc(x1_free, 1)
                store_xt(2, n, xt_out)
            if stop_after == "GNN":
                return

            pool.wait_ge(at_used, 2 * TILES + 1)
            nc.gpsimd.memset(y0[:, :, :], 0.0).then_inc(y_zero, 1)
            for n in range(GROUPS_OF_TILES[1][1]):
                pool.dma_start(x2t1[:, :, :, n * P:(n + 1) * P].bitcast(F32),
                               xt_dram[2][GROUPS_OF_TILES[1][0] + n]).then_inc(x2_in[1], 16)
            pool.wait_ge(hid_summed, 2 * F_TILES + 2)
            nc.gpsimd.memset(y1[:, :, :], 0.0).then_inc(y_zero, 1)
            x1_tiled = x1_dram.rearrange("(t p) d -> p t d", p=P)
            out_tiled = out.rearrange("(t p) d -> p t d", p=P)
            pool.dma_start(x1_0[:, :, :], x1_tiled[:, 0:n0 // P, :]).then_inc(x1_in[0], 16)
            pool.wait_ge(hid_summed, 3 * F_TILES + 2)
            pool.dma_start(x1_1[:, :, :], x1_tiled[:, n0 // P:, :]).then_inc(x1_in[1], 16)
            pool.wait_ge(lif_steps[0], LIF_STEPS * BLOCKS + 1)
            for n in range(n0 // P):
                pool.dma_start(out_tiled[:, n, :], x1_0[:, n, :]).then_inc(out_stored, 16)
            for n in range(n1 // P):
                pool.wait_ge(lif_steps[1], LIF_STEPS * (n + 1) + 1)
                pool.dma_start(out_tiled[:, n0 // P + n, :], x1_1[:, n, :]).then_inc(out_stored, 16)

        @block.scalar
        def _(act):
            visit = act.alloc_register("act_visit")
            act.reg_mov(visit, 1)
            act.wait_ge(constants, 9)
            nc.scalar.activation(std[:, 0:1], eps_col[:, :], ACT.Sqrt).then_inc(table_loaded, 1)
            act.wait_ge(edge_steps, 2)
            act.wait_ge(range_ready, 1)
            act.sem_inc(counts_copied, 2)
            for h in range(GROUP // 2):
                act.sem_inc(dst_hot_ready[h], 1)

            def dst_one_hots(t):
                first = act.value_load(group_range[0:1, ds(t, 1)], min_val=0, max_val=GROUPS - 1)
                end = act.value_load(group_range[0:1, ds(t + TILES, 1)], min_val=1, max_val=GROUPS)
                with act.Fori(first, end) as g:
                    for h in range(GROUP // 2):
                        act.wait_ge(dst_hot_ready[h], visit)
                        for q in (2 * h, 2 * h + 1):
                            ins = nc.scalar.activation(dist[:, q, :], iota[:, ds(t * P, P)], ACT.Square,
                                                       bias=minus_dst_f[:, ds(g * GROUP + q, 1)])
                        ins.then_inc(dist_ready[h], 1)
                        act.wait_ge(dist_ready[h], visit)
                        act.wait_ge(hot_used[2 * h + 1], visit)
                        nc.scalar.activation(dst_hot[:, 2 * h:2 * h + 2, :], dist[:, 2 * h:2 * h + 2, :],
                                             ACT.Relu, bias=1.0, scale=-1.0).then_inc(dst_hot_ready[h], 1)
                    act.reg_add(visit, visit, 1)

            def copy_counts(t, j):
                act.wait_ge(counts_summed, t + 1)
                act.wait_ge(counts_free, t + 1)
                for b, (c0, n) in enumerate(COUNT_COLS):
                    ins = nc.scalar.activation(counts[:, j, c0:c0 + n], bank[0:P, 3 * j + b, 0:n], ACT.Copy,
                                               accum_out=deg[:, ds(t, 1), b])
                ins.then_inc(counts_copied, 1)

            dst_one_hots(0)
            dst_one_hots(1)
            copy_counts(0, 0)
            with act.Fori(1, PAIRS) as i:
                dst_one_hots(2 * i)
                copy_counts(2 * i - 1, 1)
                dst_one_hots(2 * i + 1)
                copy_counts(2 * i, 0)
            copy_counts(TILES - 1, 1)

            def standard_deviation(l, n, j):
                act.wait_ge(ln_steps[l], LN_STEPS * n + 4)
                nc.scalar.activation(std[:, j:j + 1], mean_var[:, j, 1:2], ACT.Sqrt,
                                     bias=eps_col[:, :]).then_inc(ln_std[l], 1)

            def high_of_row(l, n, tile, func):
                act.wait_ge(row_free[l], n + 1)
                for q in range(2):
                    act.wait_ge(row_turned[l], 2 * n + q + 1)
                    nc.scalar.activation(tile[:, HI, 4 * q:4 * q + 4, :],
                                         bank[:, 6 + q, 0:4 * P].rearrange("p (k m) -> p k m", k=4),
                                         func).then_inc(row_high[l], 1)

            def high_of_turned(n, j, r):
                s0, c = ROUNDS[r]
                if r == 0:
                    act.wait_ge(turned_free, n + 1)
                act.wait_ge(counts_turned, 3 * n + r + 1)
                nc.scalar.activation(turned[:, s0:s0 + c, HI, :],
                                     bank[0:P, 4 + (3 * j + r) % 2, 0:c * P].rearrange("p (s m) -> p s m", s=c),
                                     ACT.Copy).then_inc(turned_high, 1)

            def high_of_z(l, n, j):
                for q in range(2):
                    act.wait_ge(dense_done, 2 * (2 * TILES * l + n) + q + 1)
                    nc.scalar.activation(z[:, ds(n, 1), HI, q * HALF:(q + 1) * HALF],
                                         bank[0:P, 2 * j + q, :].unsqueeze(1), ACT.Copy).then_inc(z_high, 1)

            def high_of_w(phase):
                def block(k, q):
                    act.wait_ge(w_in[q], 16 * (KD // 2 * phase + 1) + 8 * (k - q))
                    if isinstance(k, int) and k == KD - 1:
                        act.wait_ge(dense_done, 2 * TILES * phase)
                    else:
                        act.wait_ge(w_used, (KD - 1) * (TILES * phase - 1) + k + 1)
                    nc.scalar.activation(w[:, ds(k, 1), HI, :], w_raw[:, q, :].unsqueeze(1),
                                         ACT.Copy).then_inc(w_high, 1)

                with act.Fori(0, KD // 2 - 1) as m:
                    block(2 * m, 0)
                    block(2 * m + 1, 1)
                block(KD - 2, 0)
                block(KD - 1, 1)

            def first_pass(n, j):
                if not isinstance(n, int) or n + 1 < TILES:
                    high_of_row(0, n + 1, xt[1 - j], ACT.Copy)
                high_of_turned(n, j, 0)
                high_of_turned(n, j, 1)
                if not isinstance(n, int) or n + 2 < TILES:
                    standard_deviation(0, n + 2, j)
                if isinstance(n, int) and n == TILES - 1:
                    high_of_w(1)
                high_of_z(0, n, j)
                high_of_turned(n, j, 2)

            standard_deviation(0, 0, 0)
            standard_deviation(0, 1, 1)
            high_of_row(0, 0, xt[0], ACT.Copy)
            with act.Fori(0, PAIRS - 1) as i:
                first_pass(2 * i, 0)
                first_pass(2 * i + 1, 1)
            first_pass(TILES - 2, 0)
            first_pass(TILES - 1, 1)

            with act.Fori(0, TILES - 1) as n:
                high_of_row(1, n, xt_out, ACT.Relu)
            high_of_w(2)
            high_of_z(1, 0, 0)
            high_of_row(1, TILES - 1, xt_out, ACT.Relu)
            high_of_z(1, 1, 1)
            with act.Fori(1, PAIRS - 1) as i:
                high_of_z(1, 2 * i, 0)
                high_of_z(1, 2 * i + 1, 1)
            high_of_z(1, TILES - 2, 0)
            high_of_w(3)
            high_of_z(1, TILES - 1, 1)
            standard_deviation(1, 0, 0)
            with act.Fori(0, PAIRS - 1) as i:
                for j in range(2):
                    high_of_row(2, 2 * i + j, xt_out, ACT.Copy)
                    standard_deviation(1, 2 * i + j + 1, 1 - j)
            high_of_row(2, TILES - 2, xt_out, ACT.Copy)
            standard_deviation(1, TILES - 1, 1)
            high_of_row(2, TILES - 1, xt_out, ACT.Copy)
            if stop_after == "GNN":
                return

            def in_slot(m, q):
                return 16 + 8 * (m - q)

            def high_of_fc(m, q, g):
                act.wait_ge(fc_in[q], in_slot(m, q))
                act.wait_ge(hid_summed, 2 * m if g == 0 else F_TILES + m + 1)
                nc.scalar.activation(fc_w[:, q, :, HI, :], fc_raw[:, q, :, :], ACT.Copy).then_inc(fc_high, 1)

            def high_of_pr(m, j, used):
                act.wait_ge(pr_in[j % 2], in_slot(m, j % 2))
                act.wait_ge(proj_summed, used)
                nc.scalar.activation(pr_w[:, j, HI, :], pr_raw[:, j % 2, :], ACT.Copy).then_inc(pr_high, 1)

            def relu_and_high(bank_index, slot, j, c0, n):
                act.wait_ge(hid_summed, bank_index + 3)
                act.wait_ge(hid_low, bank_index + 1)
                nc.scalar.activation(relu[:, slot, 0:n], bank[:, 4 + slot, 0:n], ACT.Relu).then_inc(hid_relu, 1)
                act.wait_ge(hid_relu, bank_index + 3)
                nc.scalar.activation(hid[:, j, HI, c0:c0 + n], relu[:, slot, 0:n], ACT.Square).then_inc(hid_high, 1)

            act.sem_inc(hid_relu, 2)
            act.wait_ge(dense_done, 2 * 4 * TILES)
            act.wait_ge(fc_in[0], 16)
            nc.scalar.activation(fc_w[:, 0, :, HI, :], fc_raw[:, 0, :, :], ACT.Copy).then_inc(fc_high, 1)
            act.wait_ge(at_used, 2 * TILES + 1)
            act.wait_ge(xt_stored[2], 16 * TILES)

            def ffn_block(g, b, last=False):
                _, count, columns = GROUPS_OF_TILES[g]
                for j in range(BLOCK):
                    m = F_TILES * g + BLOCK * b + j
                    if not (last and j == BLOCK - 1):
                        high_of_fc(m + 1, (j + 1) % 2, g)
                    high_of_pr(m, j, 2 * count * b + 1 + g * 2 * GROUPS_OF_TILES[0][1] * BLOCKS)
                    for c, (c0, n) in enumerate(columns):
                        bank_index = 2 * m + c if g == 0 else F_TILES + m
                        relu_and_high(bank_index, c if g == 0 else j % 2, j, c0, n)

            with act.Fori(0, BLOCKS) as b:
                ffn_block(0, b)
            with act.Fori(0, BLOCKS - 1) as b:
                ffn_block(1, b)
            ffn_block(1, BLOCKS - 1, last=True)

        @block.vector
        def _(dve):
            dve.wait_ge(edges_in, 48)
            nc.vector.tensor_copy(src_f[:, :], edge_int[:, 0, :]).then_inc(edge_steps, 1)
            nc.vector.tensor_scalar(minus_dst_f[:, :], edge_int[:, 1, :], -1.0, None, ALU.mult).then_inc(edge_steps, 1)
            nc.vector.tensor_copy(dst_f[:, :], dst_int[:, :]).then_inc(edge_steps, 1)
            dve.wait_ge(edge_steps, 3)
            nc.vector.tensor_reduce(group_min[:, :], dst_f[:, :], AX.X, ALU.min).then_inc(edge_steps, 1)
            nc.vector.tensor_reduce(group_max[:, :], dst_f[:, :], AX.X, ALU.max).then_inc(edge_steps, 1)
            dve.wait_ge(edge_steps, 5)
            dve.wait_ge(constants, 9)
            nc.vector.tensor_scalar(below[:, :], tile_next[:, :], group_min[:, 0:1], None, ALU.is_gt).then_inc(edge_steps, 1)
            nc.vector.tensor_scalar(above[:, :], tile_first[:, :], group_max[:, 0:1], None, ALU.is_le).then_inc(edge_steps, 1)
            dve.wait_ge(edge_steps, 7)
            nc.vector.tensor_tensor(may_hold[:, :], below[:, :], above[:, :], ALU.mult).then_inc(edge_steps, 1)
            dve.wait_ge(edge_steps, 8)
            nc.vector.tensor_tensor(bounds[:, 0:TILES], may_hold[:, :], from_end[:, :], ALU.mult).then_inc(edge_steps, 1)
            nc.vector.tensor_tensor(bounds[:, TILES:], may_hold[:, :], from_start[:, :], ALU.mult).then_inc(edge_steps, 1)
            dve.wait_ge(bounds_turned, 1)
            nc.vector.tensor_reduce(bound_col[:, :], bank[0:2 * TILES, 6, 0:GROUPS], AX.X, ALU.max).then_inc(edge_steps, 1)
            dve.wait_ge(bounds_turned, 2)
            nc.vector.tensor_scalar(range_f[:, 0:TILES], bank[0:1, 7, 0:TILES], -1.0, float(GROUPS),
                                    ALU.mult, ALU.add).then_inc(edge_steps, 1)
            dve.wait_ge(edge_steps, 12)
            nc.vector.tensor_scalar(range_f[:, 0:TILES], range_f[:, 0:TILES], float(GROUPS - 1), None,
                                    ALU.min).then_inc(edge_steps, 1)
            dve.wait_ge(edge_steps, 13)
            nc.vector.scalar_tensor_tensor(out=range_f[:, TILES:], in0=range_f[:, 0:TILES], scalar=1.0,
                                           in1=bank[0:1, 7, TILES:2 * TILES], op0=ALU.add, op1=ALU.max).then_inc(edge_steps, 1)
            dve.wait_ge(edge_steps, 14)
            nc.vector.tensor_copy(group_range[:, :], range_f[:, :]).then_inc(range_ready, 1)
            dve.wait_ge(range_ready, 1)

            visit = dve.alloc_register("dve_visit")
            dve.reg_mov(visit, 1)

            with dve.Fori(0, TILES) as t:
                first = dve.value_load(group_range[0:1, ds(t, 1)], min_val=0, max_val=GROUPS - 1)
                end = dve.value_load(group_range[0:1, ds(t + TILES, 1)], min_val=1, max_val=GROUPS)
                with dve.Fori(first, end) as g:
                    for q in range(GROUP):
                        dve.wait_ge(hot_used[q], visit)
                        nc.vector.tensor_scalar(src_hot[:, q, :], iota[:, :], src_f[:, ds(g * GROUP + q, 1)],
                                                None, ALU.is_equal).then_inc(src_hot_ready[q], 1)
                    dve.reg_add(visit, visit, 1)

            def layer_norm(l, n, j, source, target):
                for q in range(2):
                    nc.vector.bn_stats(stats[:, j, q, :], source[:, q * HALF:(q + 1) * HALF]).then_inc(ln_steps[l], 1)
                dve.wait_ge(ln_steps[l], LN_STEPS * n + 2)
                nc.vector.memset(newton[:, j:j + 1], 0.0).then_inc(ln_steps[l], 1)
                nc.vector.bn_aggr(mean_var[:, j, :], stats[:, j, :, :]).then_inc(ln_steps[l], 1)
                dve.wait_ge(ln_std[l], n + 1)
                nc.vector.reciprocal(rstd[:, j:j + 1], std[:, j:j + 1]).then_inc(ln_steps[l], 1)
                nc.vector.tensor_scalar(newton[:, j:j + 1], mean_var[:, j, 1:2], EPS, None, ALU.add).then_inc(ln_steps[l], 1)
                dve.wait_ge(ln_steps[l], LN_STEPS * n + 6)
                nc.vector.scalar_tensor_tensor(out=newton[:, j:j + 1], in0=rstd[:, j:j + 1], scalar=rstd[:, j:j + 1],
                                               in1=newton[:, j:j + 1], op0=ALU.mult, op1=ALU.mult).then_inc(ln_steps[l], 1)
                dve.wait_ge(ln_steps[l], LN_STEPS * n + 7)
                nc.vector.tensor_scalar(newton[:, j:j + 1], newton[:, j:j + 1], -0.5, 1.5, ALU.mult, ALU.add).then_inc(ln_steps[l], 1)
                dve.wait_ge(ln_steps[l], LN_STEPS * n + 8)
                nc.vector.tensor_tensor(rstd[:, j:j + 1], rstd[:, j:j + 1], newton[:, j:j + 1], ALU.mult).then_inc(ln_steps[l], 1)
                dve.wait_ge(ln_steps[l], LN_STEPS * n + 9)
                nc.vector.tensor_scalar(target[:, :], source[:, :], mean_var[:, j, 0:1], rstd[:, j:j + 1],
                                        ALU.subtract, ALU.mult).then_inc(row_ready[2 * l], 1)

            def norm_x(n, j):
                if isinstance(n, int):
                    dve.wait_ge(x_in[j], 16 * (n // 2 + 1))
                else:
                    dve.wait_ge(x_in[j], 8 * (n - j) + 16)
                layer_norm(0, n, j, rows[j], rows[2 + j])

            def low_of_row(l, n, tile, relu=False):
                for q in range(2):
                    dve.wait_ge(row_high[l], 2 * n + q + 1)
                    source = bank[:, 6 + q, 0:4 * P].rearrange("p (k m) -> p k m", k=4)
                    high = tile[:, HI, 4 * q:4 * q + 4, :].bitcast(F32)
                    low = tile[:, LO, 4 * q:4 * q + 4, :]
                    if relu:
                        ins = nc.vector.scalar_tensor_tensor(out=low, in0=source, scalar=0.0, in1=high,
                                                             op0=ALU.max, op1=ALU.subtract)
                    else:
                        ins = nc.vector.tensor_tensor(low, source, high, ALU.subtract)
                    ins.then_inc(row_low[l], 1)

            def low_of_turned(n, j, r):
                s0, c = ROUNDS[r]
                dve.wait_ge(turned_high, 3 * n + r + 1)
                nc.vector.tensor_tensor(turned[:, s0:s0 + c, LO, :],
                                        bank[0:P, 4 + (3 * j + r) % 2, 0:c * P].rearrange("p (s m) -> p s m", s=c),
                                        turned[:, s0:s0 + c, HI, :].bitcast(F32), ALU.subtract).then_inc(turned_low, 1)

            def low_of_z(l, n, j):
                for q in range(2):
                    dve.wait_ge(z_high, 2 * TILES * l + 2 * n + q + 1)
                    nc.vector.tensor_tensor(z[:, ds(n, 1), LO, q * HALF:(q + 1) * HALF],
                                            bank[0:P, 2 * j + q, :].unsqueeze(1),
                                            z[:, ds(n, 1), HI, q * HALF:(q + 1) * HALF].bitcast(F32),
                                            ALU.subtract).then_inc(z_low, 1)

            def low_of_w(phase):
                with dve.Fori(0, KD // 2) as m:
                    for q in range(2):
                        dve.wait_ge(w_high, KD * phase + 2 * m + q + 1)
                        nc.vector.tensor_tensor(w[:, ds(2 * m + q, 1), LO, :], w_raw[:, q, :].unsqueeze(1),
                                                w[:, ds(2 * m + q, 1), HI, :].bitcast(F32),
                                                ALU.subtract).then_inc(w_low, 1)

            dve.sem_inc(turned_low, 2)
            dve.sem_inc(z_low, 4)
            for l in range(3):
                dve.sem_inc(row_low[l], 2)
            norm_x(0, 0)
            norm_x(1, 1)

            def first_pass(n, j):
                if not isinstance(n, int) or n + 1 < TILES:
                    low_of_row(0, n + 1, xt[1 - j])
                low_of_turned(n, j, 0)
                low_of_turned(n, j, 1)
                if not isinstance(n, int) or n + 2 < TILES:
                    norm_x(n + 2, j)
                if isinstance(n, int) and n == TILES - 1:
                    low_of_w(1)
                low_of_z(0, n, j)
                low_of_turned(n, j, 2)

            low_of_row(0, 0, xt[0])
            with dve.Fori(0, PAIRS - 1) as i:
                first_pass(2 * i, 0)
                first_pass(2 * i + 1, 1)
            first_pass(TILES - 2, 0)
            first_pass(TILES - 1, 1)

            dve.wait_ge(counts_copied, TILES + 2)
            nc.vector.tensor_reduce(deg_sum[:, :], deg[:, :, :], AX.X, ALU.add).then_inc(deg_steps, 1)
            dve.wait_ge(deg_steps, 1)
            nc.vector.tensor_reduce(deg_max[:, :], deg_sum[:, :], AX.X, ALU.max).then_inc(deg_steps, 1)
            nc.vector.tensor_scalar(dinv[:, :], deg_sum[:, :], 1.0, None, ALU.max).then_inc(deg_steps, 1)
            dve.wait_ge(deg_steps, 3)
            nc.vector.reciprocal(dinv[:, :], dinv[:, :]).then_inc(deg_steps, 1)
            dve.wait_ge(deg_turned, 1)
            nc.vector.tensor_reduce(many[:, :], bank[0:1, 5, 0:P], AX.X, ALU.max).then_inc(deg_steps, 1)
            dve.wait_ge(deg_steps, 5)
            nc.vector.tensor_scalar(many_int[:, :], many[:, :], EXACT_COUNT, None, ALU.is_gt).then_inc(many_ready, 1)

            dve.sem_inc(self_taken, 1)
            dve.sem_inc(res_used, 1)

            def take_self(l, n):
                dve.wait_ge(dense_done, 2 * (TILES * (2 * l + 1) + n + 1))
                if l == 1:
                    dve.wait_ge(x1_free, n + 1)
                if not isinstance(n, int) or n > 0:
                    dve.wait_ge(row_ready[l + 1], n)
                nc.vector.tensor_tensor(rows[1][:, :].rearrange("p (q c) -> p q c", q=2), bank[0:P, 0:2, :],
                                        bias[:, :].rearrange("p (q c) -> p q c", q=2), ALU.add).then_inc(self_taken, 1)
                if l == 1:
                    dve.wait_ge(self_taken, TILES + n + 2)
                    dve.wait_ge(res_in, 16 * (n + 1))
                    nc.vector.tensor_tensor(rows[1][:, :], rows[1][:, :], rows[0][:, :], ALU.add).then_inc(res_used, 1)

            def take_aggregate(l, n, j):
                dve.wait_ge(at_used, TILES * l + n + 2)
                dve.wait_ge((self_taken, res_used)[l], n + 2)
                target = rows[2 + j] if l == 0 else rows[1]
                ins = nc.vector.scalar_tensor_tensor(out=target[:, :].rearrange("p (q c) -> p q c", q=2),
                                                     in0=bank[0:P, 2:4, :], scalar=dinv[:, ds(n, 1)],
                                                     in1=rows[1][:, :].rearrange("p (q c) -> p q c", q=2),
                                                     op0=ALU.mult, op1=ALU.add)
                if l == 0:
                    ins.then_inc(row_ready[1], 1)
                else:
                    ins.then_inc(x1_ready, 1)
                    dve.wait_ge(x1_ready, n + 1)
                    layer_norm(1, n, j, rows[1], rows[2 + j])

            def tile_of_pass(l, n, j):
                take_self(l, n)
                low_of_row(l + 1, n - 1, xt_out, relu=(l == 0))
                if l == 0 and isinstance(n, int):
                    low_of_w(2)
                take_aggregate(l, n, j)

            for l in range(2):
                if l == 1:
                    low_of_z(1, 0, 0)
                    low_of_row(1, TILES - 1, xt_out, relu=True)
                    low_of_z(1, 1, 1)
                    with dve.Fori(1, PAIRS - 1) as i:
                        low_of_z(1, 2 * i, 0)
                        low_of_z(1, 2 * i + 1, 1)
                    low_of_z(1, TILES - 2, 0)
                    low_of_w(3)
                    low_of_z(1, TILES - 1, 1)
                dve.wait_ge(bias_in, 16 * (l + 1))
                take_self(l, 0)
                take_aggregate(l, 0, 0)
                with dve.Fori(0, PAIRS - 1) as i:
                    tile_of_pass(l, 2 * i + 1, 1)
                    tile_of_pass(l, 2 * i + 2, 0)
                tile_of_pass(l, TILES - 1, 1)
            low_of_row(2, TILES - 1, xt_out)
            if stop_after == "GNN":
                return

            def low_of_fc(m, q):
                dve.wait_ge(fc_high, m + 1)
                nc.vector.tensor_tensor(fc_w[:, q, :, LO, :], fc_raw[:, q, :, :],
                                        fc_w[:, q, :, HI, :].bitcast(F32), ALU.subtract).then_inc(fc_low, 1)

            def low_of_pr(m, j):
                dve.wait_ge(pr_high, m + 1)
                nc.vector.tensor_tensor(pr_w[:, j, LO, :], pr_raw[:, j % 2, :],
                                        pr_w[:, j, HI, :].bitcast(F32), ALU.subtract).then_inc(pr_low, 1)

            def square_and_low(bank_index, slot, j, c0, n):
                dve.wait_ge(hid_relu, bank_index + 3)
                dve.wait_ge(hid_low, bank_index + 1)
                nc.vector.tensor_tensor(square[:, slot, 0:n], relu[:, slot, 0:n], relu[:, slot, 0:n],
                                        ALU.mult).then_inc(hid_square, 1)
                dve.wait_ge(hid_square, bank_index + 1)
                dve.wait_ge(hid_high, bank_index + 1)
                nc.vector.tensor_tensor(hid[:, j, LO, c0:c0 + n], square[:, slot, 0:n],
                                        hid[:, j, HI, c0:c0 + n].bitcast(F32), ALU.subtract).then_inc(hid_low, 1)

            def lif_step(g, step, index, inp, x1_part, mem, drive, spikes):
                done = lif_steps[g]
                before = LIF_STEPS * index + step + 1
                kind, s = (step - 1) % 3, (step - 1) // 3
                source = inp if s == 0 else mem
                if step == 0:
                    dve.wait_ge(done, before)
                    nc.vector.tensor_scalar(spikes, inp, THRESHOLD, None, ALU.is_gt).then_inc(done, 1)
                elif step == LIF_STEPS - 1:
                    dve.wait_ge(done, before)
                    nc.vector.scalar_tensor_tensor(out=x1_part, in0=spikes, scalar=1.0 / STEPS, in1=x1_part,
                                                   op0=ALU.mult, op1=ALU.add).then_inc(done, 1)
                elif kind == 0:
                    dve.wait_ge(done, before)
                    nc.vector.scalar_tensor_tensor(out=drive, in0=source, scalar=BETA, in1=inp,
                                                   op0=ALU.mult, op1=ALU.add).then_inc(done, 1)
                elif kind == 1:
                    dve.wait_ge(done, before)
                    nc.vector.scalar_tensor_tensor(out=mem, in0=source, scalar=THRESHOLD, in1=drive,
                                                   op0=ALU.is_gt, op1=ALU.subtract, reverse1=True).then_inc(done, 1)
                else:
                    dve.wait_ge(done, before)
                    nc.vector.scalar_tensor_tensor(out=spikes, in0=mem, scalar=THRESHOLD, in1=spikes,
                                                   op0=ALU.is_gt, op1=ALU.add).then_inc(done, 1)

            width = n0 // P * D // BLOCKS
            y0_flat = y0[:, :, :].rearrange("p t d -> p (t d)")
            x1_0_flat = x1_0[:, :, :].rearrange("p t d -> p (t d)")

            dve.sem_inc(hid_low, 2)
            for g in range(2):
                dve.sem_inc(lif_steps[g], 1)
            dve.sem_inc(y_added, Y_START)
            low_of_fc(0, 0)

            def ffn_block(g, b, last=False):
                _, count, columns = GROUPS_OF_TILES[g]
                first_sum = g * 2 * GROUPS_OF_TILES[0][1] * BLOCKS
                for j in range(BLOCK):
                    m = F_TILES * g + BLOCK * b + j
                    if not (last and j == BLOCK - 1):
                        low_of_fc(m + 1, (j + 1) % 2)
                    low_of_pr(m, j)
                    for c, (c0, n) in enumerate(columns):
                        bank_index = 2 * m + c if g == 0 else F_TILES + m
                        square_and_low(bank_index, c if g == 0 else j % 2, j, c0, n)
                dve.wait_ge(y_zero, g + 1)
                if g == 1:
                    dve.wait_ge(x1_in[0], 16)
                for n in range(count):
                    for q in range(2):
                        index = first_sum + 2 * count * b + 2 * n + q
                        dve.wait_ge(proj_summed, index + 2)
                        dve.wait_ge(y_added, index + 1 + Y_START - 2 * count)
                        part = y[g][:, n, q * HALF:(q + 1) * HALF]
                        nc.vector.tensor_tensor(part, part, bank[0:P, 2 * (n % 2) + q, :], ALU.add).then_inc(y_added, 1)
                        if g == 1:
                            for step in range(2 * (2 * n + q), min(2 * (2 * n + q) + 2, LIF_STEPS)):
                                lif_step(0, step, b, y0_flat[:, ds(b * width, width)],
                                         x1_0_flat[:, ds(b * width, width)], lif_a[:, :], lif_b[:, :], lif_c[:, :])

            with dve.Fori(0, BLOCKS) as b:
                ffn_block(0, b)
            with dve.Fori(0, BLOCKS - 1) as b:
                ffn_block(1, b)
            ffn_block(1, BLOCKS - 1, last=True)
            dve.wait_ge(x1_in[1], 16)
            dve.wait_ge(y_added, Y_START + 2 * TILES * BLOCKS)
            for n in range(n1 // P):
                for step in range(LIF_STEPS):
                    lif_step(1, step, n, y1[:, n, :], x1_1[:, n, :], last_a[:, :], last_b[:, :], last_c[:, :])

        @block.tensor
        def _(pe):
            pe.wait_ge(constants, 9)
            pe.wait_ge(edge_steps, 10)
            nc.tensor.transpose(bank[0:2 * TILES, 6, 0:GROUPS], bounds[:, :], ident[0:GROUPS, 0:GROUPS]).then_inc(bounds_turned, 1)
            pe.wait_ge(edge_steps, 11)
            nc.tensor.matmul(bank[0:1, 7, 0:2 * TILES], bound_col[:, :], ident[0:2 * TILES, 0:2 * TILES],
                             start=True, stop=True).then_inc(bounds_turned, 1)
            pe.wait_ge(range_ready, 1)
            for q in range(GROUP):
                pe.sem_inc(hot_used[q], 1)
            visit = pe.alloc_register("pe_visit")
            pe.reg_mov(visit, 1)
            next_visit = pe.alloc_register("pe_next_visit")
            pe.reg_mov(next_visit, 2)

            def sum_counts(t, j):
                pe.wait_ge(counts_copied, t + 1)
                for b, (c0, n) in enumerate(COUNT_COLS):
                    nc.tensor.matmul(bank[0:P, 3 * j + b, 0:n], zero_w[:, :], iota[:, c0:c0 + n],
                                     start=True, stop=False)
                first = pe.value_load(group_range[0:1, ds(t, 1)], min_val=0, max_val=GROUPS - 1)
                end = pe.value_load(group_range[0:1, ds(t + TILES, 1)], min_val=1, max_val=GROUPS)
                with pe.Fori(first, end) as g:
                    for q in range(GROUP):
                        pe.wait_ge(src_hot_ready[q], visit)
                        if q % 2 == 0:
                            pe.wait_ge(dst_hot_ready[q // 2], next_visit)
                        for b, (c0, n) in enumerate(COUNT_COLS):
                            ins = nc.tensor.matmul(bank[0:P, 3 * j + b, 0:n], dst_hot[:, q, :],
                                                   src_hot[:, q, c0:c0 + n], start=False, stop=False)
                        ins.then_inc(hot_used[q], 1)
                    pe.reg_add(visit, visit, 1)
                    pe.reg_add(next_visit, next_visit, 1)
                for b, (c0, n) in enumerate(COUNT_COLS):
                    ins = nc.tensor.matmul(bank[0:P, 3 * j + b, 0:n], zero_w[:, :], iota[:, c0:c0 + n],
                                           start=False, stop=True)
                ins.then_inc(counts_summed, 1)

            with pe.Fori(0, PAIRS) as i:
                sum_counts(2 * i, 0)
                sum_counts(2 * i + 1, 1)

            pe.sem_inc(at_used, 1)

            def turn_row(l, n, j):
                pe.wait_ge(row_ready[l], n + 1)
                for q in range(2):
                    pe.wait_ge(row_low[l], 2 * n + q + 1)
                    for k in range(4):
                        c = (4 * q + k) * 128
                        ins = nc.tensor.transpose(bank[:, 6 + q, k * P:(k + 1) * P], rows[2 + j][:, c:c + 128],
                                                  ident[0:P, 0:P])
                    ins.then_inc(row_turned[l], 1)

            def turn_counts(n, j, r):
                s0, c = ROUNDS[r]
                if r == 0:
                    if isinstance(n, int):
                        pe.wait_ge(counts_in[j], 16 * (n // 2 + 1))
                    else:
                        pe.wait_ge(counts_in[j], 8 * (n - j) + 16)
                pe.wait_ge(turned_low, 3 * n + r + 1)
                for s in range(c):
                    ins = nc.tensor.transpose(bank[0:P, 4 + (3 * j + r) % 2, s * P:(s + 1) * P],
                                              counts_back[:, j, (s0 + s) * P:(s0 + s + 1) * P], ident[0:P, 0:P])
                ins.then_inc(counts_turned, 1)

            def dense(phase, n, j, first_bank):
                if phase > 0:
                    if isinstance(n, int):
                        pe.wait_ge(xt_in[j], 16 * (PAIRS * (phase - 1) + n // 2 + 1))
                    else:
                        pe.wait_ge(xt_in[j], 16 * (PAIRS * (phase - 1) + 1) + 8 * (n - j))
                for k in range(KD):
                    if isinstance(n, int) and n == 0:
                        pe.wait_ge(w_low, KD * phase + k + 1)
                    for m, (a, b) in enumerate(PASSES):
                        for q in range(2):
                            ins = nc.tensor.matmul(bank[0:P, first_bank + q, :], xt[j][:, a, k, :],
                                                   w[:, k, b, q * HALF:(q + 1) * HALF],
                                                   start=(k == 0 and m == 0), stop=(k == KD - 1 and m == 2))
                            if k == KD - 1 and m == 2:
                                ins.then_inc(dense_done, 1)
                    if k < KD - 1:
                        ins.then_inc(w_used, 1)

            def z_of_tile(l, n, j):
                pe.wait_ge(z_low, 2 * TILES * l + 2 * n + 2)
                dense(2 * l, n, j, 2 * j)

            def first_pass(n, j):
                if not isinstance(n, int) or n + 1 < TILES:
                    turn_row(0, n + 1, 1 - j)
                turn_counts(n, j, 0)
                turn_counts(n, j, 1)
                pe.wait_ge(row_low[0], 2 * n + 4)
                z_of_tile(0, n, j)
                turn_counts(n, j, 2)

            turn_row(0, 0, 0)
            first_pass(0, 0)
            first_pass(1, 1)
            with pe.Fori(1, PAIRS - 1) as i:
                first_pass(2 * i, 0)
                first_pass(2 * i + 1, 1)
            first_pass(TILES - 2, 0)
            first_pass(TILES - 1, 1)

            pe.wait_ge(deg_steps, 2)
            pe.wait_ge(turned_low, 3 * TILES + 2)
            nc.tensor.transpose(bank[0:1, 5, 0:P], deg_max[:, :], ident[0:P, 0:P]).then_inc(deg_turned, 1)
            pe.wait_ge(many_ready, 1)
            big_counts = pe.value_load(many_int[0:1, 0:1], min_val=0, max_val=1)

            def self_of_tile(l, n, j):
                pe.wait_ge(self_taken, TILES * l + n + 1)
                dense(2 * l + 1, n, j, 0)

            def aggregate(l, n):
                pe.wait_ge(at_in, 16 * (TILES * l + n + 1))
                if isinstance(n, int) and n == 0:
                    pe.wait_ge(z_low, 2 * TILES * (l + 1) + 4)
                else:
                    pe.wait_ge((row_ready[1], x1_ready)[l], n)

                def products(part, s):
                    for b in (HI, LO):
                        for q in range(2):
                            first = part == HI and s == 0 and b == HI
                            last = part == HI and s == TILES - 1 and b == LO
                            ins = nc.tensor.matmul(bank[0:P, 2 + q, :], at_tile[:, s, part, :],
                                                   z[:, s, b, q * HALF:(q + 1) * HALF], start=first, stop=last)
                    return ins

                for s in range(TILES - 1):
                    products(HI, s)
                with pe.If(big_counts):
                    for s in range(TILES):
                        products(LO, s)
                products(HI, TILES - 1).then_inc(at_used, 1)

            for l in range(2):
                if l == 1:
                    pe.wait_ge(self_taken, TILES + 1)
                    z_of_tile(1, 0, 0)
                    turn_row(1, TILES - 1, 1)
                    pe.wait_ge(row_ready[1], TILES)
                    z_of_tile(1, 1, 1)
                    with pe.Fori(1, PAIRS) as i:
                        z_of_tile(1, 2 * i, 0)
                        z_of_tile(1, 2 * i + 1, 1)
                pe.wait_ge(z_low, 2 * TILES * (l + 1) + 2)
                self_of_tile(l, 0, 0)
                aggregate(l, 0)

                def tile_of_pass(n, j):
                    self_of_tile(l, n, j)
                    turn_row(l + 1, n - 1, 1 - j)
                    aggregate(l, n)

                with pe.Fori(0, PAIRS - 1) as i:
                    tile_of_pass(2 * i + 1, 1)
                    tile_of_pass(2 * i + 2, 0)
                tile_of_pass(TILES - 1, 1)
            turn_row(2, TILES - 1, 1)
            if stop_after == "GNN":
                return

            pe.sem_inc(hid_summed, 2)
            pe.sem_inc(proj_summed, 1)

            def ffn_block(g, b):
                _, count, columns = GROUPS_OF_TILES[g]
                first_sum = g * 2 * GROUPS_OF_TILES[0][1] * BLOCKS
                banks = len(columns)
                for j in range(BLOCK):
                    m = F_TILES * g + BLOCK * b + j
                    pe.wait_ge(fc_low, m + 1)
                    for c, (c0, n) in enumerate(columns):
                        bank_index = 2 * m + c if g == 0 else F_TILES + m
                        slot = c if g == 0 else j % 2
                        pe.wait_ge(hid_relu, bank_index + 1)
                        for k in range(KD):
                            for i, (a, v) in enumerate(PASSES):
                                ins = nc.tensor.matmul(bank[:, 4 + slot, 0:n], fc_w[:, j % 2, k, a, :],
                                                       x2t[g][:, v, k, c0:c0 + n],
                                                       start=(k == 0 and i == 0), stop=(k == KD - 1 and i == 2))
                        ins.then_inc(hid_summed, 1)
                first_hid = (2 * F_TILES) * g + BLOCK * banks * b
                pe.wait_ge(pr_low, F_TILES * g + BLOCK * (b + 1))
                for n in range(count):
                    for q in range(2):
                        pe.wait_ge(y_added, first_sum + 2 * count * b + 2 * n + q + Y_START - 3)
                        for j in range(BLOCK):
                            if n == 0 and q == 0 and j in (0, BLOCK - 1):
                                pe.wait_ge(hid_low, first_hid + banks * (j if j else BLOCK - 1) + 2 + (1 if j else 0))
                            if banks == 2 and n == 3 and q == 0 and j == 0:
                                pe.wait_ge(hid_low, first_hid + banks * BLOCK + 2)
                            for i, (a, v) in enumerate(PASSES):
                                ins = nc.tensor.matmul(bank[0:P, 2 * (n % 2) + q, :], hid[:, j, a, n * P:(n + 1) * P],
                                                       pr_w[:, j, v, q * HALF:(q + 1) * HALF],
                                                       start=(j == 0 and i == 0), stop=(j == BLOCK - 1 and i == 2))
                        ins.then_inc(proj_summed, 1)

            for g in range(2):
                pe.wait_ge(x2_in[g], 16 * GROUPS_OF_TILES[g][1])
                with pe.Fori(0, BLOCKS) as b:
                    ffn_block(g, b)


def kernel(x, src, dst, L0_gnn_W_self0, L0_gnn_W_neigh0, L0_gnn_b0, L0_gnn_W_self1, L0_gnn_W_neigh1, L0_gnn_b1,
           L0_ffn_W_fc, L0_ffn_W_proj):
    import numpy as np
    import concourse.bacc as bacc
    from concourse.bass_utils import run_bass_kernel_spmd

    def columns(edges):
        return np.asarray(edges).reshape(CHUNKS, P).T

    arrays = {
        "x": x,
        "dst_cols": columns(dst),
        "src_cols": columns(src),
        "dst_rows": np.asarray(dst).reshape(GROUPS, GROUP * P),
        "w_self0": L0_gnn_W_self0, "w_neigh0": L0_gnn_W_neigh0, "b0": L0_gnn_b0,
        "w_self1": L0_gnn_W_self1, "w_neigh1": L0_gnn_W_neigh1, "b1": L0_gnn_b1,
        "w_fc": np.asarray(L0_ffn_W_fc).reshape(F_TILES, F_TILE, KD, 128).transpose(0, 3, 2, 1),
        "w_proj": np.asarray(L0_ffn_W_proj).T.reshape(F_TILES, F_TILE, D),
    }
    arrays = {name: np.ascontiguousarray(a) for name, a in arrays.items()}
    nc = bacc.Bacc("TRN2", target_bir_lowering=False, num_devices=1)
    args = {name: nc.dram_tensor(name, a.shape, mybir.dt.from_np(a.dtype), kind="ExternalInput").ap()
            for name, a in arrays.items()}
    args["out"] = nc.dram_tensor("out", (NODES, D), F32, kind="ExternalOutput").ap()
    gnn_ffn(nc, **args)
    result = run_bass_kernel_spmd(nc, [arrays], core_ids=[0])
    return result.results[0]["out"]
```

```python
from contextlib import ExitStack

import concourse.bass as bass
from concourse import mybir

F32 = mybir.dt.float32
F32R = mybir.dt.float32r
BF16 = mybir.dt.bfloat16
F16 = mybir.dt.float16
I32 = mybir.dt.int32
ALU = mybir.AluOpType
ACT = mybir.ActivationFunctionType
AX = mybir.AxisListType
ds = bass.ds

NODES, D, F, EDGES = 1250, 1024, 4096, 40000
P = 125
TILES = NODES // P
KD = D // 128
CHUNKS = EDGES // P
GROUP = 4
GROUPS = CHUNKS // GROUP
HALF = 512
COUNT_COLS = ((0, 418), (418, 416), (834, 416))
HI, LO = 0, 1
EPS = 1e-5
LN_STEPS = 9
EXACT_COUNT = 4095.0
STEPS, BETA, THRESHOLD = 5, 0.9, 1.0
F_TILE = 128
F_TILES = F // F_TILE
BLOCK = 4
BLOCKS = F_TILES // BLOCK
GROUPS_OF_TILES = ((0, 6, ((0, 376), (376, 374))), (6, 4, ((0, 500),)))
Y_START = 16
ADDED = (2 * GROUPS_OF_TILES[0][1] * BLOCKS, 2 * GROUPS_OF_TILES[1][1] * (BLOCKS - 1))
LIF_STEPS = 3 * (STEPS - 1) + 2
SPIKE_SLOTS = 6
MEM_STEPS = 2 * (STEPS - 1)
PASSES = ((HI, HI), (HI, LO), (LO, HI))


def gnn_ffn(nc, x, dst_cols, src_cols, dst_rows, w_self0, w_neigh0, b0, w_self1, w_neigh1, b1,
            w_fc, w_proj, out):
    with ExitStack() as ctx:
        def sem(name):
            return ctx.enter_context(nc.semaphore(name))

        counts_dram = nc.dram_tensor("counts_dram", (TILES, P, NODES), F32, kind="Internal").ap()
        at_dram = nc.dram_tensor("at_dram", (TILES, P, TILES, 2, P), F32, kind="Internal").ap()
        xt_dram = [nc.dram_tensor(f"xt{l}_dram", (TILES, 128, 2, KD, P), F32, kind="Internal").ap()
                   for l in range(2)]
        x2_dram = [nc.dram_tensor(f"x2{g}_dram", (128, KD, 2, count * P), F32, kind="Internal").ap()
                   for g, (_, count, _) in enumerate(GROUPS_OF_TILES)]
        x1_dram = nc.dram_tensor("x1_dram", (NODES, D), F32, kind="Internal").ap()

        cursor = [(nc.sbuf_base + 63) // 64 * 64]

        def at(address, name, shape, dt):
            return nc.alloc_sbuf_tensor_at(name, shape, dt, offset=address)

        def nbytes(shape, dt):
            n = 2 if dt in (BF16, F16) else 4
            for s in shape[1:]:
                n *= s
            return (n + 31) // 32 * 32

        def put(name, shape, dt):
            a = cursor[0]
            cursor[0] += nbytes(shape, dt)
            assert cursor[0] <= nc.sbuf_usable_end, (name, cursor[0])
            return at(a, name, shape, dt)

        ident = put("ident", [128, 128], F32)
        deg = put("deg", [P, TILES, 3], F32)
        dinv = put("dinv", [P, TILES], F32)
        deg_sum = put("deg_sum", [P, TILES], F32)
        deg_max = put("deg_max", [P, 1], F32)
        many = put("many", [1, 1], F32)
        many_int = put("many_int", [1, 1], I32)
        group_range = put("group_range", [1, 2 * TILES], I32)
        eps_col = put("eps_col", [P, 1], F32)
        stats = put("stats", [P, 2, 2, 6], F32)
        mean_var = put("mean_var", [P, 2, 2], F32)
        std = put("std", [P, 2], F32)
        rstd = put("rstd", [P, 2], F32)
        newton = put("newton", [P, 2], F32)
        ident_narrow = put("ident_narrow", [P, P], BF16)
        base = cursor[0]
        z = put("z", [P, TILES, 2, D], F32R)
        w_at = cursor[0]
        w = put("w", [128, KD, 2, D], F32R)
        w_landing = at(w_at, "w_landing", [128, KD, 2, D], F32)
        w_raw = put("w_raw", [128, 2, D], F32)
        xt = [put(f"xt{j}", [128, 2, KD, P], F32R) for j in range(2)]
        at_tile_at = cursor[0]
        at_tile = put("at_tile", [P, TILES, 2, P], F32R)
        rows = [put(f"rows{j}", [P, D], F32) for j in range(4)]
        xt_out_at = cursor[0]
        xt_out = put("xt_out", [128, 2, KD, P], F32R)
        bias = put("bias", [P, D], F32)
        counts_back = at(at_tile_at, "counts_back", [P, 2, NODES], F32)
        turned = at(xt_out_at, "turned", [P, TILES, 2, P], F32R)
        graph_end = cursor[0]

        def put_from(address, *what):
            made = []
            cursor[0] = address
            for name, shape, dt in what:
                made.append(put(name, shape, dt))
            return made

        z_end, w_end = base + nbytes([P, TILES, 2, D], F32R), base + nbytes([P, TILES, 2, D], F32R) + nbytes([128, KD, 2, D], F32R)
        raw_end = w_end + nbytes([128, 2, D], F32)
        n0, n1 = (count * P for _, count, _ in GROUPS_OF_TILES)
        pr_w, hid, y0 = put_from(base, ("pr_w", [128, BLOCK, 2, D], F32R), ("hid", [128, BLOCK, 2, n0], F32R),
                                 ("y0", [P, n0 // P, D], F32))
        assert cursor[0] <= z_end
        x2t0, fc_w = put_from(z_end, ("x2t0", [128, KD, 2, n0], F32R), ("fc_w", [128, 2, KD, 2, F_TILE], F32R))
        assert cursor[0] <= w_end
        (fc_raw,) = put_from(w_end, ("fc_raw", [128, 2, KD, F_TILE], F32))
        pr_raw, relu, square, x2t1, lif_a = put_from(
            raw_end, ("pr_raw", [128, 2, D], F32), ("relu", [128, 2, HALF], F32), ("square", [128, 2, HALF], F32),
            ("x2t1", [128, KD, 2, n1], F32R), ("lif_a", [P, D], F32))
        assert cursor[0] <= nc.sbuf_usable_end
        y1, x1_0, lif_b = put_from(z_end, ("y1", [P, n1 // P, D], F32), ("x1_0", [P, n0 // P, D], F32),
                                   ("lif_b", [P, D], F32))
        assert cursor[0] <= z_end + nbytes([128, KD, 2, n0], F32R)
        hid_at = base + nbytes([128, BLOCK, 2, D], F32R)
        hid1, lif_c = put_from(hid_at, ("hid1", [128, BLOCK, 2, n1], F32R), ("lif_c", [P, D], F32))
        assert cursor[0] <= hid_at + nbytes([128, BLOCK, 2, n0], F32R)
        x2t1_at = raw_end + nbytes([128, 2, D], F32) + 2 * nbytes([128, 2, HALF], F32)
        x1_1, sign, spikes = put_from(x2t1_at, ("x1_1", [P, n1 // P, D], F32), ("sign", [P, D], BF16),
                                      ("spikes", [P, SPIKE_SLOTS, D], BF16))
        assert cursor[0] <= x2t1_at + nbytes([128, KD, 2, n1], F32R)
        y0_at = hid_at + nbytes([128, BLOCK, 2, n0], F32R)
        hid1_more, pr_w4 = put_from(y0_at, ("hid1_more", [128, BLOCK, 2, n1], F32R), ("pr_w4", [128, 2, D], F32R))
        assert cursor[0] <= y0_at + nbytes([P, n0 // P, D], F32)
        x1_0_at = z_end + nbytes([P, n1 // P, D], F32)
        pr_w_more = [pr_w4] + put_from(x1_0_at, *((f"pr_w{j}", [128, 2, D], F32R) for j in range(BLOCK + 1, 2 * BLOCK)))
        assert cursor[0] <= x1_0_at + nbytes([P, n0 // P, D], F32)

        def hid_of(g, j):
            return (hid, hid1)[g][:, j, :, :] if j < BLOCK else hid1_more[:, j - BLOCK, :, :]

        def pr_of(j):
            return pr_w[:, j, :, :] if j < BLOCK else pr_w_more[j - BLOCK][:, :, :]
        x2t, y = (x2t0, x2t1), (y0, y1)

        cursor[0] = base
        iota = put("iota", [P, NODES], F16)
        edge_int = put("edge_int", [P, 2, CHUNKS], I32)
        src_f = put("src_f", [P, CHUNKS], F32)
        dst_f = put("dst_f", [P, CHUNKS], F32)
        minus_dst_f = put("minus_dst_f", [P, CHUNKS], F32)
        dst_int = put("dst_int", [GROUPS, GROUP * P], I32)
        dst_rows_f = put("dst_rows_f", [GROUPS, GROUP * P], F32)
        group_min = put("group_min", [GROUPS, 1], F32)
        group_max = put("group_max", [GROUPS, 1], F32)
        tile_first = put("tile_first", [GROUPS, TILES], F32)
        tile_next = put("tile_next", [GROUPS, TILES], F32)
        from_end = put("from_end", [GROUPS, TILES], F32)
        from_start = put("from_start", [GROUPS, TILES], F32)
        below = put("below", [GROUPS, TILES], F32)
        above = put("above", [GROUPS, TILES], F32)
        may_hold = put("may_hold", [GROUPS, TILES], F32)
        bounds = put("bounds", [GROUPS, 2 * TILES], F32)
        bound_col = put("bound_col", [2 * TILES, 1], F32)
        range_f = put("range_f", [1, 2 * TILES], F32)
        zero_w = put("zero_w", [P, P], F16)
        src_hot = put("src_hot", [P, GROUP, NODES], BF16)
        dst_hot = put("dst_hot", [P, GROUP, P], BF16)
        dist = put("dist", [P, GROUP, P], BF16)
        counts = put("counts", [P, 2, NODES], F32)
        assert cursor[0] <= base + nbytes([P, TILES, 2, D], F32R)

        bank = ctx.enter_context(nc.psum_tensor("bank", [128, 8, HALF], F32))

        edges_in = sem("edges_in")
        constants = sem("constants")
        edge_steps = sem("edge_steps")
        bounds_turned = sem("bounds_turned")
        range_ready = sem("range_ready")
        src_hot_ready = [sem(f"src_hot_ready{q}") for q in range(GROUP)]
        dst_hot_ready = [sem(f"dst_hot_ready{q}") for q in range(GROUP // 2)]
        dist_ready = [sem(f"dist_ready{q}") for q in range(GROUP // 2)]
        hot_used = [sem(f"hot_used{q}") for q in range(GROUP)]
        counts_summed = sem("counts_summed")
        counts_copied = sem("counts_copied")
        counts_free = sem("counts_free")
        counts_stored = sem("counts_stored")
        counts_in = [sem(f"counts_in{j}") for j in range(2)]
        counts_turned = sem("counts_turned")
        turned_high = sem("turned_high")
        turned_low = sem("turned_low")
        at_stored = sem("at_stored")
        turned_free = sem("turned_free")
        deg_steps = sem("deg_steps")
        deg_turned = sem("deg_turned")
        table_loaded = sem("table_loaded")
        many_ready = sem("many_ready")

        w_in = [sem(f"w_in{k}") for k in range(KD)]
        w_high = sem("w_high")
        w_low = sem("w_low")
        w_used = sem("w_used")
        dense_done = sem("dense_done")
        xt_in = [sem(f"xt_in{j}") for j in range(2)]
        xt_stored = [sem(f"xt_stored{l}") for l in range(2)]
        x2_stored = sem("x2_stored")
        x_in = [sem(f"x_in{j}") for j in range(2)]
        ln_steps = [sem(f"ln_steps{l}") for l in range(2)]
        ln_std = [sem(f"ln_std{l}") for l in range(2)]
        row_ready = [sem(f"row_ready{l}") for l in range(3)]
        row_turned = [sem(f"row_turned{l}") for l in range(3)]
        row_high = [sem(f"row_high{l}") for l in range(3)]
        row_low = [sem(f"row_low{l}") for l in range(3)]
        row_free = [sem(f"row_free{l}") for l in range(3)]
        z_high = sem("z_high")
        z_low = sem("z_low")
        at_in = sem("at_in")
        at_used = sem("at_used")
        bias_in = sem("bias_in")
        self_taken = sem("self_taken")
        x1_ready = sem("x1_ready")
        x1_stored = sem("x1_stored")
        x1_free = sem("x1_free")
        res_in = sem("res_in")
        res_used = sem("res_used")

        x2_in = [sem(f"x2_in{k}") for k in range(KD)]
        x2_in_last = sem("x2_in_last")
        fc_in = [sem(f"fc_in{q}") for q in range(2)]
        fc_high = sem("fc_high")
        fc_low = sem("fc_low")
        pr_in = [sem(f"pr_in{q}") for q in range(2)]
        pr_high = sem("pr_high")
        pr_low = sem("pr_low")
        hid_summed = sem("hid_summed")
        hid_relu = sem("hid_relu")
        hid_square = sem("hid_square")
        hid_high = sem("hid_high")
        hid_low = sem("hid_low")
        proj_summed = sem("proj_summed")
        y_added = sem("y_added")
        y_zero = sem("y_zero")
        x1_in = [sem(f"x1_in{g}") for g in range(2)]
        lif_steps = sem("lif_steps")
        mem_steps = sem("mem_steps")
        signs = sem("signs")
        spikes_ready = sem("spikes_ready")
        spikes_counted = sem("spikes_counted")
        result_ready = sem("result_ready")
        out_stored = [sem(f"out_stored{g}") for g in range(2)]

        ROUNDS = ((0, 4), (4, 4), (8, 2))
        PAIRS = TILES // 2

        def raw_w(k):
            return w_raw[:, k, :] if k < 2 else w_landing[:, k, LO, :]

        block = ctx.enter_context(nc.Block())

        @block.sync
        def _(sp):
            w_dram = [v.rearrange("(k p) n -> k p n", p=128) for v in (w_neigh0, w_self0, w_neigh1, w_self1)]
            x_tiles = x.rearrange("(t p) d -> t p d", p=P)

            def load_w(phase, k):
                if phase > 0:
                    if k < 2:
                        sp.wait_ge(w_low, KD * (phase - 1) + k + 1)
                    elif k < KD - 1:
                        sp.wait_ge(w_used, (KD - 1) * (TILES * phase - 1) + k + 1)
                    else:
                        sp.wait_ge(dense_done, 2 * TILES * phase)
                sp.dma_start(raw_w(k), w_dram[phase][k]).then_inc(w_in[k], 16)

            def load_xt(phase, n, j):
                sp.wait_ge(dense_done, 2 * (TILES * phase + n - 1))
                sp.dma_start(xt[j][:, :, :, :].bitcast(F32),
                             xt_dram[phase // 2][ds(n, 1)].rearrange("a p h k m -> (a p) h k m")).then_inc(xt_in[j], 16)

            sp.dma_start(dst_int[:, :], dst_rows).then_inc(edges_in, 16)
            sp.dma_start(edge_int[:, 0, :], src_cols).then_inc(edges_in, 16)
            sp.dma_start(edge_int[:, 1, :], dst_cols).then_inc(edges_in, 16)
            sp.dma_start(rows[0][:, :], x_tiles[0]).then_inc(x_in[0], 16)
            sp.dma_start(rows[1][:, :], x_tiles[1]).then_inc(x_in[1], 16)
            for k in range(KD):
                load_w(0, k)
            load_w(1, 0)
            load_w(1, 1)

            def load_counts(n, j):
                sp.wait_ge(counts_stored, 16 * (n + 1))
                if not isinstance(n, int) or n > 1:
                    sp.wait_ge(counts_turned, 3 * n - 3)
                sp.dma_start(counts_back[:, j, :], counts_dram[ds(n, 1)].rearrange("a p m -> (a p) m")).then_inc(counts_in[j], 16)

            def load_x(n, j):
                sp.wait_ge(row_ready[0], n - 1)
                sp.dma_start(rows[j][:, :], x_tiles[ds(n, 1)].rearrange("a p d -> (a p) d")).then_inc(x_in[j], 16)

            load_counts(0, 0)
            load_counts(1, 1)
            with sp.Fori(1, PAIRS) as i:
                for j in range(2):
                    load_x(2 * i + j, j)
                    load_counts(2 * i + j, j)

            def load_rest(phase, stored, need):
                sp.wait_ge(stored, need[0])
                load_xt(phase, 0, 0)
                for k in range(2, KD):
                    load_w(phase, k)
                sp.wait_ge(stored, need[1])
                load_xt(phase, 1, 1)

            for l in range(2):
                own = 2 * l + 1
                if l == 1:
                    load_rest(2, xt_stored[1], (16, 32))
                    load_w(own, 0)
                    load_w(own, 1)
                    with sp.Fori(1, PAIRS) as i:
                        for j in range(2):
                            sp.wait_ge(xt_stored[1], 16 * (2 * i + j + 1))
                            load_xt(2, 2 * i + j, j)
                load_rest(own, xt_stored[l], (16 * (TILES - 1), 16 * TILES))

                def load_at(n):
                    sp.wait_ge(at_used, TILES * l + n + 1)
                    sp.dma_start(at_tile[:, :, :, :].bitcast(F32),
                                 at_dram[ds(n, 1)].rearrange("a p s h m -> (a p) s h m")).then_inc(at_in, 16)

                def load_res(n):
                    sp.wait_ge(res_used, n + 1)
                    sp.dma_start(rows[0][:, :], x_tiles[ds(n, 1)].rearrange("a p d -> (a p) d")).then_inc(res_in, 16)

                if l == 0:
                    sp.wait_ge(counts_turned, 3 * TILES)
                load_at(0)
                if l == 0:
                    sp.wait_ge(at_stored, 16 * TILES)
                else:
                    sp.wait_ge(self_taken, TILES + 1)
                sp.dma_start(bias[:, :], (b0, b1)[l].partition_broadcast(P)).then_inc(bias_in, 16)
                if l == 0:
                    load_w(2, 0)
                    load_w(2, 1)
                else:
                    load_res(0)
                    load_res(1)
                with sp.Fori(1, PAIRS) as i:
                    for j in range(2):
                        load_xt(own, 2 * i + j, j)
                        load_at(2 * i + j - 1)
                        if l == 1:
                            load_res(2 * i + j)
                load_at(TILES - 1)

            def load_fc(m, q, f, after_first=True):
                if after_first:
                    sp.wait_ge(fc_low, m - 1)
                sp.dma_start(fc_raw[:, q, :, :], w_fc[ds(f, 1)].rearrange("a p k c -> (a p) k c")).then_inc(fc_in[q], 16)

            def load_pr(m, q, f, after_first=True):
                if after_first:
                    sp.wait_ge(pr_low, m - 1)
                sp.dma_start(pr_raw[:, q, :], w_proj[ds(f, 1)].rearrange("a p d -> (a p) d")).then_inc(pr_in[q], 16)

            sp.wait_ge(w_low, 4 * KD)
            load_fc(0, 0, 0, after_first=False)
            load_fc(1, 1, 1, after_first=False)
            sp.wait_ge(x2_stored, 32 * GROUPS_OF_TILES[0][1])
            sp.wait_ge(x1_stored, 16 * (TILES - 1))
            for k in range(KD):
                last_w = ((k + 1) * 2 * n0 - 1) // (2 * D)
                assert last_w < KD - 1
                sp.wait_ge(w_used, (KD - 1) * (4 * TILES - 1) + last_w + 1)
                sp.dma_start(x2t0[:, k, :, :].bitcast(F32), x2_dram[0][:, k, :, :]).then_inc(x2_in[k], 16)
            sp.wait_ge(dense_done, 2 * 4 * TILES)
            load_pr(0, 0, 0, after_first=False)
            load_pr(1, 1, 1, after_first=False)
            for g in range(2):
                with sp.Fori(1 - g, F_TILES // 2) as i:
                    for q in range(2):
                        load_fc(F_TILES * g + 2 * i + q, q, 2 * i + q)
                        load_pr(F_TILES * g + 2 * i + q, q, 2 * i + q)
            out_tiled = out.rearrange("(t p) d -> p t d", p=P)
            for n in range(n1 // P):
                sp.wait_ge(result_ready, n + 1)
                sp.dma_start(out_tiled[:, n0 // P + n, :], x1_1[:, n, :]).then_inc(out_stored[1], 16)
            for g, (_, count, _) in enumerate(GROUPS_OF_TILES):
                sp.wait_ge(out_stored[g], 16 * count)

        @block.gpsimd
        def _(pool):
            nc.gpsimd.iota(tile_first[:, :], pattern=[[P, TILES]], base=0, channel_multiplier=0,
                           allow_small_or_imprecise_dtypes=True).then_inc(constants, 1)
            nc.gpsimd.iota(tile_next[:, :], pattern=[[P, TILES]], base=P, channel_multiplier=0,
                           allow_small_or_imprecise_dtypes=True).then_inc(constants, 1)
            nc.gpsimd.iota(from_start[:, :], pattern=[[0, TILES]], base=1, channel_multiplier=1,
                           allow_small_or_imprecise_dtypes=True).then_inc(constants, 1)
            nc.gpsimd.iota(from_end[:, :], pattern=[[0, TILES]], base=GROUPS, channel_multiplier=-1,
                           allow_small_or_imprecise_dtypes=True).then_inc(constants, 1)
            nc.gpsimd.memset(ident[:, :], 0.0).then_inc(constants, 1)
            pool.wait_ge(constants, 5)
            nc.gpsimd.affine_select(out=ident[:, :], in_=ident[:, :], compare_op=ALU.not_equal, fill=1.0,
                                    base=0, pattern=[[-1, 128]], channel_multiplier=1).then_inc(constants, 1)
            nc.gpsimd.memset(eps_col[:, :], EPS).then_inc(constants, 1)
            nc.gpsimd.memset(zero_w[:, :], 0.0).then_inc(constants, 1)
            nc.gpsimd.iota(iota[:, :], pattern=[[1, NODES]], base=0, channel_multiplier=0,
                           allow_small_or_imprecise_dtypes=True).then_inc(constants, 1)

            pool.wait_ge(constants, 6)
            nc.gpsimd.tensor_copy(ident_narrow[:, :], ident[0:P, 0:P]).then_inc(constants, 1)

            for k in range(KD):
                pool.wait_ge(w_in[k], 16)
                nc.gpsimd.tensor_copy(w[:, k, HI, :], raw_w(k)).then_inc(w_high, 1)
                pool.wait_ge(w_high, k + 1)
                nc.gpsimd.tensor_tensor(w[:, k, LO, :], raw_w(k), w[:, k, HI, :].bitcast(F32),
                                        ALU.subtract).then_inc(w_low, 1)

            pool.sem_inc(counts_free, 2)
            pool.sem_inc(row_free[0], 2)
            pool.sem_inc(turned_free, 1)
            with pool.Fori(0, PAIRS) as i:
                for j in range(2):
                    pool.wait_ge(counts_copied, 2 * i + j + 3)
                    pool.dma_start(counts_dram[ds(2 * i + j, 1)].rearrange("a p m -> (a p) m"),
                                   counts[:, j, :]).then_inc(counts_stored, 16)
                    pool.wait_ge(counts_stored, 16 * (2 * i + j + 1))
                    pool.sem_inc(counts_free, 1)

            def store_row(l, n, tile):
                pool.wait_ge(row_high[l], 2 * n + 2)
                pool.wait_ge(row_low[l], 2 * n + 4)
                pool.dma_start(xt_dram[l][ds(n, 1)].rearrange("a p h k m -> (a p) h k m"),
                               tile[:, :, :, :].bitcast(F32)).then_inc(xt_stored[l], 16)

            def free_row(l, n):
                pool.wait_ge(xt_stored[l], 16 * (n + 1))
                pool.sem_inc(row_free[l], 1)

            def store_first_pass(n, j):
                if not isinstance(n, int) or n + 1 < TILES:
                    store_row(0, n + 1, xt[1 - j])
                pool.wait_ge(turned_high, 3 * n + 3)
                pool.wait_ge(turned_low, 3 * n + 5)
                pool.dma_start(at_dram[ds(n, 1)].rearrange("a p s h m -> (a p) s h m"),
                               turned[:, :, :, :].bitcast(F32)).then_inc(at_stored, 16)
                if not isinstance(n, int) or n + 1 < TILES:
                    free_row(0, n + 1)
                pool.wait_ge(at_stored, 16 * (n + 1))
                pool.sem_inc(turned_free, 1)

            store_row(0, 0, xt[0])
            free_row(0, 0)
            with pool.Fori(0, PAIRS - 1) as i:
                store_first_pass(2 * i, 0)
                store_first_pass(2 * i + 1, 1)
            store_first_pass(TILES - 2, 0)
            store_first_pass(TILES - 1, 1)
            pool.sem_inc(row_free[1], 1)
            with pool.Fori(0, TILES) as n:
                store_row(1, n, xt_out)
                free_row(1, n)
            pool.sem_inc(row_free[2], 1)
            pool.sem_inc(x1_free, 1)
            for g, (first, count, _) in enumerate(GROUPS_OF_TILES):
                with pool.Fori(first, first + count) as n:
                    pool.wait_ge(x1_ready, n + 1)
                    pool.dma_start(x1_dram.rearrange("(t p) d -> t p d", p=P)[ds(n, 1)].rearrange("a p d -> (a p) d"),
                                   rows[1][:, :]).then_inc(x1_stored, 16)
                    pool.wait_ge(x1_stored, 16 * (n + 1))
                    pool.sem_inc(x1_free, 1)
                    pool.wait_ge(row_high[2], 2 * n + 2)
                    pool.wait_ge(row_low[2], 2 * n + 4)
                    for h in (HI, LO):
                        pool.dma_start(x2_dram[g][:, :, h, ds((n - first) * P, P)],
                                       xt_out[:, h, :, :].bitcast(F32)).then_inc(x2_stored, 16)
                    pool.wait_ge(x2_stored, 32 * (n + 1))
                    pool.sem_inc(row_free[2], 1)

            pool.wait_ge(at_used, 2 * TILES + 1)
            nc.gpsimd.memset(y0[:, :, :], 0.0).then_inc(y_zero, 1)
            pool.dma_start(x2t1[:, :, :, :].bitcast(F32), x2_dram[1]).then_inc(x2_in_last, 16)
            pool.wait_ge(hid_summed, 2 * F_TILES + 2)
            nc.gpsimd.memset(y1[:, :, :], 0.0).then_inc(y_zero, 1)
            x1_tiled = x1_dram.rearrange("(t p) d -> p t d", p=P)
            out_tiled = out.rearrange("(t p) d -> p t d", p=P)
            pool.dma_start(x1_0[:, :, :], x1_tiled[:, 0:n0 // P, :]).then_inc(x1_in[0], 16)
            for n in range(n0 // P):
                pool.wait_ge(lif_steps, LIF_STEPS * (n + 1) + 1)
                pool.dma_start(out_tiled[:, n, :], x1_0[:, n, :]).then_inc(out_stored[0], 16)
            pool.wait_ge(hid_summed, 3 * F_TILES + 2)
            pool.dma_start(x1_1[:, :, :], x1_tiled[:, n0 // P:, :]).then_inc(x1_in[1], 16)

        @block.scalar
        def _(act):
            visit = act.alloc_register("act_visit")
            act.reg_mov(visit, 1)
            act.wait_ge(constants, 9)
            nc.scalar.activation(std[:, 0:1], eps_col[:, :], ACT.Sqrt).then_inc(table_loaded, 1)
            act.wait_ge(edge_steps, 2)
            act.wait_ge(range_ready, 1)
            act.sem_inc(counts_copied, 2)
            for h in range(GROUP // 2):
                act.sem_inc(dst_hot_ready[h], 1)

            def dst_one_hots(t):
                first = act.value_load(group_range[0:1, ds(t, 1)], min_val=0, max_val=GROUPS - 1)
                end = act.value_load(group_range[0:1, ds(t + TILES, 1)], min_val=1, max_val=GROUPS)
                with act.Fori(first, end) as g:
                    for h, (q, last) in enumerate(((0, 1), (2, 2))):
                        act.wait_ge(dst_hot_ready[h], visit)
                        for c in range(q, last + 1):
                            ins = nc.scalar.activation(dist[:, c, :], iota[:, ds(t * P, P)], ACT.Square,
                                                       bias=minus_dst_f[:, ds(g * GROUP + c, 1)])
                        ins.then_inc(dist_ready[h], 1)
                        act.wait_ge(dist_ready[h], visit)
                        act.wait_ge(hot_used[last], visit)
                        nc.scalar.activation(dst_hot[:, q:last + 1, :], dist[:, q:last + 1, :],
                                             ACT.Relu, bias=1.0, scale=-1.0).then_inc(dst_hot_ready[h], 1)
                    act.reg_add(visit, visit, 1)

            def copy_counts(t, j):
                act.wait_ge(counts_summed, t + 1)
                act.wait_ge(counts_free, t + 1)
                for b, (c0, n) in enumerate(COUNT_COLS):
                    ins = nc.scalar.activation(counts[:, j, c0:c0 + n], bank[0:P, 3 * j + b, 0:n], ACT.Copy,
                                               accum_out=deg[:, ds(t, 1), b])
                ins.then_inc(counts_copied, 1)

            def standard_deviation(l, n, j):
                act.wait_ge(ln_steps[l], LN_STEPS * n + 4)
                nc.scalar.activation(std[:, j:j + 1], mean_var[:, j, 1:2], ACT.Sqrt,
                                     bias=eps_col[:, :]).then_inc(ln_std[l], 1)

            dst_one_hots(0)
            dst_one_hots(1)
            copy_counts(0, 0)
            with act.Fori(1, PAIRS - 1) as i:
                dst_one_hots(2 * i)
                copy_counts(2 * i - 1, 1)
                dst_one_hots(2 * i + 1)
                copy_counts(2 * i, 0)
            dst_one_hots(TILES - 2)
            copy_counts(TILES - 3, 1)
            standard_deviation(0, 0, 0)
            standard_deviation(0, 1, 1)
            dst_one_hots(TILES - 1)
            copy_counts(TILES - 2, 0)
            copy_counts(TILES - 1, 1)

            def high_of_row(l, n, tile, func):
                act.wait_ge(row_free[l], n + 1)
                for q in range(2):
                    act.wait_ge(row_turned[l], 2 * n + q + 1)
                    nc.scalar.activation(tile[:, HI, 4 * q:4 * q + 4, :],
                                         bank[:, 6 + q, 0:4 * P].rearrange("p (k m) -> p k m", k=4),
                                         func).then_inc(row_high[l], 1)

            def high_of_turned(n, j, r):
                s0, c = ROUNDS[r]
                if r == 0:
                    act.wait_ge(turned_free, n + 1)
                act.wait_ge(counts_turned, 3 * n + r + 1)
                nc.scalar.activation(turned[:, s0:s0 + c, HI, :],
                                     bank[0:P, 4 + (3 * j + r) % 2, 0:c * P].rearrange("p (s m) -> p s m", s=c),
                                     ACT.Copy).then_inc(turned_high, 1)

            def high_of_z(l, n, j):
                for q in range(2):
                    act.wait_ge(dense_done, 2 * (2 * TILES * l + n) + q + 1)
                    nc.scalar.activation(z[:, ds(n, 1), HI, q * HALF:(q + 1) * HALF],
                                         bank[0:P, 2 * j + q, :].unsqueeze(1), ACT.Copy).then_inc(z_high, 1)

            def high_of_w(phase):
                for k in range(KD):
                    act.wait_ge(w_in[k], 16 * (phase + 1))
                    if k < 2:
                        act.wait_ge(w_used, (KD - 1) * (TILES * phase - 1) + k + 1)
                    nc.scalar.activation(w[:, k, HI, :], raw_w(k), ACT.Copy).then_inc(w_high, 1)

            def first_pass(n, j):
                if not isinstance(n, int) or n + 1 < TILES:
                    high_of_row(0, n + 1, xt[1 - j], ACT.Copy)
                high_of_turned(n, j, 0)
                high_of_turned(n, j, 1)
                high_of_turned(n, j, 2)
                if not isinstance(n, int) or n + 2 < TILES:
                    standard_deviation(0, n + 2, j)
                if isinstance(n, int) and n == TILES - 1:
                    high_of_w(1)
                high_of_z(0, n, j)

            high_of_row(0, 0, xt[0], ACT.Copy)
            with act.Fori(0, PAIRS - 1) as i:
                first_pass(2 * i, 0)
                first_pass(2 * i + 1, 1)
            first_pass(TILES - 2, 0)
            first_pass(TILES - 1, 1)

            with act.Fori(0, TILES - 1) as n:
                high_of_row(1, n, xt_out, ACT.Relu)
            high_of_w(2)
            high_of_z(1, 0, 0)
            high_of_row(1, TILES - 1, xt_out, ACT.Relu)
            high_of_z(1, 1, 1)
            with act.Fori(1, PAIRS - 1) as i:
                high_of_z(1, 2 * i, 0)
                high_of_z(1, 2 * i + 1, 1)
            high_of_z(1, TILES - 2, 0)
            high_of_w(3)
            high_of_z(1, TILES - 1, 1)
            standard_deviation(1, 0, 0)
            with act.Fori(0, PAIRS - 1) as i:
                for j in range(2):
                    high_of_row(2, 2 * i + j, xt_out, ACT.Copy)
                    standard_deviation(1, 2 * i + j + 1, 1 - j)
            high_of_row(2, TILES - 2, xt_out, ACT.Copy)
            act.wait_ge(fc_in[0], 16)
            act.wait_ge(dense_done, 2 * 4 * TILES)
            nc.scalar.activation(fc_w[:, 0, :, HI, :], fc_raw[:, 0, :, :], ACT.Copy).then_inc(fc_high, 1)
            standard_deviation(1, TILES - 1, 1)

            def in_slot(m, q):
                return 16 + 8 * (m - q)

            def high_of_fc(m, q, g):
                act.wait_ge(fc_in[q], in_slot(m, q))
                act.wait_ge(hid_summed, 2 * m if g == 0 else F_TILES + m + 1)
                nc.scalar.activation(fc_w[:, q, :, HI, :], fc_raw[:, q, :, :], ACT.Copy).then_inc(fc_high, 1)

            def high_of_pr(m, j, used):
                act.wait_ge(pr_in[j % 2], in_slot(m, j % 2))
                act.wait_ge(proj_summed, used)
                nc.scalar.activation(pr_of(j)[:, HI, :], pr_raw[:, j % 2, :], ACT.Copy).then_inc(pr_high, 1)

            def relu_and_high(bank_index, slot, hid, c0, n):
                act.wait_ge(hid_summed, bank_index + 3)
                act.wait_ge(hid_low, bank_index + 1)
                nc.scalar.activation(relu[:, slot, 0:n], bank[:, 4 + slot, 0:n], ACT.Relu).then_inc(hid_relu, 1)
                act.wait_ge(hid_relu, bank_index + 3)
                nc.scalar.activation(hid[:, HI, c0:c0 + n], relu[:, slot, 0:n], ACT.Square).then_inc(hid_high, 1)

            act.sem_inc(hid_relu, 2)
            def ffn_block(g, b, first=False, last=False):
                _, count, columns = GROUPS_OF_TILES[g]
                length = 2 * BLOCK if last else BLOCK
                for j in range(length):
                    m = F_TILES * g + BLOCK * b + j
                    if not (last and j == length - 1):
                        high_of_fc(m + 1, (j + 1) % 2, g)
                    if j == BLOCK:
                        act.wait_ge(lif_steps, LIF_STEPS * n0 // P + 1)
                        act.wait_ge(out_stored[0], 16 * (n0 // P))
                    if first and j == 0:
                        act.wait_ge(at_used, 2 * TILES + 1)
                    high_of_pr(m, j, 2 * count * b + 1 + g * ADDED[0])
                    for c, (c0, n) in enumerate(columns):
                        bank_index = 2 * m + c if g == 0 else F_TILES + m
                        relu_and_high(bank_index, c if g == 0 else j % 2, hid_of(g, j), c0, n)
                        if first and j == 1 and c == 0:
                            high_of_row(2, TILES - 1, xt_out, ACT.Copy)

            ffn_block(0, 0, first=True)
            with act.Fori(1, BLOCKS) as b:
                ffn_block(0, b)
            with act.Fori(0, BLOCKS - 2) as b:
                ffn_block(1, b)
            ffn_block(1, BLOCKS - 2, last=True)

            for n in range(n1 // P):
                for s in range(STEPS):
                    spike = STEPS * n + s
                    if s == 0:
                        act.wait_ge(y_added, Y_START + sum(ADDED) - 2 * (n1 // P - n - 1))
                        source = y1[:, n, :]
                    else:
                        act.wait_ge(mem_steps, MEM_STEPS * n + 2 * s + 1)
                        source = (lif_a, lif_b)[(s - 1) % 2][:, :]
                    if spike > 0:
                        act.wait_ge(spikes_ready, spike)
                    nc.scalar.activation(sign[:, :], source, ACT.Sign, bias=1.0, scale=-1.0).then_inc(signs, 1)
                    act.wait_ge(signs, spike + 1)
                    if spike >= SPIKE_SLOTS:
                        act.wait_ge(spikes_counted, spike - SPIKE_SLOTS + 1)
                    nc.scalar.activation(spikes[:, spike % SPIKE_SLOTS, :], sign[:, :], ACT.Relu,
                                         scale=-1.0).then_inc(spikes_ready, 1)

        @block.vector
        def _(dve):
            dve.wait_ge(edges_in, 48)
            nc.vector.tensor_copy(src_f[:, :], edge_int[:, 0, :]).then_inc(edge_steps, 1)
            nc.vector.tensor_scalar(minus_dst_f[:, :], edge_int[:, 1, :], -1.0, None, ALU.mult).then_inc(edge_steps, 1)
            nc.vector.tensor_copy(dst_rows_f[:, :], dst_int[:, :]).then_inc(edge_steps, 1)
            dve.wait_ge(edge_steps, 3)
            nc.vector.tensor_reduce(group_min[:, :], dst_rows_f[:, :], AX.X, ALU.min).then_inc(edge_steps, 1)
            nc.vector.tensor_reduce(group_max[:, :], dst_rows_f[:, :], AX.X, ALU.max).then_inc(edge_steps, 1)
            dve.wait_ge(edge_steps, 5)
            dve.wait_ge(constants, 9)
            nc.vector.tensor_scalar(below[:, :], tile_next[:, :], group_min[:, 0:1], None, ALU.is_gt).then_inc(edge_steps, 1)
            nc.vector.tensor_scalar(above[:, :], tile_first[:, :], group_max[:, 0:1], None, ALU.is_le).then_inc(edge_steps, 1)
            dve.wait_ge(edge_steps, 7)
            nc.vector.tensor_tensor(may_hold[:, :], below[:, :], above[:, :], ALU.mult).then_inc(edge_steps, 1)
            dve.wait_ge(edge_steps, 8)
            nc.vector.tensor_tensor(bounds[:, 0:TILES], may_hold[:, :], from_end[:, :], ALU.mult).then_inc(edge_steps, 1)
            nc.vector.tensor_tensor(bounds[:, TILES:], may_hold[:, :], from_start[:, :], ALU.mult).then_inc(edge_steps, 1)
            dve.wait_ge(bounds_turned, 1)
            nc.vector.tensor_reduce(bound_col[:, :], bank[0:2 * TILES, 6, 0:GROUPS], AX.X, ALU.max).then_inc(edge_steps, 1)
            dve.wait_ge(bounds_turned, 2)
            nc.vector.tensor_scalar(range_f[:, 0:TILES], bank[0:1, 7, 0:TILES], -1.0, float(GROUPS),
                                    ALU.mult, ALU.add).then_inc(edge_steps, 1)
            dve.wait_ge(edge_steps, 12)
            nc.vector.tensor_scalar(range_f[:, 0:TILES], range_f[:, 0:TILES], float(GROUPS - 1), None,
                                    ALU.min).then_inc(edge_steps, 1)
            dve.wait_ge(edge_steps, 13)
            nc.vector.scalar_tensor_tensor(out=range_f[:, TILES:], in0=range_f[:, 0:TILES], scalar=1.0,
                                           in1=bank[0:1, 7, TILES:2 * TILES], op0=ALU.add, op1=ALU.max).then_inc(edge_steps, 1)
            dve.wait_ge(edge_steps, 14)
            nc.vector.tensor_copy(group_range[:, :], range_f[:, :]).then_inc(range_ready, 1)
            nc.vector.tensor_copy(dst_f[:, :], edge_int[:, 1, :]).then_inc(edge_steps, 1)
            dve.wait_ge(range_ready, 1)
            dve.wait_ge(edge_steps, 15)

            visit = dve.alloc_register("dve_visit")
            dve.reg_mov(visit, 1)

            def src_one_hots(t):
                first = dve.value_load(group_range[0:1, ds(t, 1)], min_val=0, max_val=GROUPS - 1)
                end = dve.value_load(group_range[0:1, ds(t + TILES, 1)], min_val=1, max_val=GROUPS)
                with dve.Fori(first, end) as g:
                    for q in range(GROUP):
                        dve.wait_ge(hot_used[q], visit)
                        if q == GROUP - 1:
                            nc.vector.tensor_scalar(dst_hot[:, q, :], iota[:, ds(t * P, P)],
                                                    dst_f[:, ds(g * GROUP + q, 1)], None, ALU.is_equal)
                        nc.vector.tensor_scalar(src_hot[:, q, :], iota[:, :], src_f[:, ds(g * GROUP + q, 1)],
                                                None, ALU.is_equal).then_inc(src_hot_ready[q], 1)
                    dve.reg_add(visit, visit, 1)

            def layer_norm(l, n, j, source, target):
                for q in range(2):
                    nc.vector.bn_stats(stats[:, j, q, :], source[:, q * HALF:(q + 1) * HALF]).then_inc(ln_steps[l], 1)
                dve.wait_ge(ln_steps[l], LN_STEPS * n + 2)
                nc.vector.memset(newton[:, j:j + 1], 0.0).then_inc(ln_steps[l], 1)
                nc.vector.bn_aggr(mean_var[:, j, :], stats[:, j, :, :]).then_inc(ln_steps[l], 1)
                dve.wait_ge(ln_std[l], n + 1)
                nc.vector.reciprocal(rstd[:, j:j + 1], std[:, j:j + 1]).then_inc(ln_steps[l], 1)
                nc.vector.tensor_scalar(newton[:, j:j + 1], mean_var[:, j, 1:2], EPS, None, ALU.add).then_inc(ln_steps[l], 1)
                dve.wait_ge(ln_steps[l], LN_STEPS * n + 6)
                nc.vector.scalar_tensor_tensor(out=newton[:, j:j + 1], in0=rstd[:, j:j + 1], scalar=rstd[:, j:j + 1],
                                               in1=newton[:, j:j + 1], op0=ALU.mult, op1=ALU.mult).then_inc(ln_steps[l], 1)
                dve.wait_ge(ln_steps[l], LN_STEPS * n + 7)
                nc.vector.tensor_scalar(newton[:, j:j + 1], newton[:, j:j + 1], -0.5, 1.5, ALU.mult, ALU.add).then_inc(ln_steps[l], 1)
                dve.wait_ge(ln_steps[l], LN_STEPS * n + 8)
                nc.vector.tensor_tensor(rstd[:, j:j + 1], rstd[:, j:j + 1], newton[:, j:j + 1], ALU.mult).then_inc(ln_steps[l], 1)
                dve.wait_ge(ln_steps[l], LN_STEPS * n + 9)
                nc.vector.tensor_scalar(target[:, :], source[:, :], mean_var[:, j, 0:1], rstd[:, j:j + 1],
                                        ALU.subtract, ALU.mult).then_inc(row_ready[2 * l], 1)

            def norm_x(n, j):
                if isinstance(n, int):
                    dve.wait_ge(x_in[j], 16 * (n // 2 + 1))
                else:
                    dve.wait_ge(x_in[j], 8 * (n - j) + 16)
                layer_norm(0, n, j, rows[j], rows[2 + j])

            def low_of_row(l, n, tile, relu=False):
                for q in range(2):
                    dve.wait_ge(row_high[l], 2 * n + q + 1)
                    source = bank[:, 6 + q, 0:4 * P].rearrange("p (k m) -> p k m", k=4)
                    high = tile[:, HI, 4 * q:4 * q + 4, :].bitcast(F32)
                    low = tile[:, LO, 4 * q:4 * q + 4, :]
                    if relu:
                        ins = nc.vector.scalar_tensor_tensor(out=low, in0=source, scalar=0.0, in1=high,
                                                             op0=ALU.max, op1=ALU.subtract)
                    else:
                        ins = nc.vector.tensor_tensor(low, source, high, ALU.subtract)
                    ins.then_inc(row_low[l], 1)

            def low_of_turned(n, j, r):
                s0, c = ROUNDS[r]
                dve.wait_ge(turned_high, 3 * n + r + 1)
                nc.vector.tensor_tensor(turned[:, s0:s0 + c, LO, :],
                                        bank[0:P, 4 + (3 * j + r) % 2, 0:c * P].rearrange("p (s m) -> p s m", s=c),
                                        turned[:, s0:s0 + c, HI, :].bitcast(F32), ALU.subtract).then_inc(turned_low, 1)

            def low_of_z(l, n, j):
                for q in range(2):
                    dve.wait_ge(z_high, 2 * TILES * l + 2 * n + q + 1)
                    nc.vector.tensor_tensor(z[:, ds(n, 1), LO, q * HALF:(q + 1) * HALF],
                                            bank[0:P, 2 * j + q, :].unsqueeze(1),
                                            z[:, ds(n, 1), HI, q * HALF:(q + 1) * HALF].bitcast(F32),
                                            ALU.subtract).then_inc(z_low, 1)

            def low_of_w(phase):
                for k in range(KD):
                    dve.wait_ge(w_high, KD * phase + k + 1)
                    nc.vector.tensor_tensor(w[:, k, LO, :], raw_w(k), w[:, k, HI, :].bitcast(F32),
                                            ALU.subtract).then_inc(w_low, 1)

            dve.sem_inc(turned_low, 2)
            dve.sem_inc(z_low, 4)
            dve.sem_inc(self_taken, 1)
            dve.sem_inc(res_used, 1)
            for l in range(3):
                dve.sem_inc(row_low[l], 2)
            with dve.Fori(0, TILES - 1) as t:
                src_one_hots(t)
            norm_x(0, 0)
            norm_x(1, 1)
            src_one_hots(TILES - 1)

            def first_pass(n, j):
                if not isinstance(n, int) or n + 1 < TILES:
                    low_of_row(0, n + 1, xt[1 - j])
                low_of_turned(n, j, 0)
                low_of_turned(n, j, 1)
                low_of_turned(n, j, 2)
                if not isinstance(n, int) or n + 2 < TILES:
                    norm_x(n + 2, j)
                if isinstance(n, int) and n == TILES - 1:
                    low_of_w(1)
                low_of_z(0, n, j)

            dve.wait_ge(counts_copied, TILES + 2)
            nc.vector.tensor_reduce(deg_sum[:, :], deg[:, :, :], AX.X, ALU.add).then_inc(deg_steps, 1)
            dve.wait_ge(deg_steps, 1)
            nc.vector.tensor_reduce(deg_max[:, :], deg_sum[:, :], AX.X, ALU.max).then_inc(deg_steps, 1)
            low_of_row(0, 0, xt[0])
            nc.vector.tensor_scalar(dinv[:, :], deg_sum[:, :], 1.0, None, ALU.max).then_inc(deg_steps, 1)
            dve.wait_ge(deg_steps, 3)
            nc.vector.reciprocal(dinv[:, :], dinv[:, :]).then_inc(deg_steps, 1)
            dve.wait_ge(deg_turned, 1)
            nc.vector.tensor_reduce(many[:, :], bank[0:1, 3, 0:P], AX.X, ALU.max).then_inc(deg_steps, 1)
            dve.wait_ge(deg_steps, 5)
            nc.vector.tensor_scalar(many_int[:, :], many[:, :], EXACT_COUNT, None, ALU.is_gt).then_inc(many_ready, 1)

            with dve.Fori(0, PAIRS - 1) as i:
                first_pass(2 * i, 0)
                first_pass(2 * i + 1, 1)
            first_pass(TILES - 2, 0)
            first_pass(TILES - 1, 1)

            def low_of_fc(m, q):
                dve.wait_ge(fc_high, m + 1)
                nc.vector.tensor_tensor(fc_w[:, q, :, LO, :], fc_raw[:, q, :, :],
                                        fc_w[:, q, :, HI, :].bitcast(F32), ALU.subtract).then_inc(fc_low, 1)


            def take_self(l, n):
                dve.wait_ge(dense_done, 2 * (TILES * (2 * l + 1) + n + 1))
                if l == 1:
                    dve.wait_ge(x1_free, n + 1)
                if not isinstance(n, int) or n > 0:
                    dve.wait_ge(row_ready[l + 1], n)
                nc.vector.tensor_tensor(rows[1][:, :].rearrange("p (q c) -> p q c", q=2), bank[0:P, 0:2, :],
                                        bias[:, :].rearrange("p (q c) -> p q c", q=2), ALU.add).then_inc(self_taken, 1)
                if l == 1:
                    dve.wait_ge(self_taken, TILES + n + 2)
                    dve.wait_ge(res_in, 16 * (n + 1))
                    nc.vector.tensor_tensor(rows[1][:, :], rows[1][:, :], rows[0][:, :], ALU.add).then_inc(res_used, 1)

            def take_aggregate(l, n, j):
                dve.wait_ge(at_used, TILES * l + n + 2)
                dve.wait_ge((self_taken, res_used)[l], n + 2)
                target = rows[2 + j] if l == 0 else rows[1]
                ins = nc.vector.scalar_tensor_tensor(out=target[:, :].rearrange("p (q c) -> p q c", q=2),
                                                     in0=bank[0:P, 2:4, :], scalar=dinv[:, ds(n, 1)],
                                                     in1=rows[1][:, :].rearrange("p (q c) -> p q c", q=2),
                                                     op0=ALU.mult, op1=ALU.add)
                if l == 0:
                    ins.then_inc(row_ready[1], 1)
                else:
                    ins.then_inc(x1_ready, 1)
                    dve.wait_ge(x1_ready, n + 1)
                    layer_norm(1, n, j, rows[1], rows[2 + j])

            def tile_of_pass(l, n, j):
                take_self(l, n)
                low_of_row(l + 1, n - 1, xt_out, relu=(l == 0))
                if isinstance(n, int):
                    if l == 0:
                        low_of_w(2)
                    else:
                        low_of_fc(0, 0)
                take_aggregate(l, n, j)

            for l in range(2):
                if l == 1:
                    low_of_z(1, 0, 0)
                    low_of_row(1, TILES - 1, xt_out, relu=True)
                    low_of_z(1, 1, 1)
                    with dve.Fori(1, PAIRS - 1) as i:
                        low_of_z(1, 2 * i, 0)
                        low_of_z(1, 2 * i + 1, 1)
                    low_of_z(1, TILES - 2, 0)
                    low_of_w(3)
                    low_of_z(1, TILES - 1, 1)
                dve.wait_ge(bias_in, 16 * (l + 1))
                take_self(l, 0)
                take_aggregate(l, 0, 0)
                with dve.Fori(0, PAIRS - 1) as i:
                    tile_of_pass(l, 2 * i + 1, 1)
                    tile_of_pass(l, 2 * i + 2, 0)
                tile_of_pass(l, TILES - 1, 1)

            def low_of_pr(m, j):
                dve.wait_ge(pr_high, m + 1)
                nc.vector.tensor_tensor(pr_of(j)[:, LO, :], pr_raw[:, j % 2, :],
                                        pr_of(j)[:, HI, :].bitcast(F32), ALU.subtract).then_inc(pr_low, 1)

            def square_and_low(bank_index, slot, hid, c0, n):
                dve.wait_ge(hid_relu, bank_index + 3)
                dve.wait_ge(hid_low, bank_index + 1)
                nc.vector.tensor_tensor(square[:, slot, 0:n], relu[:, slot, 0:n], relu[:, slot, 0:n],
                                        ALU.mult).then_inc(hid_square, 1)
                dve.wait_ge(hid_square, bank_index + 1)
                dve.wait_ge(hid_high, bank_index + 1)
                nc.vector.tensor_tensor(hid[:, LO, c0:c0 + n], square[:, slot, 0:n],
                                        hid[:, HI, c0:c0 + n].bitcast(F32), ALU.subtract).then_inc(hid_low, 1)

            def lif_step(step, n):
                mem, drive, count = lif_a[:, :].unsqueeze(1), lif_b[:, :].unsqueeze(1), lif_c[:, :].unsqueeze(1)
                inp, x1_part = y0[:, ds(n, 1), :], x1_0[:, ds(n, 1), :]
                kind, s = (step - 1) % 3, (step - 1) // 3
                source = inp if s == 0 else mem
                dve.wait_ge(lif_steps, LIF_STEPS * n + step + 1)
                if step == 0:
                    ins = nc.vector.tensor_scalar(count, inp, THRESHOLD, None, ALU.is_gt)
                elif step == LIF_STEPS - 1:
                    ins = nc.vector.scalar_tensor_tensor(out=x1_part, in0=count, scalar=1.0 / STEPS, in1=x1_part,
                                                         op0=ALU.mult, op1=ALU.add)
                elif kind == 0:
                    ins = nc.vector.scalar_tensor_tensor(out=drive, in0=source, scalar=BETA, in1=inp,
                                                         op0=ALU.mult, op1=ALU.add)
                elif kind == 1:
                    ins = nc.vector.scalar_tensor_tensor(out=mem, in0=source, scalar=THRESHOLD, in1=drive,
                                                         op0=ALU.is_gt, op1=ALU.subtract, reverse1=True)
                else:
                    ins = nc.vector.scalar_tensor_tensor(out=count, in0=mem, scalar=THRESHOLD, in1=count,
                                                         op0=ALU.is_gt, op1=ALU.add)
                ins.then_inc(lif_steps, 1)

            dve.sem_inc(hid_low, 2)
            dve.sem_inc(lif_steps, 1)
            dve.sem_inc(mem_steps, 1)
            dve.sem_inc(y_added, Y_START)

            def hidden_part(g, b, first=False, last=False, spiking=False):
                _, count, columns = GROUPS_OF_TILES[g]
                length = 2 * BLOCK if last else BLOCK
                for j in range(length):
                    m = F_TILES * g + BLOCK * b + j
                    if not (last and j == length - 1):
                        low_of_fc(m + 1, (j + 1) % 2)
                    low_of_pr(m, j)
                    for c, (c0, n) in enumerate(columns):
                        bank_index = 2 * m + c if g == 0 else F_TILES + m
                        square_and_low(bank_index, c if g == 0 else j % 2, hid_of(g, j), c0, n)
                        if first and j == 1 and c == 0:
                            low_of_row(2, TILES - 1, xt_out)
                    if spiking and j > 0:
                        lif_step(j - 1, b)

            def add_share(g, b, n):
                _, count, _ = GROUPS_OF_TILES[g]
                first_sum = g * ADDED[0]
                for q in range(2):
                    index = first_sum + 2 * count * b + 2 * n + q
                    dve.wait_ge(proj_summed, index + 2)
                    dve.wait_ge(y_added, index + 1 + Y_START - 2 * count)
                    part = y[g][:, n, q * HALF:(q + 1) * HALF]
                    nc.vector.tensor_tensor(part, part, bank[0:P, 2 * (n % 2) + q, :], ALU.add).then_inc(y_added, 1)

            def ffn_block(g, b, first=False, spiking=False):
                hidden_part(g, b, first=first, spiking=spiking)
                dve.wait_ge(y_zero, g + 1)
                if spiking:
                    dve.wait_ge(x1_in[0], 16)
                for n in range(GROUPS_OF_TILES[g][1]):
                    add_share(g, b, n)
                    if spiking:
                        for step in range(BLOCK - 1 + 3 * n, min(BLOCK - 1 + 3 * n + 3, LIF_STEPS)):
                            lif_step(step, b)

            ffn_block(0, 0, first=True)
            with dve.Fori(1, BLOCKS) as b:
                ffn_block(0, b)
            dve.wait_ge(y_added, Y_START + ADDED[0])
            assert LIF_STEPS <= BLOCK - 1 + 3 * (n1 // P) and n0 // P == BLOCKS - 2
            with dve.Fori(0, n0 // P) as b:
                ffn_block(1, b, spiking=True)
            hidden_part(1, BLOCKS - 2, last=True)

            def mem_step(n, step):
                t = step // 2
                mems = (lif_a, lif_b)
                inp = y1[:, n, :]
                source = inp if t == 0 else mems[(t - 1) % 2][:, :]
                if step == 0:
                    dve.wait_ge(y_added, Y_START + sum(ADDED) - 2 * (n1 // P - n - 1))
                dve.wait_ge(mem_steps, MEM_STEPS * n + step + 1)
                if step % 2 == 0:
                    ins = nc.vector.scalar_tensor_tensor(out=lif_c[:, :], in0=source, scalar=BETA, in1=inp,
                                                         op0=ALU.mult, op1=ALU.add)
                else:
                    read = STEPS * n + t + (t >= 2) - (t == 0)
                    if read > 0:
                        dve.wait_ge(signs, read)
                    ins = nc.vector.scalar_tensor_tensor(out=mems[t % 2][:, :], in0=source, scalar=THRESHOLD,
                                                         in1=lif_c[:, :], op0=ALU.is_gt, op1=ALU.subtract, reverse1=True)
                ins.then_inc(mem_steps, 1)

            def result(n):
                dve.wait_ge(x1_in[1], 16)
                dve.wait_ge(spikes_counted, STEPS * (n + 1))
                tile = x1_1[:, n, :].rearrange("p (q c) -> p q c", q=2)
                nc.vector.scalar_tensor_tensor(out=tile, in0=bank[0:P, 4 + 2 * (n % 2):6 + 2 * (n % 2), :],
                                               scalar=1.0 / STEPS, in1=tile,
                                               op0=ALU.mult, op1=ALU.add).then_inc(result_ready, 1)

            count = n1 // P
            for n in range(count):
                add_share(1, BLOCKS - 2, n)
                for step in range(MEM_STEPS):
                    if n > 0 and step == 4:
                        result(n - 1)
                    mem_step(n, step)
            result(count - 1)

        @block.tensor
        def _(pe):
            pe.wait_ge(constants, 9)
            pe.wait_ge(edge_steps, 10)
            nc.tensor.transpose(bank[0:2 * TILES, 6, 0:GROUPS], bounds[:, :], ident[0:GROUPS, 0:GROUPS]).then_inc(bounds_turned, 1)
            pe.wait_ge(edge_steps, 11)
            nc.tensor.matmul(bank[0:1, 7, 0:2 * TILES], bound_col[:, :], ident[0:2 * TILES, 0:2 * TILES],
                             start=True, stop=True).then_inc(bounds_turned, 1)
            pe.wait_ge(range_ready, 1)
            for q in range(GROUP):
                pe.sem_inc(hot_used[q], 1)
            visit = pe.alloc_register("pe_visit")
            pe.reg_mov(visit, 1)
            next_visit = pe.alloc_register("pe_next_visit")
            pe.reg_mov(next_visit, 2)

            def sum_counts(t, j):
                pe.wait_ge(counts_copied, t + 1)
                for b, (c0, n) in enumerate(COUNT_COLS):
                    nc.tensor.matmul(bank[0:P, 3 * j + b, 0:n], zero_w[:, :], iota[:, c0:c0 + n],
                                     start=True, stop=False)
                first = pe.value_load(group_range[0:1, ds(t, 1)], min_val=0, max_val=GROUPS - 1)
                end = pe.value_load(group_range[0:1, ds(t + TILES, 1)], min_val=1, max_val=GROUPS)
                with pe.Fori(first, end) as g:
                    for q in range(GROUP):
                        pe.wait_ge(src_hot_ready[q], visit)
                        if q in (0, 2):
                            pe.wait_ge(dst_hot_ready[q // 2], next_visit)
                        for b, (c0, n) in enumerate(COUNT_COLS):
                            ins = nc.tensor.matmul(bank[0:P, 3 * j + b, 0:n], dst_hot[:, q, :],
                                                   src_hot[:, q, c0:c0 + n], start=False, stop=False)
                        ins.then_inc(hot_used[q], 1)
                    pe.reg_add(visit, visit, 1)
                    pe.reg_add(next_visit, next_visit, 1)
                for b, (c0, n) in enumerate(COUNT_COLS):
                    ins = nc.tensor.matmul(bank[0:P, 3 * j + b, 0:2], zero_w[:, :], iota[:, 0:2],
                                           start=False, stop=True)
                ins.then_inc(counts_summed, 1)

            with pe.Fori(0, PAIRS) as i:
                sum_counts(2 * i, 0)
                sum_counts(2 * i + 1, 1)

            pe.sem_inc(at_used, 1)

            def turn_row(l, n, j):
                pe.wait_ge(row_ready[l], n + 1)
                for q in range(2):
                    pe.wait_ge(row_low[l], 2 * n + q + 1)
                    for k in range(4):
                        c = (4 * q + k) * 128
                        ins = nc.tensor.transpose(bank[:, 6 + q, k * P:(k + 1) * P], rows[2 + j][:, c:c + 128],
                                                  ident[0:P, 0:P])
                    ins.then_inc(row_turned[l], 1)

            def turn_counts(n, j, r):
                s0, c = ROUNDS[r]
                if r == 0:
                    if isinstance(n, int):
                        pe.wait_ge(counts_in[j], 16 * (n // 2 + 1))
                    else:
                        pe.wait_ge(counts_in[j], 8 * (n - j) + 16)
                pe.wait_ge(turned_low, 3 * n + r + 1)
                for s in range(c):
                    ins = nc.tensor.transpose(bank[0:P, 4 + (3 * j + r) % 2, s * P:(s + 1) * P],
                                              counts_back[:, j, (s0 + s) * P:(s0 + s + 1) * P], ident[0:P, 0:P])
                ins.then_inc(counts_turned, 1)

            def dense(phase, n, j, first_bank, between=None):
                if phase > 0:
                    if isinstance(n, int):
                        pe.wait_ge(xt_in[j], 16 * (PAIRS * (phase - 1) + n // 2 + 1))
                    else:
                        pe.wait_ge(xt_in[j], 16 * (PAIRS * (phase - 1) + 1) + 8 * (n - j))
                for k in range(KD):
                    if k == KD // 2 and between is not None:
                        between()
                    if isinstance(n, int) and n == 0:
                        pe.wait_ge(w_low, KD * phase + k + 1)
                    for m, (a, b) in enumerate(PASSES):
                        for q in range(2):
                            ins = nc.tensor.matmul(bank[0:P, first_bank + q, :], xt[j][:, a, k, :],
                                                   w[:, k, b, q * HALF:(q + 1) * HALF],
                                                   start=(k == 0 and m == 0), stop=(k == KD - 1 and m == 2))
                            if k == KD - 1 and m == 2:
                                ins.then_inc(dense_done, 1)
                    if k < KD - 1:
                        ins.then_inc(w_used, 1)

            def z_of_tile(l, n, j, between=None):
                pe.wait_ge(z_low, 2 * TILES * l + 2 * n + 2)
                dense(2 * l, n, j, 2 * j, between)

            def first_pass(n, j):
                if not isinstance(n, int) or n + 1 < TILES:
                    turn_row(0, n + 1, 1 - j)
                turn_counts(n, j, 0)
                turn_counts(n, j, 1)
                pe.wait_ge(row_low[0], 2 * n + 4)
                z_of_tile(0, n, j, between=lambda: turn_counts(n, j, 2))

            turn_row(0, 0, 0)
            pe.wait_ge(deg_steps, 2)
            nc.tensor.transpose(bank[0:1, 3, 0:P], deg_max[:, :], ident[0:P, 0:P]).then_inc(deg_turned, 1)
            first_pass(0, 0)
            pe.wait_ge(many_ready, 1)
            big_counts = pe.value_load(many_int[0:1, 0:1], min_val=0, max_val=1)
            first_pass(1, 1)
            with pe.Fori(1, PAIRS - 1) as i:
                first_pass(2 * i, 0)
                first_pass(2 * i + 1, 1)
            first_pass(TILES - 2, 0)
            first_pass(TILES - 1, 1)

            def self_of_tile(l, n, j):
                pe.wait_ge(self_taken, TILES * l + n + 1)
                dense(2 * l + 1, n, j, 0)

            def aggregate(l, n):
                pe.wait_ge(at_in, 16 * (TILES * l + n + 1))
                if isinstance(n, int) and n == 0:
                    pe.wait_ge(z_low, 2 * TILES * (l + 1) + 4)
                else:
                    pe.wait_ge((row_ready[1], x1_ready)[l], n)

                def products(part, s):
                    for b in (HI, LO):
                        for q in range(2):
                            first = part == HI and s == 0 and b == HI
                            last = part == HI and s == TILES - 1 and b == LO
                            ins = nc.tensor.matmul(bank[0:P, 2 + q, :], at_tile[:, s, part, :],
                                                   z[:, s, b, q * HALF:(q + 1) * HALF], start=first, stop=last)
                    return ins

                for s in range(TILES - 1):
                    products(HI, s)
                with pe.If(big_counts):
                    for s in range(TILES):
                        products(LO, s)
                products(HI, TILES - 1).then_inc(at_used, 1)

            for l in range(2):
                if l == 1:
                    pe.wait_ge(self_taken, TILES + 1)
                    z_of_tile(1, 0, 0)
                    turn_row(1, TILES - 1, 1)
                    pe.wait_ge(row_ready[1], TILES)
                    z_of_tile(1, 1, 1)
                    with pe.Fori(1, PAIRS) as i:
                        z_of_tile(1, 2 * i, 0)
                        z_of_tile(1, 2 * i + 1, 1)
                pe.wait_ge(z_low, 2 * TILES * (l + 1) + 2)
                self_of_tile(l, 0, 0)
                aggregate(l, 0)

                def tile_of_pass(n, j):
                    self_of_tile(l, n, j)
                    turn_row(l + 1, n - 1, 1 - j)
                    aggregate(l, n)

                with pe.Fori(0, PAIRS - 1) as i:
                    tile_of_pass(2 * i + 1, 1)
                    tile_of_pass(2 * i + 2, 0)
                tile_of_pass(TILES - 1, 1)

            pe.sem_inc(hid_summed, 2)
            pe.sem_inc(proj_summed, 1)

            def ffn_block(g, b, first=False, last=False):
                _, count, columns = GROUPS_OF_TILES[g]
                first_sum = g * ADDED[0]
                banks = len(columns)
                length = 2 * BLOCK if last else BLOCK
                for j in range(length):
                    m = F_TILES * g + BLOCK * b + j
                    pe.wait_ge(fc_low, m + 1)
                    for c, (c0, n) in enumerate(columns):
                        bank_index = 2 * m + c if g == 0 else F_TILES + m
                        slot = c if g == 0 else j % 2
                        pe.wait_ge(hid_relu, bank_index + 1)
                        for k in range(KD):
                            if first and j == 0 and c == 0:
                                pe.wait_ge(x2_in[k], 16)
                            for i, (a, v) in enumerate(PASSES):
                                ins = nc.tensor.matmul(bank[:, 4 + slot, 0:n], fc_w[:, j % 2, k, a, :],
                                                       x2t[g][:, k, v, c0:c0 + n],
                                                       start=(k == 0 and i == 0), stop=(k == KD - 1 and i == 2))
                        ins.then_inc(hid_summed, 1)
                    if first and j == 1:
                        turn_row(2, TILES - 1, 1)
                first_hid = (2 * F_TILES) * g + BLOCK * banks * b
                pe.wait_ge(pr_low, F_TILES * g + BLOCK * b + length)
                for n in range(count):
                    for q in range(2):
                        pe.wait_ge(y_added, first_sum + 2 * count * b + 2 * n + q + Y_START - 3)
                        for j in range(length):
                            if n == 0 and q == 0 and j in (0, length - 1):
                                pe.wait_ge(hid_low, first_hid + banks * (j if j else length - 1) + 2 + (1 if j else 0))
                            if banks == 2 and n == 3 and q == 0 and j == 0:
                                pe.wait_ge(hid_low, first_hid + banks * BLOCK + 2)
                            for i, (a, v) in enumerate(PASSES):
                                ins = nc.tensor.matmul(bank[0:P, 2 * (n % 2) + q, :], hid_of(g, j)[:, a, n * P:(n + 1) * P],
                                                       pr_of(j)[:, v, q * HALF:(q + 1) * HALF],
                                                       start=(j == 0 and i == 0), stop=(j == length - 1 and i == 2))
                        ins.then_inc(proj_summed, 1)
                        if last and q == 0 and n >= 2:
                            for spike in range(STEPS * (n - 2), STEPS * (n - 1)):
                                add_spikes(spike)

            def add_spikes(spike):
                n, s = spike // STEPS, spike % STEPS
                pe.wait_ge(spikes_ready, spike + 1)
                if spike == 0:
                    pe.wait_ge(constants, 10)
                if s == 0 and n >= 2:
                    pe.wait_ge(result_ready, n - 1)
                for q in range(2):
                    ins = nc.tensor.matmul(bank[0:P, 4 + 2 * (n % 2) + q, :], ident_narrow[:, :],
                                           spikes[:, spike % SPIKE_SLOTS, q * HALF:(q + 1) * HALF],
                                           start=(s == 0), stop=(s == STEPS - 1))
                ins.then_inc(spikes_counted, 1)

            ffn_block(0, 0, first=True)
            with pe.Fori(1, BLOCKS) as b:
                ffn_block(0, b)
            pe.wait_ge(x2_in_last, 16)
            with pe.Fori(0, BLOCKS - 2) as b:
                ffn_block(1, b)
            ffn_block(1, BLOCKS - 2, last=True)
            for spike in range(STEPS * (n1 // P - 2), STEPS * (n1 // P)):
                add_spikes(spike)


def kernel(x, src, dst, L0_gnn_W_self0, L0_gnn_W_neigh0, L0_gnn_b0, L0_gnn_W_self1, L0_gnn_W_neigh1, L0_gnn_b1,
           L0_ffn_W_fc, L0_ffn_W_proj):
    import numpy as np
    import concourse.bacc as bacc
    from concourse.bass_utils import run_bass_kernel_spmd

    def columns(edges):
        return np.asarray(edges).reshape(CHUNKS, P).T

    arrays = {
        "x": x,
        "dst_cols": columns(dst),
        "src_cols": columns(src),
        "dst_rows": np.asarray(dst).reshape(GROUPS, GROUP * P),
        "w_self0": L0_gnn_W_self0, "w_neigh0": L0_gnn_W_neigh0, "b0": L0_gnn_b0,
        "w_self1": L0_gnn_W_self1, "w_neigh1": L0_gnn_W_neigh1, "b1": L0_gnn_b1,
        "w_fc": np.asarray(L0_ffn_W_fc).reshape(F_TILES, F_TILE, KD, 128).transpose(0, 3, 2, 1),
        "w_proj": np.asarray(L0_ffn_W_proj).T.reshape(F_TILES, F_TILE, D),
    }
    arrays = {name: np.ascontiguousarray(a) for name, a in arrays.items()}
    nc = bacc.Bacc("TRN2", target_bir_lowering=False, num_devices=1)
    args = {name: nc.dram_tensor(name, a.shape, mybir.dt.from_np(a.dtype), kind="ExternalInput").ap()
            for name, a in arrays.items()}
    args["out"] = nc.dram_tensor("out", (NODES, D), F32, kind="ExternalOutput").ap()
    gnn_ffn(nc, **args)
    result = run_bass_kernel_spmd(nc, [arrays], core_ids=[0])
    return result.results[0]["out"]
```

```python
from contextlib import ExitStack

import concourse.bass as bass
from concourse import mybir

F32 = mybir.dt.float32
F32R = mybir.dt.float32r
BF16 = mybir.dt.bfloat16
F16 = mybir.dt.float16
I32 = mybir.dt.int32
ALU = mybir.AluOpType
ACT = mybir.ActivationFunctionType
AX = mybir.AxisListType
ds = bass.ds

NODES, D, F, EDGES = 1250, 1024, 4096, 40000
P = 125
TILES = NODES // P
KD = D // 128
CHUNKS = EDGES // P
GROUP = 4
GROUPS = CHUNKS // GROUP
HALF = 512
COUNT_COLS = ((0, 418), (418, 416), (834, 416))
HI, LO = 0, 1
EPS = 1e-5
LN_STEPS = 9
EXACT_COUNT = 4095.0
STEPS, BETA, THRESHOLD = 5, 0.9, 1.0
F_TILE = 128
F_TILES = F // F_TILE
BLOCK = 4
BLOCKS = F_TILES // BLOCK
GROUPS_OF_TILES = ((0, 6, ((0, 376), (376, 374))), (6, 4, ((0, 500),)))
Y_START = 16
ADDED = (2 * GROUPS_OF_TILES[0][1] * BLOCKS, 2 * GROUPS_OF_TILES[1][1] * (BLOCKS - 1))
LIF_STEPS = 3 * (STEPS - 1) + 2
SPIKE_SLOTS = 13
MEM_STEPS = 2 * (STEPS - 1)
PASSES = ((HI, HI), (HI, LO), (LO, HI))


def gnn_ffn(nc, x, dst_cols, src_cols, dst_rows, w_self0, w_neigh0, b0, w_self1, w_neigh1, b1,
            w_fc, w_proj, out):
    with ExitStack() as ctx:
        def sem(name):
            return ctx.enter_context(nc.semaphore(name))

        counts_dram = nc.dram_tensor("counts_dram", (TILES, P, NODES), F32, kind="Internal").ap()
        at_dram = nc.dram_tensor("at_dram", (TILES, P, TILES, 2, P), F32, kind="Internal").ap()
        xt_dram = [nc.dram_tensor(f"xt{l}_dram", (TILES, 128, 2, KD, P), F32, kind="Internal").ap()
                   for l in range(2)]
        x2_dram = [nc.dram_tensor(f"x2{g}_dram", (128, KD, 2, count * P), F32, kind="Internal").ap()
                   for g, (_, count, _) in enumerate(GROUPS_OF_TILES)]
        x1_dram = nc.dram_tensor("x1_dram", (NODES, D), F32, kind="Internal").ap()

        cursor = [(nc.sbuf_base + 63) // 64 * 64]

        def at(address, name, shape, dt):
            return nc.alloc_sbuf_tensor_at(name, shape, dt, offset=address)

        def nbytes(shape, dt):
            n = 2 if dt in (BF16, F16) else 4
            for s in shape[1:]:
                n *= s
            return (n + 31) // 32 * 32

        def put(name, shape, dt):
            a = cursor[0]
            cursor[0] += nbytes(shape, dt)
            assert cursor[0] <= nc.sbuf_usable_end, (name, cursor[0])
            return at(a, name, shape, dt)

        ident = put("ident", [128, 128], F32)
        deg = put("deg", [P, TILES, 3], F32)
        dinv = put("dinv", [P, TILES], F32)
        deg_sum = put("deg_sum", [P, TILES], F32)
        deg_max = put("deg_max", [P, 1], F32)
        many = put("many", [1, 1], F32)
        many_int = put("many_int", [1, 1], I32)
        group_range = put("group_range", [1, 2 * TILES], I32)
        eps_col = put("eps_col", [P, 1], F32)
        stats = put("stats", [P, 2, 2, 6], F32)
        mean_var = put("mean_var", [P, 2, 2], F32)
        std = put("std", [P, 2], F32)
        rstd = put("rstd", [P, 2], F32)
        newton = put("newton", [P, 2], F32)
        ident_narrow = put("ident_narrow", [P, P], BF16)
        base = cursor[0]
        z = put("z", [P, TILES, 2, D], F32R)
        w_at = cursor[0]
        w = put("w", [128, KD, 2, D], F32R)
        w_landing = at(w_at, "w_landing", [128, KD, 2, D], F32)
        w_raw = put("w_raw", [128, 2, D], F32)
        xt = [put(f"xt{j}", [128, 2, KD, P], F32R) for j in range(2)]
        at_tile_at = cursor[0]
        at_tile = put("at_tile", [P, TILES, 2, P], F32R)
        rows = [put(f"rows{j}", [P, D], F32) for j in range(4)]
        xt_out_at = cursor[0]
        xt_out = put("xt_out", [128, 2, KD, P], F32R)
        bias = put("bias", [P, D], F32)
        counts_back = at(at_tile_at, "counts_back", [P, 2, NODES], F32)
        turned = at(xt_out_at, "turned", [P, TILES, 2, P], F32R)
        graph_end = cursor[0]

        def put_from(address, *what):
            made = []
            cursor[0] = address
            for name, shape, dt in what:
                made.append(put(name, shape, dt))
            return made

        z_end, w_end = base + nbytes([P, TILES, 2, D], F32R), base + nbytes([P, TILES, 2, D], F32R) + nbytes([128, KD, 2, D], F32R)
        raw_end = w_end + nbytes([128, 2, D], F32)
        n0, n1 = (count * P for _, count, _ in GROUPS_OF_TILES)
        pr_w, hid, y0 = put_from(base, ("pr_w", [128, BLOCK, 2, D], F32R), ("hid", [128, BLOCK, 2, n0], F32R),
                                 ("y0", [P, n0 // P, D], F32))
        assert cursor[0] <= z_end
        x2t0, fc_w = put_from(z_end, ("x2t0", [128, KD, 2, n0], F32R), ("fc_w", [128, 2, KD, 2, F_TILE], F32R))
        assert cursor[0] <= w_end
        (fc_raw,) = put_from(w_end, ("fc_raw", [128, 2, KD, F_TILE], F32))
        pr_raw, relu, square, x2t1, lif_a = put_from(
            raw_end, ("pr_raw", [128, 2, D], F32), ("relu", [128, 2, HALF], F32), ("square", [128, 2, HALF], F32),
            ("x2t1", [128, KD, 2, n1], F32R), ("lif_a", [P, D], F32))
        assert cursor[0] <= nc.sbuf_usable_end
        y1, x1_0, lif_b = put_from(z_end, ("y1", [P, n1 // P, D], F32), ("x1_0", [P, n0 // P, D], F32),
                                   ("lif_b", [P, D], F32))
        assert cursor[0] <= z_end + nbytes([128, KD, 2, n0], F32R)
        hid_at = base + nbytes([128, BLOCK, 2, D], F32R)
        hid1, lif_c = put_from(hid_at, ("hid1", [128, BLOCK, 2, n1], F32R), ("lif_c", [P, D], F32))
        assert cursor[0] <= hid_at + nbytes([128, BLOCK, 2, n0], F32R)
        x2t1_at = raw_end + nbytes([128, 2, D], F32) + 2 * nbytes([128, 2, HALF], F32)
        x1_1, sign, spikes = put_from(x2t1_at, ("x1_1", [P, n1 // P, D], F32), ("sign", [P, 2, HALF], BF16),
                                      ("spikes", [P, SPIKE_SLOTS, HALF], BF16))
        assert cursor[0] <= x2t1_at + nbytes([128, KD, 2, n1], F32R)
        y0_at = hid_at + nbytes([128, BLOCK, 2, n0], F32R)
        hid1_more, pr_w4 = put_from(y0_at, ("hid1_more", [128, BLOCK, 2, n1], F32R), ("pr_w4", [128, 2, D], F32R))
        assert cursor[0] <= y0_at + nbytes([P, n0 // P, D], F32)
        x1_0_at = z_end + nbytes([P, n1 // P, D], F32)
        pr_w_more = [pr_w4] + put_from(x1_0_at, *((f"pr_w{j}", [128, 2, D], F32R) for j in range(BLOCK + 1, 2 * BLOCK)))
        assert cursor[0] <= x1_0_at + nbytes([P, n0 // P, D], F32)

        def hid_of(g, j):
            return (hid, hid1)[g][:, j, :, :] if j < BLOCK else hid1_more[:, j - BLOCK, :, :]

        def pr_of(j):
            return pr_w[:, j, :, :] if j < BLOCK else pr_w_more[j - BLOCK][:, :, :]
        x2t, y = (x2t0, x2t1), (y0, y1)

        cursor[0] = base
        iota = put("iota", [P, NODES], F16)
        edge_int = put("edge_int", [P, 2, CHUNKS], I32)
        src_f = put("src_f", [P, CHUNKS], F32)
        dst_f = put("dst_f", [P, CHUNKS], F32)
        minus_dst_f = put("minus_dst_f", [P, CHUNKS], F32)
        dst_int = put("dst_int", [GROUPS, GROUP * P], I32)
        dst_rows_f = put("dst_rows_f", [GROUPS, GROUP * P], F32)
        group_min = put("group_min", [GROUPS, 1], F32)
        group_max = put("group_max", [GROUPS, 1], F32)
        tile_first = put("tile_first", [GROUPS, TILES], F32)
        tile_next = put("tile_next", [GROUPS, TILES], F32)
        from_end = put("from_end", [GROUPS, TILES], F32)
        from_start = put("from_start", [GROUPS, TILES], F32)
        below = put("below", [GROUPS, TILES], F32)
        above = put("above", [GROUPS, TILES], F32)
        may_hold = put("may_hold", [GROUPS, TILES], F32)
        bounds = put("bounds", [GROUPS, 2 * TILES], F32)
        bound_col = put("bound_col", [2 * TILES, 1], F32)
        range_f = put("range_f", [1, 2 * TILES], F32)
        zero_w = put("zero_w", [P, P], F16)
        src_hot = put("src_hot", [P, GROUP, NODES], BF16)
        dst_hot = put("dst_hot", [P, GROUP, P], BF16)
        dist = put("dist", [P, GROUP, P], BF16)
        counts = put("counts", [P, 2, NODES], F32)
        assert cursor[0] <= base + nbytes([P, TILES, 2, D], F32R)

        bank = ctx.enter_context(nc.psum_tensor("bank", [128, 8, HALF], F32))

        rows_in = sem("rows_in")
        edges_in = sem("edges_in")
        constants = sem("constants")
        edge_steps = sem("edge_steps")
        bounds_turned = sem("bounds_turned")
        range_ready = sem("range_ready")
        src_hot_ready = [sem(f"src_hot_ready{q}") for q in range(GROUP)]
        dst_hot_ready = [sem(f"dst_hot_ready{q}") for q in range(GROUP // 2)]
        dist_ready = [sem(f"dist_ready{q}") for q in range(GROUP // 2)]
        hot_used = [sem(f"hot_used{q}") for q in range(GROUP)]
        counts_summed = sem("counts_summed")
        counts_copied = sem("counts_copied")
        counts_free = sem("counts_free")
        counts_stored = sem("counts_stored")
        counts_in = [sem(f"counts_in{j}") for j in range(2)]
        counts_turned = sem("counts_turned")
        turned_high = sem("turned_high")
        turned_low = sem("turned_low")
        at_stored = sem("at_stored")
        turned_free = sem("turned_free")
        deg_steps = sem("deg_steps")
        deg_turned = sem("deg_turned")
        table_loaded = sem("table_loaded")
        many_ready = sem("many_ready")

        w_in = [sem(f"w_in{k}") for k in range(KD)]
        w_high = sem("w_high")
        w_low = sem("w_low")
        w_used = sem("w_used")
        dense_done = sem("dense_done")
        xt_in = [sem(f"xt_in{j}") for j in range(2)]
        xt_stored = [sem(f"xt_stored{l}") for l in range(2)]
        x2_stored = sem("x2_stored")
        x_in = [sem(f"x_in{j}") for j in range(2)]
        ln_steps = [sem(f"ln_steps{l}") for l in range(2)]
        ln_std = [sem(f"ln_std{l}") for l in range(2)]
        row_ready = [sem(f"row_ready{l}") for l in range(3)]
        row_turned = [sem(f"row_turned{l}") for l in range(3)]
        row_high = [sem(f"row_high{l}") for l in range(3)]
        row_low = [sem(f"row_low{l}") for l in range(3)]
        row_free = [sem(f"row_free{l}") for l in range(3)]
        z_high = sem("z_high")
        z_low = sem("z_low")
        at_in = sem("at_in")
        at_used = sem("at_used")
        bias_in = sem("bias_in")
        self_taken = sem("self_taken")
        x1_ready = sem("x1_ready")
        x1_stored = sem("x1_stored")
        x1_free = sem("x1_free")
        res_in = sem("res_in")
        res_used = sem("res_used")

        x2_in = [sem(f"x2_in{k}") for k in range(KD)]
        x2_in_last = sem("x2_in_last")
        fc_in = [sem(f"fc_in{q}") for q in range(2)]
        fc_high = sem("fc_high")
        fc_low = sem("fc_low")
        pr_in = [sem(f"pr_in{q}") for q in range(2)]
        pr_high = sem("pr_high")
        pr_low = sem("pr_low")
        hid_summed = sem("hid_summed")
        hid_relu = sem("hid_relu")
        hid_square = sem("hid_square")
        hid_high = sem("hid_high")
        hid_low = sem("hid_low")
        proj_summed = sem("proj_summed")
        y_added = sem("y_added")
        y_zero = sem("y_zero")
        x1_in = [sem(f"x1_in{g}") for g in range(2)]
        lif_steps = sem("lif_steps")
        mem_steps = sem("mem_steps")
        signs = sem("signs")
        spikes_ready = sem("spikes_ready")
        spikes_counted = sem("spikes_counted")
        result_ready = sem("result_ready")
        out_stored = [sem(f"out_stored{g}") for g in range(2)]

        ROUNDS = ((0, 4), (4, 4), (8, 2))
        PAIRS = TILES // 2

        def range_registers(engine, name):
            return [engine.alloc_register(f"{name}_{end}{j}") for j in range(2) for end in ("first", "end")]

        def load_ranges(engine, registers, i):
            engine.load(registers, group_range[0:1, ds(4 * i, 4)])
            values = [bass.RuntimeValue.of_register_unchecked(register, min_val=end, max_val=GROUPS - 1 + end)
                      for register, end in zip(registers, (0, 1, 0, 1))]
            return values[0:2], values[2:4]

        LAST_HALVES = 2 * n1 // P
        MEM_STAGES = [[(half - late, step + late * MEM_STEPS // 2) for step in range(MEM_STEPS // 2) for late in (0, 1)
                       if 0 <= half - late < LAST_HALVES] for half in range(LAST_HALVES + 1)]
        MEM_ORDER = [entry for stage in MEM_STAGES for entry in stage]
        SPIKE_STAGES = [[(half, 0)] * (half < LAST_HALVES) + [(h, (step + 1) // 2) for h, step in stage if step % 2 == 1]
                        for half, stage in enumerate(MEM_STAGES)]
        SPIKE_ORDER = [entry for stage in SPIKE_STAGES for entry in stage]

        def mem_of(half, t):
            return (lif_a, lif_b)[t % 2][:, half % 2 * HALF:(half % 2 + 1) * HALF]

        def half_of(tiles, half):
            return tiles[:, half // 2, half % 2 * HALF:(half % 2 + 1) * HALF]

        def raw_w(k):
            return w_raw[:, k, :] if k < 2 else w_landing[:, k, LO, :]

        block = ctx.enter_context(nc.Block())

        @block.sync
        def _(sp):
            w_dram = [v.rearrange("(k p) n -> k p n", p=128) for v in (w_neigh0, w_self0, w_neigh1, w_self1)]
            x_tiles = x.rearrange("(t p) d -> t p d", p=P)

            def load_w(phase, k):
                if phase > 0:
                    if k < 2:
                        sp.wait_ge(w_low, KD * (phase - 1) + k + 1)
                    elif k < KD - 1:
                        sp.wait_ge(w_used, (KD - 1) * (TILES * phase - 1) + k + 1)
                    else:
                        sp.wait_ge(dense_done, 2 * TILES * phase)
                sp.dma_start(raw_w(k), w_dram[phase][k]).then_inc(w_in[k], 16)

            def load_xt(phase, n, j):
                sp.wait_ge(dense_done, 2 * (TILES * phase + n - 1))
                sp.dma_start(xt[j][:, :, :, :].bitcast(F32),
                             xt_dram[phase // 2][ds(n, 1)].rearrange("a p h k m -> (a p) h k m")).then_inc(xt_in[j], 16)

            sp.dma_start(dst_int[:, :], dst_rows).then_inc(rows_in, 16)
            sp.dma_start(edge_int[:, 0, :], src_cols).then_inc(edges_in, 16)
            sp.dma_start(edge_int[:, 1, :], dst_cols).then_inc(edges_in, 16)
            sp.dma_start(rows[0][:, :], x_tiles[0]).then_inc(x_in[0], 16)
            sp.dma_start(rows[1][:, :], x_tiles[1]).then_inc(x_in[1], 16)
            for k in range(KD):
                load_w(0, k)
            load_w(1, 0)
            load_w(1, 1)

            def load_counts(n, j):
                sp.wait_ge(counts_stored, 16 * (n + 1))
                if not isinstance(n, int) or n > 1:
                    sp.wait_ge(counts_turned, 3 * n - 3)
                sp.dma_start(counts_back[:, j, :], counts_dram[ds(n, 1)].rearrange("a p m -> (a p) m")).then_inc(counts_in[j], 16)

            def load_x(n, j):
                sp.wait_ge(row_ready[0], n - 1)
                sp.dma_start(rows[j][:, :], x_tiles[ds(n, 1)].rearrange("a p d -> (a p) d")).then_inc(x_in[j], 16)

            load_counts(0, 0)
            load_counts(1, 1)
            with sp.Fori(1, PAIRS) as i:
                for j in range(2):
                    load_x(2 * i + j, j)
                    load_counts(2 * i + j, j)

            def load_rest(phase, stored, need):
                sp.wait_ge(stored, need)
                load_xt(phase, 0, 0)
                for k in range(2, KD):
                    load_w(phase, k)

            for l in range(2):
                own = 2 * l + 1
                if l == 1:
                    load_rest(2, xt_stored[1], 16)
                    sp.wait_ge(xt_stored[1], 32)
                    load_xt(2, 1, 1)
                    load_w(own, 0)
                    load_w(own, 1)
                    with sp.Fori(1, PAIRS) as i:
                        for j in range(2):
                            sp.wait_ge(xt_stored[1], 16 * (2 * i + j + 1))
                            load_xt(2, 2 * i + j, j)
                load_rest(own, xt_stored[l], 16 * (TILES - 1))

                def load_at(n):
                    sp.wait_ge(at_used, TILES * l + n + 1)
                    sp.dma_start(at_tile[:, :, :, :].bitcast(F32),
                                 at_dram[ds(n, 1)].rearrange("a p s h m -> (a p) s h m")).then_inc(at_in, 16)

                def load_res(n):
                    sp.wait_ge(res_used, n + 1)
                    sp.dma_start(rows[0][:, :], x_tiles[ds(n, 1)].rearrange("a p d -> (a p) d")).then_inc(res_in, 16)

                if l == 0:
                    sp.wait_ge(counts_turned, 3 * TILES)
                load_at(0)
                sp.wait_ge(xt_stored[l], 16 * TILES)
                load_xt(own, 1, 1)
                if l == 0:
                    sp.wait_ge(at_stored, 16 * TILES)
                else:
                    sp.wait_ge(self_taken, TILES + 1)
                sp.dma_start(bias[:, :], (b0, b1)[l].partition_broadcast(P)).then_inc(bias_in, 16)
                if l == 0:
                    load_w(2, 0)
                    load_w(2, 1)
                else:
                    load_res(0)
                    load_res(1)
                with sp.Fori(1, PAIRS) as i:
                    for j in range(2):
                        load_xt(own, 2 * i + j, j)
                        load_at(2 * i + j - 1)
                        if l == 1:
                            load_res(2 * i + j)
                load_at(TILES - 1)

            def load_fc(m, q, f, after_first=True):
                if after_first:
                    sp.wait_ge(fc_low, m - 1)
                sp.dma_start(fc_raw[:, q, :, :], w_fc[ds(f, 1)].rearrange("a p k c -> (a p) k c")).then_inc(fc_in[q], 16)

            def load_pr(m, q, f, after_first=True):
                if after_first:
                    sp.wait_ge(pr_low, m - 1)
                sp.dma_start(pr_raw[:, q, :], w_proj[ds(f, 1)].rearrange("a p d -> (a p) d")).then_inc(pr_in[q], 16)

            sp.wait_ge(w_low, 4 * KD)
            sp.wait_ge(x2_stored, 32 * GROUPS_OF_TILES[0][1])
            for k in range(KD):
                last_w = ((k + 1) * 2 * n0 - 1) // (2 * D)
                assert last_w < KD - 1
                sp.wait_ge(w_used, (KD - 1) * (4 * TILES - 1) + last_w + 1)
                sp.dma_start(x2t0[:, k, :, :].bitcast(F32), x2_dram[0][:, k, :, :]).then_inc(x2_in[k], 16)
                if k in (2, 5):
                    load_fc(k // 3, k // 3, k // 3, after_first=False)
            sp.wait_ge(dense_done, 2 * 4 * TILES)
            load_pr(0, 0, 0, after_first=False)
            load_pr(1, 1, 1, after_first=False)
            for g in range(2):
                with sp.Fori(1 - g, F_TILES // 2) as i:
                    for q in range(2):
                        load_fc(F_TILES * g + 2 * i + q, q, 2 * i + q)
                        load_pr(F_TILES * g + 2 * i + q, q, 2 * i + q)
            out_tiled = out.rearrange("(t p) d -> p t d", p=P)
            for half in range(LAST_HALVES):
                sp.wait_ge(result_ready, half + 1)
                sp.dma_start(half_of(out_tiled[:, n0 // P:, :], half), half_of(x1_1, half)).then_inc(out_stored[1], 16)
            sp.wait_ge(out_stored[0], 16 * (n0 // P))
            sp.wait_ge(out_stored[1], 16 * LAST_HALVES)

        @block.gpsimd
        def _(pool):
            nc.gpsimd.iota(tile_first[:, :], pattern=[[P, TILES]], base=0, channel_multiplier=0,
                           allow_small_or_imprecise_dtypes=True).then_inc(constants, 1)
            nc.gpsimd.iota(tile_next[:, :], pattern=[[P, TILES]], base=P, channel_multiplier=0,
                           allow_small_or_imprecise_dtypes=True).then_inc(constants, 1)
            nc.gpsimd.iota(from_start[:, :], pattern=[[0, TILES]], base=1, channel_multiplier=1,
                           allow_small_or_imprecise_dtypes=True).then_inc(constants, 1)
            nc.gpsimd.iota(from_end[:, :], pattern=[[0, TILES]], base=GROUPS, channel_multiplier=-1,
                           allow_small_or_imprecise_dtypes=True).then_inc(constants, 1)
            nc.gpsimd.memset(ident[:, :], 0.0).then_inc(constants, 1)
            pool.wait_ge(constants, 5)
            nc.gpsimd.affine_select(out=ident[:, :], in_=ident[:, :], compare_op=ALU.not_equal, fill=1.0,
                                    base=0, pattern=[[-1, 128]], channel_multiplier=1).then_inc(constants, 1)
            nc.gpsimd.memset(eps_col[:, :], EPS).then_inc(constants, 1)
            nc.gpsimd.memset(zero_w[:, :], 0.0).then_inc(constants, 1)
            nc.gpsimd.iota(iota[:, :], pattern=[[1, NODES]], base=0, channel_multiplier=0,
                           allow_small_or_imprecise_dtypes=True).then_inc(constants, 1)

            pool.wait_ge(constants, 6)
            nc.gpsimd.tensor_copy(ident_narrow[:, :], ident[0:P, 0:P]).then_inc(constants, 1)

            for k in range(KD):
                pool.wait_ge(w_in[k], 16)
                nc.gpsimd.tensor_copy(w[:, k, HI, :], raw_w(k)).then_inc(w_high, 1)
                pool.wait_ge(w_high, k + 1)
                nc.gpsimd.tensor_tensor(w[:, k, LO, :], raw_w(k), w[:, k, HI, :].bitcast(F32),
                                        ALU.subtract).then_inc(w_low, 1)

            pool.sem_inc(counts_free, 2)
            pool.sem_inc(row_free[0], 2)
            pool.sem_inc(turned_free, 1)
            with pool.Fori(0, PAIRS) as i:
                for j in range(2):
                    pool.wait_ge(counts_copied, 2 * i + j + 3)
                    pool.dma_start(counts_dram[ds(2 * i + j, 1)].rearrange("a p m -> (a p) m"),
                                   counts[:, j, :]).then_inc(counts_stored, 16)
                    pool.wait_ge(counts_stored, 16 * (2 * i + j + 1))
                    pool.sem_inc(counts_free, 1)

            def store_row(l, n, tile):
                pool.wait_ge(row_high[l], 2 * n + 2)
                pool.wait_ge(row_low[l], 2 * n + 4)
                pool.dma_start(xt_dram[l][ds(n, 1)].rearrange("a p h k m -> (a p) h k m"),
                               tile[:, :, :, :].bitcast(F32)).then_inc(xt_stored[l], 16)

            def free_row(l, n):
                pool.wait_ge(xt_stored[l], 16 * (n + 1))
                pool.sem_inc(row_free[l], 1)

            def store_first_pass(n, j):
                pool.wait_ge(turned_high, 3 * n + 3)
                pool.wait_ge(turned_low, 3 * n + 5)
                pool.dma_start(at_dram[ds(n, 1)].rearrange("a p s h m -> (a p) s h m"),
                               turned[:, :, :, :].bitcast(F32)).then_inc(at_stored, 16)
                free_row(0, n)
                pool.wait_ge(at_stored, 16 * (n + 1))
                pool.sem_inc(turned_free, 1)
                if not isinstance(n, int) or n + 1 < TILES:
                    store_row(0, n + 1, xt[1 - j])

            store_row(0, 0, xt[0])
            with pool.Fori(0, PAIRS - 1) as i:
                store_first_pass(2 * i, 0)
                store_first_pass(2 * i + 1, 1)
            store_first_pass(TILES - 2, 0)
            store_first_pass(TILES - 1, 1)
            pool.sem_inc(row_free[1], 1)
            with pool.Fori(0, TILES) as n:
                store_row(1, n, xt_out)
                free_row(1, n)
            pool.sem_inc(row_free[2], 1)
            pool.sem_inc(x1_free, 1)
            for g, (first, count, _) in enumerate(GROUPS_OF_TILES):
                with pool.Fori(first, first + count) as n:
                    pool.wait_ge(x1_ready, n + 1)
                    pool.dma_start(x1_dram.rearrange("(t p) d -> t p d", p=P)[ds(n, 1)].rearrange("a p d -> (a p) d"),
                                   rows[1][:, :]).then_inc(x1_stored, 16)
                    pool.wait_ge(x1_stored, 16 * (n + 1))
                    pool.sem_inc(x1_free, 1)
                    pool.wait_ge(row_high[2], 2 * n + 2)
                    pool.wait_ge(row_low[2], 2 * n + 4)
                    for h in (HI, LO):
                        pool.dma_start(x2_dram[g][:, :, h, ds((n - first) * P, P)],
                                       xt_out[:, h, :, :].bitcast(F32)).then_inc(x2_stored, 16)
                    pool.wait_ge(x2_stored, 32 * (n + 1))
                    pool.sem_inc(row_free[2], 1)

            pool.wait_ge(at_used, 2 * TILES + 1)
            nc.gpsimd.memset(y0[:, :, :], 0.0).then_inc(y_zero, 1)
            pool.dma_start(x2t1[:, :, :, :].bitcast(F32), x2_dram[1]).then_inc(x2_in_last, 16)
            pool.wait_ge(hid_summed, 2 * F_TILES + 2)
            nc.gpsimd.memset(y1[:, :, :], 0.0).then_inc(y_zero, 1)
            x1_tiled = x1_dram.rearrange("(t p) d -> p t d", p=P)
            out_tiled = out.rearrange("(t p) d -> p t d", p=P)
            pool.dma_start(x1_0[:, :, :], x1_tiled[:, 0:n0 // P, :]).then_inc(x1_in[0], 16)
            for n in range(n0 // P):
                pool.wait_ge(lif_steps, LIF_STEPS * (n + 1) + 1)
                pool.dma_start(out_tiled[:, n, :], x1_0[:, n, :]).then_inc(out_stored[0], 16)
            pool.wait_ge(hid_summed, 3 * F_TILES + 2)
            pool.dma_start(x1_1[:, :, :], x1_tiled[:, n0 // P:, :]).then_inc(x1_in[1], 16)

        @block.scalar
        def _(act):
            visit = act.alloc_register("act_visit")
            act.reg_mov(visit, 1)
            act.wait_ge(constants, 9)
            nc.scalar.activation(std[:, 0:1], eps_col[:, :], ACT.Sqrt).then_inc(table_loaded, 1)
            act.wait_ge(edge_steps, 10)
            act.wait_ge(range_ready, 1)
            act.sem_inc(counts_copied, 2)
            for h in range(GROUP // 2):
                act.sem_inc(dst_hot_ready[h], 1)

            registers = range_registers(act, "act")

            def dst_one_hots(t, first, end):
                with act.Fori(first, end) as g:
                    for h, (q, last) in enumerate(((0, 1), (2, 2))):
                        act.wait_ge(dst_hot_ready[h], visit)
                        for c in range(q, last + 1):
                            ins = nc.scalar.activation(dist[:, c, :], iota[:, ds(t * P, P)], ACT.Square,
                                                       bias=minus_dst_f[:, ds(g * GROUP + c, 1)])
                        ins.then_inc(dist_ready[h], 1)
                        act.wait_ge(dist_ready[h], visit)
                        act.wait_ge(hot_used[last], visit)
                        nc.scalar.activation(dst_hot[:, q:last + 1, :], dist[:, q:last + 1, :],
                                             ACT.Relu, bias=1.0, scale=-1.0).then_inc(dst_hot_ready[h], 1)
                    act.reg_add(visit, visit, 1)

            def copy_counts(t, j):
                act.wait_ge(counts_summed, t + 1)
                act.wait_ge(counts_free, t + 1)
                for b, (c0, n) in enumerate(COUNT_COLS):
                    ins = nc.scalar.activation(counts[:, j, c0:c0 + n], bank[0:P, 3 * j + b, 0:n], ACT.Copy,
                                               accum_out=deg[:, ds(t, 1), b])
                ins.then_inc(counts_copied, 1)

            def standard_deviation(l, n, j):
                act.wait_ge(ln_steps[l], LN_STEPS * n + 4)
                nc.scalar.activation(std[:, j:j + 1], mean_var[:, j, 1:2], ACT.Sqrt,
                                     bias=eps_col[:, :]).then_inc(ln_std[l], 1)

            even, odd = load_ranges(act, registers, 0)
            dst_one_hots(0, *even)
            dst_one_hots(1, *odd)
            copy_counts(0, 0)
            with act.Fori(1, PAIRS - 1) as i:
                even, odd = load_ranges(act, registers, i)
                dst_one_hots(2 * i, *even)
                copy_counts(2 * i - 1, 1)
                dst_one_hots(2 * i + 1, *odd)
                copy_counts(2 * i, 0)
            even, odd = load_ranges(act, registers, PAIRS - 1)
            dst_one_hots(TILES - 2, *even)
            copy_counts(TILES - 3, 1)
            standard_deviation(0, 0, 0)
            standard_deviation(0, 1, 1)
            dst_one_hots(TILES - 1, *odd)
            copy_counts(TILES - 2, 0)
            copy_counts(TILES - 1, 1)

            def high_of_row(l, n, tile, func):
                act.wait_ge(row_free[l], n + 1)
                for q in range(2):
                    act.wait_ge(row_turned[l], 2 * n + q + 1)
                    nc.scalar.activation(tile[:, HI, 4 * q:4 * q + 4, :],
                                         bank[:, 6 + q, 0:4 * P].rearrange("p (k m) -> p k m", k=4),
                                         func).then_inc(row_high[l], 1)

            def high_of_turned(n, j, r):
                s0, c = ROUNDS[r]
                if r == 0:
                    act.wait_ge(turned_free, n + 1)
                act.wait_ge(counts_turned, 3 * n + r + 1)
                nc.scalar.activation(turned[:, s0:s0 + c, HI, :],
                                     bank[0:P, 4 + (3 * j + r) % 2, 0:c * P].rearrange("p (s m) -> p s m", s=c),
                                     ACT.Copy).then_inc(turned_high, 1)

            def high_of_z(l, n, j):
                for q in range(2):
                    act.wait_ge(dense_done, 2 * (2 * TILES * l + n) + q + 1)
                    nc.scalar.activation(z[:, ds(n, 1), HI, q * HALF:(q + 1) * HALF],
                                         bank[0:P, 2 * j + q, :].unsqueeze(1), ACT.Copy).then_inc(z_high, 1)

            def high_of_w(phase):
                for k in range(KD):
                    act.wait_ge(w_in[k], 16 * (phase + 1))
                    if k < 2:
                        act.wait_ge(w_used, (KD - 1) * (TILES * phase - 1) + k + 1)
                    nc.scalar.activation(w[:, k, HI, :], raw_w(k), ACT.Copy).then_inc(w_high, 1)

            def first_pass(n, j):
                if not isinstance(n, int) or n + 1 < TILES:
                    high_of_row(0, n + 1, xt[1 - j], ACT.Copy)
                high_of_turned(n, j, 0)
                high_of_turned(n, j, 1)
                if not isinstance(n, int) or n + 2 < TILES:
                    standard_deviation(0, n + 2, j)
                high_of_turned(n, j, 2)
                if isinstance(n, int) and n == TILES - 1:
                    high_of_w(1)
                high_of_z(0, n, j)

            high_of_row(0, 0, xt[0], ACT.Copy)
            with act.Fori(0, PAIRS - 1) as i:
                first_pass(2 * i, 0)
                first_pass(2 * i + 1, 1)
            first_pass(TILES - 2, 0)
            first_pass(TILES - 1, 1)

            act.sem_inc(hid_relu, 2)
            with act.Fori(0, TILES - 1) as n:
                high_of_row(1, n, xt_out, ACT.Relu)
            high_of_w(2)
            high_of_z(1, 0, 0)
            high_of_row(1, TILES - 1, xt_out, ACT.Relu)
            high_of_z(1, 1, 1)
            with act.Fori(1, PAIRS - 1) as i:
                high_of_z(1, 2 * i, 0)
                high_of_z(1, 2 * i + 1, 1)
            high_of_z(1, TILES - 2, 0)
            high_of_w(3)
            high_of_z(1, TILES - 1, 1)
            standard_deviation(1, 0, 0)
            with act.Fori(0, PAIRS - 1) as i:
                for j in range(2):
                    high_of_row(2, 2 * i + j, xt_out, ACT.Copy)
                    standard_deviation(1, 2 * i + j + 1, 1 - j)
            high_of_row(2, TILES - 2, xt_out, ACT.Copy)
            act.wait_ge(fc_in[0], 16)
            act.wait_ge(dense_done, 2 * 4 * TILES)
            nc.scalar.activation(fc_w[:, 0, :, HI, :], fc_raw[:, 0, :, :], ACT.Copy).then_inc(fc_high, 1)
            standard_deviation(1, TILES - 1, 1)

            def in_slot(m, q):
                return 16 + 8 * (m - q)

            def high_of_fc(m, q, g):
                act.wait_ge(fc_in[q], in_slot(m, q))
                act.wait_ge(hid_summed, 2 * m if g == 0 else F_TILES + m + 1)
                nc.scalar.activation(fc_w[:, q, :, HI, :], fc_raw[:, q, :, :], ACT.Copy).then_inc(fc_high, 1)

            def high_of_pr(m, j, used):
                act.wait_ge(pr_in[j % 2], in_slot(m, j % 2))
                act.wait_ge(proj_summed, used)
                nc.scalar.activation(pr_of(j)[:, HI, :], pr_raw[:, j % 2, :], ACT.Copy).then_inc(pr_high, 1)

            def relu_and_high(bank_index, slot, hid, c0, n):
                act.wait_ge(hid_summed, bank_index + 3)
                act.wait_ge(hid_low, bank_index + 1)
                nc.scalar.activation(relu[:, slot, 0:n], bank[:, 4 + slot, 0:n], ACT.Relu).then_inc(hid_relu, 1)
                act.wait_ge(hid_relu, bank_index + 3)
                nc.scalar.activation(hid[:, HI, c0:c0 + n], relu[:, slot, 0:n], ACT.Square).then_inc(hid_high, 1)

            def ffn_block(g, b, first=False, last=False):
                _, count, columns = GROUPS_OF_TILES[g]
                length = 2 * BLOCK if last else BLOCK
                for j in range(length):
                    m = F_TILES * g + BLOCK * b + j
                    if not (last and j == length - 1):
                        high_of_fc(m + 1, (j + 1) % 2, g)
                    if j == BLOCK:
                        act.wait_ge(lif_steps, LIF_STEPS * n0 // P + 1)
                        act.wait_ge(out_stored[0], 16 * (n0 // P))
                    if first and j == 0:
                        act.wait_ge(at_used, 2 * TILES + 1)
                    high_of_pr(m, j, 2 * count * b + 1 + g * ADDED[0])
                    for c, (c0, n) in enumerate(columns):
                        bank_index = 2 * m + c if g == 0 else F_TILES + m
                        relu_and_high(bank_index, c if g == 0 else j % 2, hid_of(g, j), c0, n)
                        if first and j == 1 and c == 0:
                            high_of_row(2, TILES - 1, xt_out, ACT.Copy)

            ffn_block(0, 0, first=True)
            with act.Fori(1, BLOCKS) as b:
                ffn_block(0, b)
            with act.Fori(0, BLOCKS - 2) as b:
                ffn_block(1, b)
            ffn_block(1, BLOCKS - 2, last=True)

            def spikes_from_signs(spike):
                act.wait_ge(signs, spike + 1)
                if spike >= SPIKE_SLOTS:
                    act.wait_ge(spikes_counted, spike - SPIKE_SLOTS + 1)
                nc.scalar.activation(spikes[:, spike % SPIKE_SLOTS, :], sign[:, spike % 2, :], ACT.Relu,
                                     scale=-1.0).then_inc(spikes_ready, 1)

            for spike, (half, s) in enumerate(SPIKE_ORDER):
                if s == 0:
                    act.wait_ge(y_added, Y_START + sum(ADDED) - LAST_HALVES + half + 1)
                    source = half_of(y1, half)
                else:
                    act.wait_ge(mem_steps, MEM_ORDER.index((half, 2 * s - 1)) + 1)
                    source = mem_of(half, s - 1)
                if spike >= 2:
                    act.wait_ge(spikes_ready, spike - 1)
                nc.scalar.activation(sign[:, spike % 2, :], source, ACT.Sign, bias=1.0, scale=-1.0).then_inc(signs, 1)
                if spike > 0:
                    spikes_from_signs(spike - 1)
            spikes_from_signs(len(SPIKE_ORDER) - 1)

        @block.vector
        def _(dve):
            dve.wait_ge(rows_in, 16)
            nc.vector.tensor_copy(dst_rows_f[:, :], dst_int[:, :]).then_inc(edge_steps, 1)
            dve.wait_ge(edge_steps, 1)
            nc.vector.tensor_reduce(group_min[:, :], dst_rows_f[:, :], AX.X, ALU.min).then_inc(edge_steps, 1)
            nc.vector.tensor_reduce(group_max[:, :], dst_rows_f[:, :], AX.X, ALU.max).then_inc(edge_steps, 1)
            dve.wait_ge(edge_steps, 3)
            dve.wait_ge(constants, 4)
            nc.vector.tensor_scalar(below[:, :], tile_next[:, :], group_min[:, 0:1], None, ALU.is_gt).then_inc(edge_steps, 1)
            nc.vector.tensor_scalar(above[:, :], tile_first[:, :], group_max[:, 0:1], None, ALU.is_le).then_inc(edge_steps, 1)
            dve.wait_ge(edge_steps, 5)
            nc.vector.tensor_tensor(may_hold[:, :], below[:, :], above[:, :], ALU.mult).then_inc(edge_steps, 1)
            dve.wait_ge(edge_steps, 6)
            nc.vector.tensor_tensor(bounds[:, 0:TILES], may_hold[:, :], from_end[:, :], ALU.mult).then_inc(edge_steps, 1)
            nc.vector.tensor_tensor(bounds[:, TILES:], may_hold[:, :], from_start[:, :], ALU.mult).then_inc(edge_steps, 1)
            dve.wait_ge(edges_in, 32)
            nc.vector.tensor_copy(src_f[:, :], edge_int[:, 0, :]).then_inc(edge_steps, 1)
            nc.vector.tensor_scalar(minus_dst_f[:, :], edge_int[:, 1, :], -1.0, None, ALU.mult).then_inc(edge_steps, 1)
            dve.wait_ge(bounds_turned, 1)
            nc.vector.tensor_reduce(bound_col[:, :], bank[0:2 * TILES, 6, 0:GROUPS], AX.X, ALU.max).then_inc(edge_steps, 1)
            nc.vector.tensor_copy(dst_f[:, :], edge_int[:, 1, :]).then_inc(edge_steps, 1)
            dve.wait_ge(bounds_turned, 2)
            nc.vector.tensor_scalar(range_f[:, 0:TILES], bank[0:1, 7, 0:TILES], -1.0, float(GROUPS),
                                    ALU.mult, ALU.add).then_inc(edge_steps, 1)
            dve.wait_ge(edge_steps, 13)
            nc.vector.tensor_scalar(range_f[:, 0:TILES], range_f[:, 0:TILES], float(GROUPS - 1), None,
                                    ALU.min).then_inc(edge_steps, 1)
            dve.wait_ge(edge_steps, 14)
            nc.vector.scalar_tensor_tensor(out=range_f[:, TILES:], in0=range_f[:, 0:TILES], scalar=1.0,
                                           in1=bank[0:1, 7, TILES:2 * TILES], op0=ALU.add, op1=ALU.max).then_inc(edge_steps, 1)
            dve.wait_ge(edge_steps, 15)
            nc.vector.tensor_copy(group_range[:, :].rearrange("p (t e) -> p e t", e=2),
                                  range_f[:, :].rearrange("p (e t) -> p e t", e=2)).then_inc(range_ready, 1)
            dve.wait_ge(range_ready, 1)
            dve.wait_ge(constants, 9)

            visit = dve.alloc_register("dve_visit")
            dve.reg_mov(visit, 1)

            registers = range_registers(dve, "dve")

            def src_one_hots(t, first, end):
                with dve.Fori(first, end) as g:
                    for q in range(GROUP):
                        dve.wait_ge(hot_used[q], visit)
                        if q == GROUP - 1:
                            nc.vector.tensor_scalar(dst_hot[:, q, :], iota[:, ds(t * P, P)],
                                                    dst_f[:, ds(g * GROUP + q, 1)], None, ALU.is_equal)
                        nc.vector.tensor_scalar(src_hot[:, q, :], iota[:, :], src_f[:, ds(g * GROUP + q, 1)],
                                                None, ALU.is_equal).then_inc(src_hot_ready[q], 1)
                    dve.reg_add(visit, visit, 1)

            def layer_norm(l, n, j, source, target):
                for q in range(2):
                    nc.vector.bn_stats(stats[:, j, q, :], source[:, q * HALF:(q + 1) * HALF]).then_inc(ln_steps[l], 1)
                dve.wait_ge(ln_steps[l], LN_STEPS * n + 2)
                nc.vector.memset(newton[:, j:j + 1], 0.0).then_inc(ln_steps[l], 1)
                nc.vector.bn_aggr(mean_var[:, j, :], stats[:, j, :, :]).then_inc(ln_steps[l], 1)
                dve.wait_ge(ln_std[l], n + 1)
                nc.vector.reciprocal(rstd[:, j:j + 1], std[:, j:j + 1]).then_inc(ln_steps[l], 1)
                nc.vector.tensor_scalar(newton[:, j:j + 1], mean_var[:, j, 1:2], EPS, None, ALU.add).then_inc(ln_steps[l], 1)
                dve.wait_ge(ln_steps[l], LN_STEPS * n + 6)
                nc.vector.scalar_tensor_tensor(out=newton[:, j:j + 1], in0=rstd[:, j:j + 1], scalar=rstd[:, j:j + 1],
                                               in1=newton[:, j:j + 1], op0=ALU.mult, op1=ALU.mult).then_inc(ln_steps[l], 1)
                dve.wait_ge(ln_steps[l], LN_STEPS * n + 7)
                nc.vector.tensor_scalar(newton[:, j:j + 1], newton[:, j:j + 1], -0.5, 1.5, ALU.mult, ALU.add).then_inc(ln_steps[l], 1)
                dve.wait_ge(ln_steps[l], LN_STEPS * n + 8)
                nc.vector.tensor_tensor(rstd[:, j:j + 1], rstd[:, j:j + 1], newton[:, j:j + 1], ALU.mult).then_inc(ln_steps[l], 1)
                dve.wait_ge(ln_steps[l], LN_STEPS * n + 9)
                nc.vector.tensor_scalar(target[:, :], source[:, :], mean_var[:, j, 0:1], rstd[:, j:j + 1],
                                        ALU.subtract, ALU.mult).then_inc(row_ready[2 * l], 1)

            def norm_x(n, j):
                if isinstance(n, int):
                    dve.wait_ge(x_in[j], 16 * (n // 2 + 1))
                else:
                    dve.wait_ge(x_in[j], 8 * (n - j) + 16)
                layer_norm(0, n, j, rows[j], rows[2 + j])

            def low_of_row(l, n, tile, relu=False):
                for q in range(2):
                    dve.wait_ge(row_high[l], 2 * n + q + 1)
                    source = bank[:, 6 + q, 0:4 * P].rearrange("p (k m) -> p k m", k=4)
                    high = tile[:, HI, 4 * q:4 * q + 4, :].bitcast(F32)
                    low = tile[:, LO, 4 * q:4 * q + 4, :]
                    if relu:
                        ins = nc.vector.scalar_tensor_tensor(out=low, in0=source, scalar=0.0, in1=high,
                                                             op0=ALU.max, op1=ALU.subtract)
                    else:
                        ins = nc.vector.tensor_tensor(low, source, high, ALU.subtract)
                    ins.then_inc(row_low[l], 1)

            def low_of_turned(n, j, r):
                s0, c = ROUNDS[r]
                dve.wait_ge(turned_high, 3 * n + r + 1)
                nc.vector.tensor_tensor(turned[:, s0:s0 + c, LO, :],
                                        bank[0:P, 4 + (3 * j + r) % 2, 0:c * P].rearrange("p (s m) -> p s m", s=c),
                                        turned[:, s0:s0 + c, HI, :].bitcast(F32), ALU.subtract).then_inc(turned_low, 1)

            def low_of_z(l, n, j):
                for q in range(2):
                    dve.wait_ge(z_high, 2 * TILES * l + 2 * n + q + 1)
                    nc.vector.tensor_tensor(z[:, ds(n, 1), LO, q * HALF:(q + 1) * HALF],
                                            bank[0:P, 2 * j + q, :].unsqueeze(1),
                                            z[:, ds(n, 1), HI, q * HALF:(q + 1) * HALF].bitcast(F32),
                                            ALU.subtract).then_inc(z_low, 1)

            def low_of_w(phase):
                for k in range(KD):
                    dve.wait_ge(w_high, KD * phase + k + 1)
                    nc.vector.tensor_tensor(w[:, k, LO, :], raw_w(k), w[:, k, HI, :].bitcast(F32),
                                            ALU.subtract).then_inc(w_low, 1)

            dve.sem_inc(turned_low, 2)
            dve.sem_inc(z_low, 4)
            dve.sem_inc(self_taken, 1)
            dve.sem_inc(res_used, 1)
            for l in range(3):
                dve.sem_inc(row_low[l], 2)
            with dve.Fori(0, PAIRS - 1) as i:
                even, odd = load_ranges(dve, registers, i)
                src_one_hots(2 * i, *even)
                src_one_hots(2 * i + 1, *odd)
            even, odd = load_ranges(dve, registers, PAIRS - 1)
            src_one_hots(TILES - 2, *even)
            norm_x(0, 0)
            norm_x(1, 1)
            src_one_hots(TILES - 1, *odd)

            def first_pass(n, j):
                if not isinstance(n, int) or n + 1 < TILES:
                    low_of_row(0, n + 1, xt[1 - j])
                low_of_turned(n, j, 0)
                low_of_turned(n, j, 1)
                if not isinstance(n, int) or n + 2 < TILES:
                    norm_x(n + 2, j)
                low_of_turned(n, j, 2)
                if isinstance(n, int) and n == TILES - 1:
                    low_of_w(1)
                low_of_z(0, n, j)

            dve.wait_ge(counts_copied, TILES + 2)
            nc.vector.tensor_reduce(deg_sum[:, :], deg[:, :, :], AX.X, ALU.add).then_inc(deg_steps, 1)
            dve.wait_ge(deg_steps, 1)
            nc.vector.tensor_reduce(deg_max[:, :], deg_sum[:, :], AX.X, ALU.max).then_inc(deg_steps, 1)
            low_of_row(0, 0, xt[0])
            nc.vector.tensor_scalar(dinv[:, :], deg_sum[:, :], 1.0, None, ALU.max).then_inc(deg_steps, 1)
            dve.wait_ge(deg_steps, 3)
            nc.vector.reciprocal(dinv[:, :], dinv[:, :]).then_inc(deg_steps, 1)
            dve.wait_ge(deg_turned, 1)
            nc.vector.tensor_reduce(many[:, :], bank[0:1, 3, 0:P], AX.X, ALU.max).then_inc(deg_steps, 1)
            dve.wait_ge(deg_steps, 5)
            nc.vector.tensor_scalar(many_int[:, :], many[:, :], EXACT_COUNT, None, ALU.is_gt).then_inc(many_ready, 1)

            with dve.Fori(0, PAIRS - 1) as i:
                first_pass(2 * i, 0)
                first_pass(2 * i + 1, 1)
            first_pass(TILES - 2, 0)
            first_pass(TILES - 1, 1)

            def low_of_fc(m, q):
                dve.wait_ge(fc_high, m + 1)
                nc.vector.tensor_tensor(fc_w[:, q, :, LO, :], fc_raw[:, q, :, :],
                                        fc_w[:, q, :, HI, :].bitcast(F32), ALU.subtract).then_inc(fc_low, 1)


            def take_self(l, n):
                dve.wait_ge(dense_done, 2 * (TILES * (2 * l + 1) + n + 1))
                if l == 1:
                    dve.wait_ge(x1_free, n + 1)
                if not isinstance(n, int) or n > 0:
                    dve.wait_ge(row_ready[l + 1], n)
                nc.vector.tensor_tensor(rows[1][:, :].rearrange("p (q c) -> p q c", q=2), bank[0:P, 0:2, :],
                                        bias[:, :].rearrange("p (q c) -> p q c", q=2), ALU.add).then_inc(self_taken, 1)
                if l == 1:
                    dve.wait_ge(self_taken, TILES + n + 2)
                    dve.wait_ge(res_in, 16 * (n + 1))
                    nc.vector.tensor_tensor(rows[1][:, :], rows[1][:, :], rows[0][:, :], ALU.add).then_inc(res_used, 1)

            def take_aggregate(l, n, j):
                dve.wait_ge(at_used, TILES * l + n + 2)
                dve.wait_ge((self_taken, res_used)[l], n + 2)
                target = rows[2 + j] if l == 0 else rows[1]
                ins = nc.vector.scalar_tensor_tensor(out=target[:, :].rearrange("p (q c) -> p q c", q=2),
                                                     in0=bank[0:P, 2:4, :], scalar=dinv[:, ds(n, 1)],
                                                     in1=rows[1][:, :].rearrange("p (q c) -> p q c", q=2),
                                                     op0=ALU.mult, op1=ALU.add)
                if l == 0:
                    ins.then_inc(row_ready[1], 1)
                else:
                    ins.then_inc(x1_ready, 1)
                    dve.wait_ge(x1_ready, n + 1)
                    layer_norm(1, n, j, rows[1], rows[2 + j])

            def tile_of_pass(l, n, j):
                take_self(l, n)
                low_of_row(l + 1, n - 1, xt_out, relu=(l == 0))
                if isinstance(n, int):
                    if l == 0:
                        low_of_w(2)
                    else:
                        low_of_fc(0, 0)
                take_aggregate(l, n, j)

            for l in range(2):
                if l == 1:
                    low_of_z(1, 0, 0)
                    low_of_row(1, TILES - 1, xt_out, relu=True)
                    low_of_z(1, 1, 1)
                    with dve.Fori(1, PAIRS - 1) as i:
                        low_of_z(1, 2 * i, 0)
                        low_of_z(1, 2 * i + 1, 1)
                    low_of_z(1, TILES - 2, 0)
                    low_of_w(3)
                    low_of_z(1, TILES - 1, 1)
                dve.wait_ge(bias_in, 16 * (l + 1))
                take_self(l, 0)
                take_aggregate(l, 0, 0)
                with dve.Fori(0, PAIRS - 1) as i:
                    tile_of_pass(l, 2 * i + 1, 1)
                    tile_of_pass(l, 2 * i + 2, 0)
                tile_of_pass(l, TILES - 1, 1)

            def low_of_pr(m, j):
                dve.wait_ge(pr_high, m + 1)
                nc.vector.tensor_tensor(pr_of(j)[:, LO, :], pr_raw[:, j % 2, :],
                                        pr_of(j)[:, HI, :].bitcast(F32), ALU.subtract).then_inc(pr_low, 1)

            def square_and_low(bank_index, slot, hid, c0, n):
                dve.wait_ge(hid_relu, bank_index + 3)
                dve.wait_ge(hid_low, bank_index + 1)
                nc.vector.tensor_tensor(square[:, slot, 0:n], relu[:, slot, 0:n], relu[:, slot, 0:n],
                                        ALU.mult).then_inc(hid_square, 1)
                dve.wait_ge(hid_square, bank_index + 1)
                dve.wait_ge(hid_high, bank_index + 1)
                nc.vector.tensor_tensor(hid[:, LO, c0:c0 + n], square[:, slot, 0:n],
                                        hid[:, HI, c0:c0 + n].bitcast(F32), ALU.subtract).then_inc(hid_low, 1)

            def lif_step(step, n):
                mem, drive, count = lif_a[:, :].unsqueeze(1), lif_b[:, :].unsqueeze(1), lif_c[:, :].unsqueeze(1)
                inp, x1_part = y0[:, ds(n, 1), :], x1_0[:, ds(n, 1), :]
                kind, s = (step - 1) % 3, (step - 1) // 3
                source = inp if s == 0 else mem
                dve.wait_ge(lif_steps, LIF_STEPS * n + step + 1)
                if step == 0:
                    ins = nc.vector.tensor_scalar(count, inp, THRESHOLD, None, ALU.is_gt)
                elif step == LIF_STEPS - 1:
                    ins = nc.vector.scalar_tensor_tensor(out=x1_part, in0=count, scalar=1.0 / STEPS, in1=x1_part,
                                                         op0=ALU.mult, op1=ALU.add)
                elif kind == 0:
                    ins = nc.vector.scalar_tensor_tensor(out=drive, in0=source, scalar=BETA, in1=inp,
                                                         op0=ALU.mult, op1=ALU.add)
                elif kind == 1:
                    ins = nc.vector.scalar_tensor_tensor(out=mem, in0=source, scalar=THRESHOLD, in1=drive,
                                                         op0=ALU.is_gt, op1=ALU.subtract, reverse1=True)
                else:
                    ins = nc.vector.scalar_tensor_tensor(out=count, in0=mem, scalar=THRESHOLD, in1=count,
                                                         op0=ALU.is_gt, op1=ALU.add)
                ins.then_inc(lif_steps, 1)

            dve.sem_inc(hid_low, 2)
            dve.sem_inc(lif_steps, 1)
            dve.sem_inc(y_added, Y_START)

            def hidden_part(g, b, first=False, last=False, spiking=False):
                _, count, columns = GROUPS_OF_TILES[g]
                length = 2 * BLOCK if last else BLOCK
                for j in range(length):
                    m = F_TILES * g + BLOCK * b + j
                    if not (last and j == length - 1):
                        low_of_fc(m + 1, (j + 1) % 2)
                    low_of_pr(m, j)
                    for c, (c0, n) in enumerate(columns):
                        bank_index = 2 * m + c if g == 0 else F_TILES + m
                        square_and_low(bank_index, c if g == 0 else j % 2, hid_of(g, j), c0, n)
                        if first and j == 1 and c == 0:
                            low_of_row(2, TILES - 1, xt_out)
                    if spiking and j > 0:
                        lif_step(j - 1, b)

            def add_share(g, b, n, halves=(0, 1)):
                _, count, _ = GROUPS_OF_TILES[g]
                first_sum = g * ADDED[0]
                for q in halves:
                    index = first_sum + 2 * count * b + 2 * n + q
                    dve.wait_ge(proj_summed, index + 2)
                    dve.wait_ge(y_added, index + 1 + Y_START - 2 * count)
                    part = y[g][:, n, q * HALF:(q + 1) * HALF]
                    nc.vector.tensor_tensor(part, part, bank[0:P, 2 * (n % 2) + q, :], ALU.add).then_inc(y_added, 1)

            def ffn_block(g, b, first=False, spiking=False):
                hidden_part(g, b, first=first, spiking=spiking)
                dve.wait_ge(y_zero, g + 1)
                if spiking:
                    dve.wait_ge(x1_in[0], 16)
                for n in range(GROUPS_OF_TILES[g][1]):
                    add_share(g, b, n)
                    if spiking:
                        for step in range(BLOCK - 1 + 3 * n, min(BLOCK - 1 + 3 * n + 3, LIF_STEPS)):
                            lif_step(step, b)

            ffn_block(0, 0, first=True)
            with dve.Fori(1, BLOCKS) as b:
                ffn_block(0, b)
            dve.wait_ge(y_added, Y_START + ADDED[0])
            assert LIF_STEPS <= BLOCK - 1 + 3 * (n1 // P) and n0 // P == BLOCKS - 2
            with dve.Fori(0, n0 // P) as b:
                ffn_block(1, b, spiking=True)
            hidden_part(1, BLOCKS - 2, last=True)

            def mem_step(half, step):
                t = step // 2
                drive = lif_c[:, half % 2 * HALF:(half % 2 + 1) * HALF]
                inp = half_of(y1, half)
                source = inp if t == 0 else mem_of(half, t - 1)
                if step > 0:
                    dve.wait_ge(mem_steps, MEM_ORDER.index((half, step - 1)) + 1)
                else:
                    dve.wait_ge(y_added, Y_START + sum(ADDED) - LAST_HALVES + half + 1)
                    if half >= 2:
                        dve.wait_ge(mem_steps, MEM_ORDER.index((half - 2, MEM_STEPS - 1)) + 1)
                if step % 2 == 0:
                    ins = nc.vector.scalar_tensor_tensor(out=drive, in0=source, scalar=BETA, in1=inp,
                                                         op0=ALU.mult, op1=ALU.add)
                else:
                    if t >= 2 or half >= 2:
                        dve.wait_ge(signs, SPIKE_ORDER.index((half, t - 1) if t >= 2 else (half - 2, t + 3)) + 1)
                    ins = nc.vector.scalar_tensor_tensor(out=mem_of(half, t), in0=source, scalar=THRESHOLD,
                                                         in1=drive, op0=ALU.is_gt, op1=ALU.subtract, reverse1=True)
                ins.then_inc(mem_steps, 1)

            def result(half):
                dve.wait_ge(x1_in[1], 16)
                dve.wait_ge(spikes_counted, SPIKE_ORDER.index((half, STEPS - 1)) + 1)
                part = half_of(x1_1, half)
                nc.vector.scalar_tensor_tensor(out=part, in0=bank[0:P, 4 + half % 4, :],
                                               scalar=1.0 / STEPS, in1=part,
                                               op0=ALU.mult, op1=ALU.add).then_inc(result_ready, 1)

            for half, stage in enumerate(MEM_STAGES):
                if half < LAST_HALVES:
                    add_share(1, BLOCKS - 2, half // 2, halves=(half % 2,))
                for place, entry in enumerate(stage):
                    mem_step(*entry)
                    if half >= 3 and place == 1:
                        result(half - 3)
            result(LAST_HALVES - 2)
            result(LAST_HALVES - 1)

        @block.tensor
        def _(pe):
            pe.wait_ge(constants, 6)
            pe.wait_ge(edge_steps, 8)
            nc.tensor.transpose(bank[0:2 * TILES, 6, 0:GROUPS], bounds[:, :], ident[0:GROUPS, 0:GROUPS]).then_inc(bounds_turned, 1)
            pe.wait_ge(edge_steps, 11)
            nc.tensor.matmul(bank[0:1, 7, 0:2 * TILES], bound_col[:, :], ident[0:2 * TILES, 0:2 * TILES],
                             start=True, stop=True).then_inc(bounds_turned, 1)
            pe.wait_ge(range_ready, 1)
            pe.wait_ge(constants, 9)
            for q in range(GROUP):
                pe.sem_inc(hot_used[q], 1)
            visit = pe.alloc_register("pe_visit")
            pe.reg_mov(visit, 1)
            next_visit = pe.alloc_register("pe_next_visit")
            pe.reg_mov(next_visit, 2)

            registers = range_registers(pe, "pe")

            def sum_counts(t, j, first, end):
                pe.wait_ge(counts_copied, t + 1)
                for b, (c0, n) in enumerate(COUNT_COLS):
                    nc.tensor.matmul(bank[0:P, 3 * j + b, 0:n], zero_w[:, :], iota[:, c0:c0 + n],
                                     start=True, stop=False)
                with pe.Fori(first, end) as g:
                    for q in range(GROUP):
                        pe.wait_ge(src_hot_ready[q], visit)
                        if q in (0, 2):
                            pe.wait_ge(dst_hot_ready[q // 2], next_visit)
                        for b, (c0, n) in enumerate(COUNT_COLS):
                            ins = nc.tensor.matmul(bank[0:P, 3 * j + b, 0:n], dst_hot[:, q, :],
                                                   src_hot[:, q, c0:c0 + n], start=False, stop=False)
                        ins.then_inc(hot_used[q], 1)
                    pe.reg_add(visit, visit, 1)
                    pe.reg_add(next_visit, next_visit, 1)
                for b, (c0, n) in enumerate(COUNT_COLS):
                    ins = nc.tensor.matmul(bank[0:P, 3 * j + b, 0:2], zero_w[:, :], iota[:, 0:2],
                                           start=False, stop=True)
                ins.then_inc(counts_summed, 1)

            with pe.Fori(0, PAIRS) as i:
                even, odd = load_ranges(pe, registers, i)
                sum_counts(2 * i, 0, *even)
                sum_counts(2 * i + 1, 1, *odd)

            pe.sem_inc(at_used, 1)

            def turn_row(l, n, j):
                pe.wait_ge(row_ready[l], n + 1)
                for q in range(2):
                    pe.wait_ge(row_low[l], 2 * n + q + 1)
                    for k in range(4):
                        c = (4 * q + k) * 128
                        ins = nc.tensor.transpose(bank[:, 6 + q, k * P:(k + 1) * P], rows[2 + j][:, c:c + 128],
                                                  ident[0:P, 0:P])
                    ins.then_inc(row_turned[l], 1)

            def turn_counts(n, j, r):
                s0, c = ROUNDS[r]
                if r == 0:
                    if isinstance(n, int):
                        pe.wait_ge(counts_in[j], 16 * (n // 2 + 1))
                    else:
                        pe.wait_ge(counts_in[j], 8 * (n - j) + 16)
                pe.wait_ge(turned_low, 3 * n + r + 1)
                for s in range(c):
                    ins = nc.tensor.transpose(bank[0:P, 4 + (3 * j + r) % 2, s * P:(s + 1) * P],
                                              counts_back[:, j, (s0 + s) * P:(s0 + s + 1) * P], ident[0:P, 0:P])
                ins.then_inc(counts_turned, 1)

            def dense(phase, n, j, first_bank, between=None):
                if phase > 0:
                    if isinstance(n, int):
                        pe.wait_ge(xt_in[j], 16 * (PAIRS * (phase - 1) + n // 2 + 1))
                    else:
                        pe.wait_ge(xt_in[j], 16 * (PAIRS * (phase - 1) + 1) + 8 * (n - j))
                for k in range(KD):
                    if k == KD // 2 and between is not None:
                        between()
                    if isinstance(n, int) and n == 0:
                        pe.wait_ge(w_low, KD * phase + k + 1)
                    for m, (a, b) in enumerate(PASSES):
                        for q in range(2):
                            ins = nc.tensor.matmul(bank[0:P, first_bank + q, :], xt[j][:, a, k, :],
                                                   w[:, k, b, q * HALF:(q + 1) * HALF],
                                                   start=(k == 0 and m == 0), stop=(k == KD - 1 and m == 2))
                            if k == KD - 1 and m == 2:
                                ins.then_inc(dense_done, 1)
                    if k < KD - 1:
                        ins.then_inc(w_used, 1)

            def z_of_tile(l, n, j, between=None):
                pe.wait_ge(z_low, 2 * TILES * l + 2 * n + 2)
                dense(2 * l, n, j, 2 * j, between)

            def first_pass(n, j):
                if not isinstance(n, int) or n + 1 < TILES:
                    turn_row(0, n + 1, 1 - j)
                turn_counts(n, j, 0)
                turn_counts(n, j, 1)
                pe.wait_ge(row_low[0], 2 * n + 4)
                z_of_tile(0, n, j, between=lambda: turn_counts(n, j, 2))

            turn_row(0, 0, 0)
            pe.wait_ge(deg_steps, 2)
            nc.tensor.transpose(bank[0:1, 3, 0:P], deg_max[:, :], ident[0:P, 0:P]).then_inc(deg_turned, 1)
            first_pass(0, 0)
            pe.wait_ge(many_ready, 1)
            big_counts = pe.value_load(many_int[0:1, 0:1], min_val=0, max_val=1)
            first_pass(1, 1)
            with pe.Fori(1, PAIRS - 1) as i:
                first_pass(2 * i, 0)
                first_pass(2 * i + 1, 1)
            first_pass(TILES - 2, 0)
            first_pass(TILES - 1, 1)

            def self_of_tile(l, n, j):
                pe.wait_ge(self_taken, TILES * l + n + 1)
                dense(2 * l + 1, n, j, 0)

            def aggregate(l, n):
                pe.wait_ge(at_in, 16 * (TILES * l + n + 1))
                if isinstance(n, int) and n == 0:
                    pe.wait_ge(z_low, 2 * TILES * (l + 1) + 4)
                else:
                    pe.wait_ge((row_ready[1], x1_ready)[l], n)

                def products(part, s):
                    for b in (HI, LO):
                        for q in range(2):
                            first = part == HI and s == 0 and b == HI
                            last = part == HI and s == TILES - 1 and b == LO
                            ins = nc.tensor.matmul(bank[0:P, 2 + q, :], at_tile[:, s, part, :],
                                                   z[:, s, b, q * HALF:(q + 1) * HALF], start=first, stop=last)
                    return ins

                for s in range(TILES - 1):
                    products(HI, s)
                with pe.If(big_counts):
                    for s in range(TILES):
                        products(LO, s)
                products(HI, TILES - 1).then_inc(at_used, 1)

            for l in range(2):
                if l == 1:
                    pe.wait_ge(self_taken, TILES + 1)
                    z_of_tile(1, 0, 0)
                    turn_row(1, TILES - 1, 1)
                    pe.wait_ge(row_ready[1], TILES)
                    z_of_tile(1, 1, 1)
                    with pe.Fori(1, PAIRS) as i:
                        z_of_tile(1, 2 * i, 0)
                        z_of_tile(1, 2 * i + 1, 1)
                pe.wait_ge(z_low, 2 * TILES * (l + 1) + 2)
                self_of_tile(l, 0, 0)
                aggregate(l, 0)

                def tile_of_pass(n, j):
                    self_of_tile(l, n, j)
                    turn_row(l + 1, n - 1, 1 - j)
                    aggregate(l, n)

                with pe.Fori(0, PAIRS - 1) as i:
                    tile_of_pass(2 * i + 1, 1)
                    tile_of_pass(2 * i + 2, 0)
                tile_of_pass(TILES - 1, 1)

            pe.sem_inc(hid_summed, 2)
            pe.sem_inc(proj_summed, 1)

            def ffn_block(g, b, first=False, last=False):
                _, count, columns = GROUPS_OF_TILES[g]
                first_sum = g * ADDED[0]
                banks = len(columns)
                length = 2 * BLOCK if last else BLOCK
                for j in range(length):
                    m = F_TILES * g + BLOCK * b + j
                    pe.wait_ge(fc_low, m + 1)

                    def hidden_products(c, k):
                        c0, n = columns[c]
                        if k == 0:
                            pe.wait_ge(hid_relu, (2 * m + c if g == 0 else F_TILES + m) + 1)
                        for i, (a, v) in enumerate(PASSES):
                            ins = nc.tensor.matmul(bank[:, 4 + (c if g == 0 else j % 2), 0:n], fc_w[:, j % 2, k, a, :],
                                                   x2t[g][:, k, v, c0:c0 + n],
                                                   start=(k == 0 and i == 0), stop=(k == KD - 1 and i == 2))
                        if k == KD - 1:
                            ins.then_inc(hid_summed, 1)

                    if first and j == 0:
                        for k in range(KD):
                            pe.wait_ge(x2_in[k], 16)
                            for c in range(banks):
                                hidden_products(c, k)
                    else:
                        for c in range(banks):
                            for k in range(KD):
                                hidden_products(c, k)
                    if first and j == 1:
                        turn_row(2, TILES - 1, 1)
                first_hid = (2 * F_TILES) * g + BLOCK * banks * b

                def products(n, q, j):
                    if j == 0:
                        pe.wait_ge(y_added, first_sum + 2 * count * b + 2 * n + q + Y_START - 3)
                    for i, (a, v) in enumerate(PASSES):
                        ins = nc.tensor.matmul(bank[0:P, 2 * (n % 2) + q, :], hid_of(g, j)[:, a, n * P:(n + 1) * P],
                                               pr_of(j)[:, v, q * HALF:(q + 1) * HALF],
                                               start=(j == 0 and i == 0), stop=(j == length - 1 and i == 2))
                    if j == length - 1:
                        ins.then_inc(proj_summed, 1)

                for j in range(length):
                    if j in (0, length - 1):
                        pe.wait_ge(hid_low, first_hid + banks * (j if j else length - 1) + 2 + (1 if j else 0))
                    pe.wait_ge(pr_low, F_TILES * g + BLOCK * b + j + 1)
                    for q in range(2):
                        products(0, q, j)
                for n in range(1, count):
                    if banks == 2 and n == 3:
                        pe.wait_ge(hid_low, first_hid + banks * BLOCK + 2)
                    for q in range(2):
                        for j in range(length):
                            products(n, q, j)
                        if last:
                            add_spikes(2 * n + q - 2)

            def add_spikes(stage):
                for half, s in SPIKE_STAGES[stage]:
                    spike = SPIKE_ORDER.index((half, s))
                    pe.wait_ge(spikes_ready, spike + 1)
                    if spike == 0:
                        pe.wait_ge(constants, 10)
                    if s == 0 and half >= 4:
                        pe.wait_ge(result_ready, half - 3)
                    nc.tensor.matmul(bank[0:P, 4 + half % 4, :], ident_narrow[:, :], spikes[:, spike % SPIKE_SLOTS, :],
                                     start=(s == 0), stop=(s == STEPS - 1)).then_inc(spikes_counted, 1)

            ffn_block(0, 0, first=True)
            with pe.Fori(1, BLOCKS) as b:
                ffn_block(0, b)
            pe.wait_ge(x2_in_last, 16)
            with pe.Fori(0, BLOCKS - 2) as b:
                ffn_block(1, b)
            ffn_block(1, BLOCKS - 2, last=True)
            for stage in range(LAST_HALVES - 2, LAST_HALVES + 1):
                add_spikes(stage)


def kernel(x, src, dst, L0_gnn_W_self0, L0_gnn_W_neigh0, L0_gnn_b0, L0_gnn_W_self1, L0_gnn_W_neigh1, L0_gnn_b1,
           L0_ffn_W_fc, L0_ffn_W_proj):
    import numpy as np
    import concourse.bacc as bacc
    from concourse.bass_utils import run_bass_kernel_spmd

    def columns(edges):
        return np.asarray(edges).reshape(CHUNKS, P).T

    arrays = {
        "x": x,
        "dst_cols": columns(dst),
        "src_cols": columns(src),
        "dst_rows": np.asarray(dst).reshape(GROUPS, GROUP * P),
        "w_self0": L0_gnn_W_self0, "w_neigh0": L0_gnn_W_neigh0, "b0": L0_gnn_b0,
        "w_self1": L0_gnn_W_self1, "w_neigh1": L0_gnn_W_neigh1, "b1": L0_gnn_b1,
        "w_fc": np.asarray(L0_ffn_W_fc).reshape(F_TILES, F_TILE, KD, 128).transpose(0, 3, 2, 1),
        "w_proj": np.asarray(L0_ffn_W_proj).T.reshape(F_TILES, F_TILE, D),
    }
    arrays = {name: np.ascontiguousarray(a) for name, a in arrays.items()}
    nc = bacc.Bacc("TRN2", target_bir_lowering=False, num_devices=1)
    args = {name: nc.dram_tensor(name, a.shape, mybir.dt.from_np(a.dtype), kind="ExternalInput").ap()
            for name, a in arrays.items()}
    args["out"] = nc.dram_tensor("out", (NODES, D), F32, kind="ExternalOutput").ap()
    gnn_ffn(nc, **args)
    result = run_bass_kernel_spmd(nc, [arrays], core_ids=[0])
    return result.results[0]["out"]
```
